# Optimizing a Trainium2 kernel written in Bass

```python
import numpy as np
import jax
import jax.numpy as jnp

def _softmax(x, axis=-1):
    return jax.nn.softmax(x, axis=axis)

def _gelu(x):
    return jax.nn.gelu(x, approximate=True)

def _silu(x):
    return jax.nn.silu(x)

def _sigmoid(x):
    return jax.nn.sigmoid(x)

def _layernorm(x, axis=-1, eps=1e-05):
    m = jnp.mean(x, axis=axis, keepdims=True)
    v = jnp.var(x, axis=axis, keepdims=True)
    return (x - m) / jnp.sqrt(v + eps)

def _scatter_add(tgt, idx, src, axis=0):
    return tgt.at[idx].add(src)

def _segment_sum(src, seg, n):
    return jax.ops.segment_sum(src, seg, n)
kernel_name = 'mk_xattn_ffn_d4_seqx_r8_736357'

def setup_inputs(seed: int=0):
    np.random.seed(seed)
    _w = jnp.asarray

    def _rec_inputs():
        import jax
        import jax.numpy as jnp
        _rk = jax.random.key(seed)
        x = -0.0002928 + 1 * jax.random.normal(jax.random.fold_in(_rk, 1), (32, 64, 128), jnp.float32)
        _lenS = 64 - jax.random.randint(jax.random.fold_in(_rk, 7), (32,), 0, max(1, 64 // 4) + 1, jnp.int32)
        _lenS2 = 64 - jax.random.randint(jax.random.fold_in(_rk, 8), (32,), 0, max(1, 64 // 4) + 1, jnp.int32)
        _ctx_1024P = jax.random.normal(jax.random.fold_in(_rk, 11), (32, 16, 128), jnp.float32)
        _ctx_1024c = jax.random.dirichlet(jax.random.fold_in(_rk, 511), 0.3 * jnp.ones((16,), jnp.float32), (32, 64))
        _ctx_1024t = jnp.einsum('bsk,bkd->bsd', _ctx_1024c, _ctx_1024P)
        _ctx_1024t = _ctx_1024t * jax.lax.rsqrt(jnp.mean(jnp.square(_ctx_1024t)) + 1e-12) * 0.953939
        ctx_1024 = -1.39393e-06 + 0.999914 * (_ctx_1024t + 0.3 * jax.random.normal(jax.random.fold_in(_rk, 611), (32, 64, 128), jnp.float32))
        _validS = jnp.arange(64)[None, :] < _lenS[:, None]
        _validS2 = jnp.arange(64)[None, :] < _lenS2[:, None]
        _causal = jnp.tril(jnp.ones((64, 64), dtype=bool))
        mask_BxS2_ik0 = jnp.where(jnp.broadcast_to(_validS2[:, :], (32, 64)), 0, 1).astype(jnp.int32)
        mask_BxSxS2_ik1 = jnp.where(jnp.broadcast_to(_validS2[:, None, :], (32, 64, 64)), 1, 0).astype(jnp.int32)
        mask_BxS2_if0 = jnp.where(jnp.ones((32, 64), dtype=bool), 0, 1).astype(jnp.int32)
        return (x, ctx_1024, mask_BxS2_ik0, mask_BxSxS2_ik1, mask_BxS2_if0)
    x, ctx_1024, mask_BxS2_ik0, mask_BxSxS2_ik1, mask_BxS2_if0 = _rec_inputs()

    def _L0_xattn_setup():
        import jax, jax.numpy as jnp
        import numpy as np
        B, S, D, H = (2, 256, 128, 16)
        DK = D // H
        SQRT_DK = DK ** 0.5
        NEG = -1000000000.0
        key = jax.random.key(seed)
        ks = jax.random.split(key, 7)
        scale = 1.0 / np.sqrt(D)
        return {'x': jax.random.normal(ks[0], (B, S, D), jnp.float32), 'encoder_output': jax.random.normal(ks[1], (B, S, D), jnp.float32), 'mask': jax.random.randint(ks[2], (B, S), 0, 2, jnp.int32), 'WQ': jax.random.normal(ks[3], (D, D), jnp.float32) * scale, 'WK': jax.random.normal(ks[4], (D, D), jnp.float32) * scale, 'WV': jax.random.normal(ks[5], (D, D), jnp.float32) * scale, 'WO': jax.random.normal(ks[6], (D, D), jnp.float32) * scale}
    _L0_xattn_all = _L0_xattn_setup()
    _L0_xattn_in = {k: v for k, v in _L0_xattn_all.items() if k in ('WQ', 'WK', 'WV', 'WO')}
    del _L0_xattn_all

    def _L0_ffn_setup():
        import jax, jax.numpy as jnp
        import numpy as np
        import math
        D_MODEL = 128
        D_FF = 512
        NUM_EXPERTS = 8
        NUM_SHARED = 1
        E_ROUTED = NUM_EXPERTS - NUM_SHARED
        TOP_K = 2
        CAP_FACTOR = 1.25
        B, S = (4, 256)
        T = B * S
        CAPACITY = math.ceil(CAP_FACTOR * T * TOP_K / E_ROUTED)
        SHARED_SCALE = 1.0

        def _layernorm(x, g, b, eps=1e-05):
            mu = jnp.mean(x, axis=-1, keepdims=True)
            var = jnp.mean((x - mu) ** 2, axis=-1, keepdims=True)
            return (x - mu) * jax.lax.rsqrt(var + eps) * g + b
        key = jax.random.key(seed)
        ks = jax.random.split(key, 10)
        s = 0.02
        return {'x': jax.random.normal(ks[0], (B, S, D_MODEL), dtype=jnp.float32), 'ln_g': jnp.ones((D_MODEL,), jnp.float32), 'ln_b': jnp.zeros((D_MODEL,), jnp.float32), 'Wr': jax.random.normal(ks[1], (D_MODEL, E_ROUTED), jnp.float32) * s, 'W1': jax.random.normal(ks[2], (E_ROUTED, D_MODEL, D_FF), jnp.float32) * s, 'W3': jax.random.normal(ks[3], (E_ROUTED, D_MODEL, D_FF), jnp.float32) * s, 'W2': jax.random.normal(ks[4], (E_ROUTED, D_FF, D_MODEL), jnp.float32) * s, 'W1s': jax.random.normal(ks[5], (D_MODEL, D_FF), jnp.float32) * s, 'W3s': jax.random.normal(ks[6], (D_MODEL, D_FF), jnp.float32) * s, 'W2s': jax.random.normal(ks[7], (D_FF, D_MODEL), jnp.float32) * s}
    _L0_ffn_all = _L0_ffn_setup()
    _L0_ffn_in = {k: v for k, v in _L0_ffn_all.items() if k in ('ln_g', 'ln_b', 'Wr', 'W1', 'W3', 'W2', 'W1s', 'W3s', 'W2s')}
    del _L0_ffn_all

    def _L1_xattn_setup():
        import jax, jax.numpy as jnp
        import numpy as np
        B, S, D, DFF = (4, 256, 128, 512)
        EPS = 1e-05

        def layernorm(x, gamma, beta):
            mu = jnp.mean(x, axis=-1, keepdims=True)
            var = jnp.var(x, axis=-1, keepdims=True)
            return (x - mu) * jax.lax.rsqrt(var + EPS) * gamma + beta

        def attention(Q, K, V, causal):
            d_k = Q.shape[-1]
            scores = jnp.einsum('bqd,bkd->bqk', Q, K) / jnp.sqrt(jnp.asarray(d_k, Q.dtype))
            if causal:
                q_len, k_len = (scores.shape[-2], scores.shape[-1])
                mask = jnp.tril(jnp.ones((q_len, k_len), dtype=bool))
                scores = jnp.where(mask[None], scores, jnp.asarray(-jnp.inf, scores.dtype))
            w = jax.nn.softmax(scores, axis=-1)
            return jnp.einsum('bqk,bkd->bqd', w, V)
        key = jax.random.key(seed)
        ks = jax.random.split(key, 12)
        sd = 0.02
        return {'y': jax.random.normal(ks[0], (B, S, D), jnp.float32), 'Z': jax.random.normal(ks[1], (B, S, D), jnp.float32), 'w1': jax.random.normal(ks[2], (D, DFF), jnp.float32) * sd, 'b1': jnp.zeros((DFF,), jnp.float32), 'w2': jax.random.normal(ks[3], (DFF, D), jnp.float32) * sd, 'b2': jnp.zeros((D,), jnp.float32), 'g1': jnp.ones((D,), jnp.float32), 'beta1': jnp.zeros((D,), jnp.float32), 'g2': jnp.ones((D,), jnp.float32), 'beta2': jnp.zeros((D,), jnp.float32), 'g3': jnp.ones((D,), jnp.float32), 'beta3': jnp.zeros((D,), jnp.float32)}
    _L1_xattn_all = _L1_xattn_setup()
    _L1_xattn_in = {k: v for k, v in _L1_xattn_all.items() if k in ('w1', 'b1', 'w2', 'b2', 'g1', 'beta1', 'g2', 'beta2', 'g3', 'beta3')}
    del _L1_xattn_all

    def _L1_ffn_setup():
        import jax, jax.numpy as jnp
        import numpy as np
        import math
        E = 8
        K = 2
        CF = 1.2
        D = 128
        H = 512
        key = jax.random.key(seed)
        k0, k1, k2, k3 = jax.random.split(key, 4)
        B, T = (8, 256)
        x_btd = jax.random.normal(k0, (B, T, D), jnp.float32)
        Wr = jax.random.normal(k1, (D, E), jnp.float32) / np.sqrt(D)
        br = jnp.zeros((E,), jnp.float32)
        W1 = jax.random.normal(k2, (E, D, H), jnp.float32) / np.sqrt(D)
        b1 = jnp.zeros((E, H), jnp.float32)
        W2 = jax.random.normal(k3, (E, H, D), jnp.float32) / np.sqrt(H)
        b2 = jnp.zeros((E, D), jnp.float32)
        return dict(x_btd=x_btd, Wr=Wr, br=br, W1=W1, b1=b1, W2=W2, b2=b2)
    _L1_ffn_all = _L1_ffn_setup()
    _L1_ffn_in = {k: v for k, v in _L1_ffn_all.items() if k in ('Wr', 'br', 'W1', 'b1', 'W2', 'b2')}
    del _L1_ffn_all

    def _L2_xattn_setup():
        import jax, jax.numpy as jnp
        import numpy as np
        NEG = -9000000000000000.0
        EPS = 1e-05
        key = jax.random.key(seed)
        k1, k2, k3, k4 = jax.random.split(key, 4)
        B, S, D = (4, 256, 128)
        q = jax.random.normal(k1, (B, S, D), dtype=jnp.float32)
        k = jax.random.normal(k2, (B, S, D), dtype=jnp.float32)
        v = jax.random.normal(k3, (B, S, D), dtype=jnp.float32)
        mask = jax.random.randint(k4, (B, S, S), 0, 2, dtype=jnp.int32)
        gamma = jnp.ones((D,), dtype=jnp.float32)
        beta = jnp.zeros((D,), dtype=jnp.float32)
        return {'q': q, 'k': k, 'v': v, 'mask': mask, 'gamma': gamma, 'beta': beta}
    _L2_xattn_all = _L2_xattn_setup()
    _L2_xattn_in = {k: v for k, v in _L2_xattn_all.items() if k in ('gamma', 'beta')}
    del _L2_xattn_all

    def _L2_ffn_setup():
        import jax, jax.numpy as jnp
        import numpy as np
        DIM = 128
        E = 16
        TOPK = 2
        G = 4
        TOPK_G = 2
        INTER = 64
        N_SHARED = 2
        ROUTE_SCALE = 1.0

        def _gate(xf, gate_w, gate_b):
            scores = xf @ gate_w.T
            scores = jax.nn.softmax(scores.astype(jnp.float32), axis=-1)
            orig = scores
            scores = scores + gate_b
            T = xf.shape[0]
            sg = scores.reshape(T, G, E // G)
            group_scores = jax.lax.top_k(sg, 2)[0].sum(-1)
            _, gidx = jax.lax.top_k(group_scores, TOPK_G)
            keep = jax.nn.one_hot(gidx, G).sum(axis=1) > 0
            sg = jnp.where(keep[:, :, None], sg, -jnp.inf)
            scores = sg.reshape(T, E)
            _, idx = jax.lax.top_k(scores, TOPK)
            weights = jnp.take_along_axis(orig, idx, axis=1)
            weights = (weights * ROUTE_SCALE).astype(xf.dtype)
            return (weights, idx)
        key = jax.random.key(seed)
        ks = jax.random.split(key, 16)
        s = lambda fan_in: 1.0 / np.sqrt(fan_in)
        inp = {'x': jax.random.normal(ks[0], (4, 128, DIM), dtype=jnp.float32), 'gate_w': jax.random.normal(ks[1], (E, DIM), dtype=jnp.float32) * s(DIM), 'gate_b': jnp.zeros((E,), dtype=jnp.float32), 'We1': jax.random.normal(ks[2], (E, DIM, INTER), dtype=jnp.float32) * s(DIM), 'be1': jnp.zeros((E, INTER), dtype=jnp.float32), 'We2': jax.random.normal(ks[3], (E, INTER, DIM), dtype=jnp.float32) * s(INTER), 'be2': jnp.zeros((E, DIM), dtype=jnp.float32), 'We3': jax.random.normal(ks[4], (E, DIM, INTER), dtype=jnp.float32) * s(DIM), 'be3': jnp.zeros((E, INTER), dtype=jnp.float32), 'ws1': jax.random.normal(ks[5], (DIM, N_SHARED * INTER), dtype=jnp.float32) * s(DIM), 'bs1': jnp.zeros((N_SHARED * INTER,), dtype=jnp.float32), 'ws2': jax.random.normal(ks[6], (N_SHARED * INTER, DIM), dtype=jnp.float32) * s(N_SHARED * INTER), 'bs2': jnp.zeros((DIM,), dtype=jnp.float32), 'ws3': jax.random.normal(ks[7], (DIM, N_SHARED * INTER), dtype=jnp.float32) * s(DIM), 'bs3': jnp.zeros((N_SHARED * INTER,), dtype=jnp.float32)}
        return inp
    _L2_ffn_all = _L2_ffn_setup()
    _L2_ffn_in = {k: v for k, v in _L2_ffn_all.items() if k in ('gate_w', 'gate_b', 'We1', 'be1', 'We2', 'be2', 'We3', 'be3', 'ws1', 'bs1', 'ws2', 'bs2', 'ws3', 'bs3')}
    del _L2_ffn_all

    def _L3_xattn_setup():
        import jax, jax.numpy as jnp
        import numpy as np
        import math
        B, M, D, H, NK = (4, 256, 128, 16, 5)
        HD = D // H

        def _gather_pad0(x, idx):
            Bx, Hx, W, hd = x.shape
            valid = (idx >= 0) & (idx < W)
            idxc = jnp.clip(idx, 0, W - 1).reshape(Bx, Hx, -1)
            g = jnp.take_along_axis(x, idxc[..., None], axis=2)
            g = g.reshape(idx.shape + (hd,))
            return g * valid[..., None].astype(x.dtype)
        key = jax.random.key(seed)
        ks = jax.random.split(key, 9)
        w = lambda k, shape: jax.random.normal(k, shape, jnp.float32) * 0.02
        return {'k': jax.random.normal(ks[0], (B, M, D), jnp.float32), 'v': jax.random.normal(ks[1], (B, M, D), jnp.float32), 'q': jax.random.normal(ks[2], (B, M, D), jnp.float32), 'mask': jnp.zeros((B, M), jnp.int32), 'Wk': w(ks[3], (D, D)), 'bk': jnp.zeros((D,), jnp.float32), 'Wv': w(ks[4], (D, D)), 'bv': jnp.zeros((D,), jnp.float32), 'Wq': w(ks[5], (D, D)), 'bq': jnp.zeros((D,), jnp.float32), 'Woff': w(ks[6], (H * NK, D)), 'boff': jnp.zeros((H * NK,), jnp.float32), 'Wo': w(ks[7], (D, D)), 'bo': jnp.zeros((D,), jnp.float32)}
    _L3_xattn_all = _L3_xattn_setup()
    _L3_xattn_in = {k: v for k, v in _L3_xattn_all.items() if k in ('Wk', 'bk', 'Wv', 'bv', 'Wq', 'bq', 'Woff', 'boff', 'Wo', 'bo')}
    del _L3_xattn_all

    def _L3_ffn_setup():
        import jax, jax.numpy as jnp
        import numpy as np
        TOP_K = 2
        TEMP = 1.0
        key = jax.random.key(seed)
        ks = jax.random.split(key, 5)
        B, S, D, E = (4, 256, 128, 8)
        F = 4 * D
        x = jax.random.normal(ks[0], (B, S, D), dtype=jnp.float32)
        Wg = jax.random.normal(ks[1], (D, E), dtype=jnp.float32) * (1.0 / np.sqrt(D))
        bg = jnp.zeros((E,), dtype=jnp.float32)
        W1 = jax.random.normal(ks[2], (E, D, F), dtype=jnp.float32) * (1.0 / np.sqrt(D))
        b1 = jnp.zeros((E, F), dtype=jnp.float32)
        W2 = jax.random.normal(ks[3], (E, F, D), dtype=jnp.float32) * (1.0 / np.sqrt(F))
        b2 = jnp.zeros((E, D), dtype=jnp.float32)
        return {'x': x, 'Wg': Wg, 'bg': bg, 'W1': W1, 'b1': b1, 'W2': W2, 'b2': b2}
    _L3_ffn_all = _L3_ffn_setup()
    _L3_ffn_in = {k: v for k, v in _L3_ffn_all.items() if k in ('Wg', 'bg', 'W1', 'b1', 'W2', 'b2')}
    del _L3_ffn_all
    return {'x': x, 'ctx_1024': ctx_1024, 'mask_BxS2_ik0': mask_BxS2_ik0, 'mask_BxSxS2_ik1': mask_BxSxS2_ik1, 'mask_BxS2_if0': mask_BxS2_if0, 'L0_xattn_WQ': _L0_xattn_in['WQ'], 'L0_xattn_WK': _L0_xattn_in['WK'], 'L0_xattn_WV': _L0_xattn_in['WV'], 'L0_xattn_WO': _L0_xattn_in['WO'], 'L0_ffn_ln_g': _L0_ffn_in['ln_g'], 'L0_ffn_ln_b': _L0_ffn_in['ln_b'], 'L0_ffn_Wr': _L0_ffn_in['Wr'], 'L0_ffn_W1': _L0_ffn_in['W1'], 'L0_ffn_W3': _L0_ffn_in['W3'], 'L0_ffn_W2': _L0_ffn_in['W2'], 'L0_ffn_W1s': _L0_ffn_in['W1s'], 'L0_ffn_W3s': _L0_ffn_in['W3s'], 'L0_ffn_W2s': _L0_ffn_in['W2s'], 'L1_xattn_w1': _L1_xattn_in['w1'], 'L1_xattn_b1': _L1_xattn_in['b1'], 'L1_xattn_w2': _L1_xattn_in['w2'], 'L1_xattn_b2': _L1_xattn_in['b2'], 'L1_xattn_g1': _L1_xattn_in['g1'], 'L1_xattn_beta1': _L1_xattn_in['beta1'], 'L1_xattn_g2': _L1_xattn_in['g2'], 'L1_xattn_beta2': _L1_xattn_in['beta2'], 'L1_xattn_g3': _L1_xattn_in['g3'], 'L1_xattn_beta3': _L1_xattn_in['beta3'], 'L1_ffn_Wr': _L1_ffn_in['Wr'], 'L1_ffn_br': _L1_ffn_in['br'], 'L1_ffn_W1': _L1_ffn_in['W1'], 'L1_ffn_b1': _L1_ffn_in['b1'], 'L1_ffn_W2': _L1_ffn_in['W2'], 'L1_ffn_b2': _L1_ffn_in['b2'], 'L2_xattn_gamma': _L2_xattn_in['gamma'], 'L2_xattn_beta': _L2_xattn_in['beta'], 'L2_ffn_gate_w': _L2_ffn_in['gate_w'], 'L2_ffn_gate_b': _L2_ffn_in['gate_b'], 'L2_ffn_We1': _L2_ffn_in['We1'], 'L2_ffn_be1': _L2_ffn_in['be1'], 'L2_ffn_We2': _L2_ffn_in['We2'], 'L2_ffn_be2': _L2_ffn_in['be2'], 'L2_ffn_We3': _L2_ffn_in['We3'], 'L2_ffn_be3': _L2_ffn_in['be3'], 'L2_ffn_ws1': _L2_ffn_in['ws1'], 'L2_ffn_bs1': _L2_ffn_in['bs1'], 'L2_ffn_ws2': _L2_ffn_in['ws2'], 'L2_ffn_bs2': _L2_ffn_in['bs2'], 'L2_ffn_ws3': _L2_ffn_in['ws3'], 'L2_ffn_bs3': _L2_ffn_in['bs3'], 'L3_xattn_Wk': _L3_xattn_in['Wk'], 'L3_xattn_bk': _L3_xattn_in['bk'], 'L3_xattn_Wv': _L3_xattn_in['Wv'], 'L3_xattn_bv': _L3_xattn_in['bv'], 'L3_xattn_Wq': _L3_xattn_in['Wq'], 'L3_xattn_bq': _L3_xattn_in['bq'], 'L3_xattn_Woff': _L3_xattn_in['Woff'], 'L3_xattn_boff': _L3_xattn_in['boff'], 'L3_xattn_Wo': _L3_xattn_in['Wo'], 'L3_xattn_bo': _L3_xattn_in['bo'], 'L3_ffn_Wg': _L3_ffn_in['Wg'], 'L3_ffn_bg': _L3_ffn_in['bg'], 'L3_ffn_W1': _L3_ffn_in['W1'], 'L3_ffn_b1': _L3_ffn_in['b1'], 'L3_ffn_W2': _L3_ffn_in['W2'], 'L3_ffn_b2': _L3_ffn_in['b2']}

def reference(x, ctx_1024, mask_BxS2_ik0, mask_BxSxS2_ik1, mask_BxS2_if0, L0_xattn_WQ, L0_xattn_WK, L0_xattn_WV, L0_xattn_WO, L0_ffn_ln_g, L0_ffn_ln_b, L0_ffn_Wr, L0_ffn_W1, L0_ffn_W3, L0_ffn_W2, L0_ffn_W1s, L0_ffn_W3s, L0_ffn_W2s, L1_xattn_w1, L1_xattn_b1, L1_xattn_w2, L1_xattn_b2, L1_xattn_g1, L1_xattn_beta1, L1_xattn_g2, L1_xattn_beta2, L1_xattn_g3, L1_xattn_beta3, L1_ffn_Wr, L1_ffn_br, L1_ffn_W1, L1_ffn_b1, L1_ffn_W2, L1_ffn_b2, L2_xattn_gamma, L2_xattn_beta, L2_ffn_gate_w, L2_ffn_gate_b, L2_ffn_We1, L2_ffn_be1, L2_ffn_We2, L2_ffn_be2, L2_ffn_We3, L2_ffn_be3, L2_ffn_ws1, L2_ffn_bs1, L2_ffn_ws2, L2_ffn_bs2, L2_ffn_ws3, L2_ffn_bs3, L3_xattn_Wk, L3_xattn_bk, L3_xattn_Wv, L3_xattn_bv, L3_xattn_Wq, L3_xattn_bq, L3_xattn_Woff, L3_xattn_boff, L3_xattn_Wo, L3_xattn_bo, L3_ffn_Wg, L3_ffn_bg, L3_ffn_W1, L3_ffn_b1, L3_ffn_W2, L3_ffn_b2):
    import jax
    import jax.numpy as jnp

    def _L0_xattn_ref(x, encoder_output, mask, WQ, WK, WV, WO):
        import jax, jax.numpy as jnp
        import numpy as np
        B, S, D, H = (2, 256, 128, 16)
        DK = D // H
        SQRT_DK = DK ** 0.5
        NEG = -1000000000.0
        b, s, d = x.shape
        q = (x @ WQ).reshape(b, s, H, DK).transpose(0, 2, 1, 3)
        k = (encoder_output @ WK).reshape(b, s, H, DK).transpose(0, 2, 1, 3)
        v = (encoder_output @ WV).reshape(b, s, H, DK).transpose(0, 2, 1, 3)
        scores = jnp.einsum('bhqd,bhkd->bhqk', q, k) / SQRT_DK
        future = jnp.triu(jnp.ones((s, s), jnp.int32), 1)
        m = mask[:, None, :, None] + future[None, None, :, :]
        scores = jnp.where(m != 0, NEG, scores)
        attn = jax.nn.softmax(scores, axis=-1)
        ctx = jnp.einsum('bhqk,bhkd->bqhd', attn, v).reshape(b, s, d)
        return ctx @ WO

    def _L0_ffn_ref(x, ln_g, ln_b, Wr, W1, W3, W2, W1s, W3s, W2s):
        import jax, jax.numpy as jnp
        import numpy as np
        import math
        D_MODEL = 128
        D_FF = 512
        NUM_EXPERTS = 8
        NUM_SHARED = 1
        E_ROUTED = NUM_EXPERTS - NUM_SHARED
        TOP_K = 2
        CAP_FACTOR = 1.25
        B, S = (4, 256)
        T = B * S
        CAPACITY = math.ceil(CAP_FACTOR * T * TOP_K / E_ROUTED)
        SHARED_SCALE = 1.0

        def _layernorm(x, g, b, eps=1e-05):
            mu = jnp.mean(x, axis=-1, keepdims=True)
            var = jnp.mean((x - mu) ** 2, axis=-1, keepdims=True)
            return (x - mu) * jax.lax.rsqrt(var + eps) * g + b
        Bx, Sx, D = x.shape
        Tn = Bx * Sx
        h = _layernorm(x, ln_g, ln_b).reshape(Tn, D)
        logits = h @ Wr
        top_vals, top_idx = jax.lax.top_k(logits, TOP_K)
        gates = jax.nn.softmax(top_vals, axis=-1)
        idx = top_idx.T.reshape(-1)
        gat = gates.T.reshape(-1)
        tok = jnp.tile(jnp.arange(Tn), TOP_K)
        onehot = jax.nn.one_hot(idx, E_ROUTED, dtype=jnp.int32)
        pos = jnp.sum(jnp.cumsum(onehot, axis=0) * onehot, axis=-1) - 1
        keep = pos < CAPACITY
        pos_c = jnp.where(keep, pos, CAPACITY)
        xe = jnp.zeros((E_ROUTED, CAPACITY, D), h.dtype).at[idx, pos_c].set(h[tok], mode='drop')
        a = jnp.einsum('ecd,edf->ecf', xe, W1)
        b = jnp.einsum('ecd,edf->ecf', xe, W3)
        ye = jnp.einsum('ecf,efd->ecd', jax.nn.silu(a) * b, W2)
        out_slots = ye[jnp.clip(idx, 0, E_ROUTED - 1), jnp.clip(pos_c, 0, CAPACITY - 1)]
        out_slots = out_slots * (gat * keep.astype(gat.dtype))[:, None]
        routed = jnp.zeros((Tn, D), h.dtype).at[tok].add(out_slots)
        shared = jax.nn.silu(h @ W1s) * (h @ W3s) @ W2s
        out = routed + SHARED_SCALE * shared
        return out.reshape(Bx, Sx, D)

    def _L1_xattn_ref(y, Z, w1, b1, w2, b2, g1, beta1, g2, beta2, g3, beta3):
        import jax, jax.numpy as jnp
        import numpy as np
        B, S, D, DFF = (4, 256, 128, 512)
        EPS = 1e-05

        def layernorm(x, gamma, beta):
            mu = jnp.mean(x, axis=-1, keepdims=True)
            var = jnp.var(x, axis=-1, keepdims=True)
            return (x - mu) * jax.lax.rsqrt(var + EPS) * gamma + beta

        def attention(Q, K, V, causal):
            d_k = Q.shape[-1]
            scores = jnp.einsum('bqd,bkd->bqk', Q, K) / jnp.sqrt(jnp.asarray(d_k, Q.dtype))
            if causal:
                q_len, k_len = (scores.shape[-2], scores.shape[-1])
                mask = jnp.tril(jnp.ones((q_len, k_len), dtype=bool))
                scores = jnp.where(mask[None], scores, jnp.asarray(-jnp.inf, scores.dtype))
            w = jax.nn.softmax(scores, axis=-1)
            return jnp.einsum('bqk,bkd->bqd', w, V)
        sa = attention(y, y, y, causal=True)
        y = layernorm(y + sa, g1, beta1)
        ca = attention(y, Z, Z, causal=False)
        y = layernorm(y + ca, g2, beta2)
        h = jax.nn.relu(jnp.einsum('bsd,df->bsf', y, w1) + b1)
        ff = jnp.einsum('bsf,fd->bsd', h, w2) + b2
        y = layernorm(y + ff, g3, beta3)
        return y

    def _L1_ffn_ref(x_btd, Wr, br, W1, b1, W2, b2):
        import jax, jax.numpy as jnp
        import numpy as np
        import math
        E = 8
        K = 2
        CF = 1.2
        D = 128
        H = 512
        B, T, Dm = x_btd.shape
        N = B * T
        x = x_btd.reshape(N, Dm)
        cap = int(math.ceil(CF * N / E))
        probs = jax.nn.softmax(x @ Wr + br, axis=-1)
        gates, ids = jax.lax.top_k(probs, K)
        flat_ids = ids.reshape(-1)
        flat_g = gates.reshape(-1)
        M = N * K
        order = jnp.lexsort((-flat_g, flat_ids))
        s_ids = flat_ids[order]
        s_tok = (order // K).astype(jnp.int32)
        s_g = flat_g[order]
        counts = jnp.bincount(flat_ids, length=E)
        starts = jnp.concatenate([jnp.zeros((1,), counts.dtype), jnp.cumsum(counts)[:-1]])
        rank = jnp.arange(M) - starts[s_ids]
        valid = rank < cap
        pos = jnp.where(valid, s_ids * cap + rank, E * cap)
        disp_tok = jnp.zeros((E * cap + 1,), jnp.int32).at[pos].set(s_tok)[:E * cap]
        disp_g = jnp.zeros((E * cap + 1,), x.dtype).at[pos].set(s_g)[:E * cap]
        xg = x[disp_tok].reshape(E, cap, Dm)
        h = jax.nn.silu(jnp.einsum('ecd,edh->ech', xg, W1) + b1[:, None, :])
        out = jnp.einsum('ech,ehd->ecd', h, W2) + b2[:, None, :]
        gated = out * disp_g.reshape(E, cap, 1)
        y = jnp.zeros((N, Dm), x.dtype).at[disp_tok].add(gated.reshape(E * cap, Dm))
        return y.reshape(B, T, Dm)

    def _L2_xattn_ref(q, k, v, mask, gamma, beta):
        import jax, jax.numpy as jnp
        import numpy as np
        NEG = -9000000000000000.0
        EPS = 1e-05
        d_k = q.shape[-1]
        logits = jnp.einsum('bsd,btd->bst', q, k) / jnp.sqrt(jnp.asarray(d_k, q.dtype))
        logits = jnp.where(mask == 0, jnp.asarray(NEG, logits.dtype), logits)
        attn = jax.nn.softmax(logits, axis=-1)
        x = jnp.einsum('bst,btd->bsd', attn, v)
        mu = jnp.mean(x, axis=-1, keepdims=True)
        var = jnp.mean(jnp.square(x - mu), axis=-1, keepdims=True)
        xhat = (x - mu) * jax.lax.rsqrt(var + EPS)
        return xhat * gamma + beta

    def _L2_ffn_ref(x, gate_w, gate_b, We1, be1, We2, be2, We3, be3, ws1, bs1, ws2, bs2, ws3, bs3):
        import jax, jax.numpy as jnp
        import numpy as np
        DIM = 128
        E = 16
        TOPK = 2
        G = 4
        TOPK_G = 2
        INTER = 64
        N_SHARED = 2
        ROUTE_SCALE = 1.0

        def _gate(xf, gate_w, gate_b):
            scores = xf @ gate_w.T
            scores = jax.nn.softmax(scores.astype(jnp.float32), axis=-1)
            orig = scores
            scores = scores + gate_b
            T = xf.shape[0]
            sg = scores.reshape(T, G, E // G)
            group_scores = jax.lax.top_k(sg, 2)[0].sum(-1)
            _, gidx = jax.lax.top_k(group_scores, TOPK_G)
            keep = jax.nn.one_hot(gidx, G).sum(axis=1) > 0
            sg = jnp.where(keep[:, :, None], sg, -jnp.inf)
            scores = sg.reshape(T, E)
            _, idx = jax.lax.top_k(scores, TOPK)
            weights = jnp.take_along_axis(orig, idx, axis=1)
            weights = (weights * ROUTE_SCALE).astype(xf.dtype)
            return (weights, idx)
        shape = x.shape
        xf = x.reshape(-1, DIM)
        weights, idx = _gate(xf, gate_w, gate_b)
        combine = (jax.nn.one_hot(idx, E, dtype=xf.dtype) * weights[..., None]).sum(1)
        h1 = jnp.einsum('td,edi->tei', xf, We1) + be1
        h3 = jnp.einsum('td,edi->tei', xf, We3) + be3
        h = jax.nn.silu(h1) * h3
        yo = jnp.einsum('tei,eid->ted', h, We2) + be2
        y = jnp.einsum('te,ted->td', combine, yo)
        z = jax.nn.silu(xf @ ws1 + bs1) * (xf @ ws3 + bs3) @ ws2 + bs2
        return (y + z).reshape(shape)

    def _L3_xattn_ref(k, v, q, mask, Wk, bk, Wv, bv, Wq, bq, Woff, boff, Wo, bo):
        import jax, jax.numpy as jnp
        import numpy as np
        import math
        B, M, D, H, NK = (4, 256, 128, 16, 5)
        HD = D // H

        def _gather_pad0(x, idx):
            Bx, Hx, W, hd = x.shape
            valid = (idx >= 0) & (idx < W)
            idxc = jnp.clip(idx, 0, W - 1).reshape(Bx, Hx, -1)
            g = jnp.take_along_axis(x, idxc[..., None], axis=2)
            g = g.reshape(idx.shape + (hd,))
            return g * valid[..., None].astype(x.dtype)
        Bq, Q, _ = q.shape
        key_len = k.shape[1]
        K = jnp.einsum('bmd,ed->bme', k, Wk) + bk
        V = jnp.einsum('bmd,ed->bme', v, Wv) + bv
        Qp = jnp.einsum('bqd,ed->bqe', q, Wq) + bq
        off = jnp.einsum('bqd,ed->bqe', Qp, Woff) + boff
        off = off.reshape(Bq, Q, H, NK).transpose(0, 2, 1, 3)
        Kh = K.reshape(Bq, key_len, H, HD).transpose(0, 2, 1, 3)
        Vh = V.reshape(Bq, key_len, H, HD).transpose(0, 2, 1, 3)
        Qh = Qp.reshape(Bq, Q, H, HD).transpose(0, 2, 1, 3)
        loc = jnp.arange(Q, dtype=jnp.float32)[:, None]
        left = -NK // 2
        ref = jnp.arange(left, NK + left, dtype=jnp.float32)
        sign_lens = (1 - mask).sum(-1).astype(jnp.float32) - 1.0
        loc_x = jnp.mod(ref + off + loc, sign_lens[:, None, None, None])
        xg = loc_x / (key_len - 1) * 2.0 - 1.0
        ix = ((xg + 1.0) * key_len - 1.0) / 2.0
        x0 = jnp.floor(ix)
        dx = ix - x0
        i0 = x0.astype(jnp.int32)
        i1 = i0 + 1
        w0 = (1.0 - dx)[..., None]
        w1 = dx[..., None]
        sk = 0.5 * (w0 * _gather_pad0(Kh, i0) + w1 * _gather_pad0(Kh, i1))
        sv = 0.5 * (w0 * _gather_pad0(Vh, i0) + w1 * _gather_pad0(Vh, i1))
        scores = jnp.einsum('bhqd,bhqkd->bhqk', Qh / math.sqrt(HD), sk)
        attn = jax.nn.softmax(scores, axis=-1)
        ctx = jnp.einsum('bhqk,bhqkd->bhqd', attn, sv)
        ctx = ctx.transpose(0, 2, 1, 3).reshape(Bq, Q, H * HD)
        return jnp.einsum('bqd,ed->bqe', ctx, Wo) + bo

    def _L3_ffn_ref(x, Wg, bg, W1, b1, W2, b2):
        import jax, jax.numpy as jnp
        import numpy as np
        TOP_K = 2
        TEMP = 1.0
        gates = (jnp.einsum('bsd,de->bse', x, Wg) + bg) / (TEMP + 1e-06)
        weights, indices = jax.lax.top_k(gates, TOP_K)
        weights = jax.nn.softmax(weights, axis=-1)
        h = jax.nn.silu(jnp.einsum('bsd,edf->bsef', x, W1) + b1)
        all_out = jnp.einsum('bsef,efd->bsed', h, W2) + b2
        gathered = jnp.take_along_axis(all_out, indices[..., None], axis=2)
        out = jnp.sum(gathered * weights[..., None], axis=2)
        return out
    x = x + _L0_xattn_ref(_layernorm(x, axis=-1), ctx_1024, mask_BxS2_ik0, L0_xattn_WQ, L0_xattn_WK, L0_xattn_WV, L0_xattn_WO)
    x = x + _L0_ffn_ref(_layernorm(x, axis=-1), L0_ffn_ln_g, L0_ffn_ln_b, L0_ffn_Wr, L0_ffn_W1, L0_ffn_W3, L0_ffn_W2, L0_ffn_W1s, L0_ffn_W3s, L0_ffn_W2s)
    x = x + _L1_xattn_ref(_layernorm(x, axis=-1), ctx_1024, L1_xattn_w1, L1_xattn_b1, L1_xattn_w2, L1_xattn_b2, L1_xattn_g1, L1_xattn_beta1, L1_xattn_g2, L1_xattn_beta2, L1_xattn_g3, L1_xattn_beta3)
    x = x + _L1_ffn_ref(_layernorm(x, axis=-1), L1_ffn_Wr, L1_ffn_br, L1_ffn_W1, L1_ffn_b1, L1_ffn_W2, L1_ffn_b2)
    x = x + _L2_xattn_ref(_layernorm(x, axis=-1), ctx_1024, ctx_1024, mask_BxSxS2_ik1, L2_xattn_gamma, L2_xattn_beta)
    x = x + _L2_ffn_ref(_layernorm(x, axis=-1), L2_ffn_gate_w, L2_ffn_gate_b, L2_ffn_We1, L2_ffn_be1, L2_ffn_We2, L2_ffn_be2, L2_ffn_We3, L2_ffn_be3, L2_ffn_ws1, L2_ffn_bs1, L2_ffn_ws2, L2_ffn_bs2, L2_ffn_ws3, L2_ffn_bs3)
    x = x + _L3_xattn_ref(ctx_1024, ctx_1024, _layernorm(x, axis=-1), mask_BxS2_if0, L3_xattn_Wk, L3_xattn_bk, L3_xattn_Wv, L3_xattn_bv, L3_xattn_Wq, L3_xattn_bq, L3_xattn_Woff, L3_xattn_boff, L3_xattn_Wo, L3_xattn_bo)
    x = x + _L3_ffn_ref(_layernorm(x, axis=-1), L3_ffn_Wg, L3_ffn_bg, L3_ffn_W1, L3_ffn_b1, L3_ffn_W2, L3_ffn_b2)
    return x

_drawn_inputs = setup_inputs


def setup_inputs(seed=0):
    import zlib

    import numpy as np

    out = dict(_drawn_inputs(seed))
    spreads = {'L0_ffn_ln_g': (1.0, 0.6),
     'L0_ffn_ln_b': (0.0, 0.8),
     'L1_xattn_b1': (0.0, 0.378),
     'L1_xattn_b2': (0.0, 0.272),
     'L1_xattn_g1': (1.0, 0.2),
     'L1_xattn_beta1': (0.0, 0.1),
     'L1_xattn_g2': (1.0, 0.2),
     'L1_xattn_beta2': (0.0, 0.273),
     'L1_xattn_g3': (1.0, 0.2),
     'L1_xattn_beta3': (0.0, 0.1),
     'L1_ffn_br': (0.0, 0.436),
     'L1_ffn_b1': (0.0, 0.535),
     'L1_ffn_b2': (0.0, 0.33),
     'L2_xattn_gamma': (1.0, 0.2),
     'L2_xattn_beta': (0.0, 0.268),
     'L2_ffn_gate_b': (0.0, 0.1),
     'L2_ffn_be1': (0.0, 0.8),
     'L2_ffn_be2': (0.0, 0.601),
     'L2_ffn_be3': (0.0, 0.61),
     'L2_ffn_bs1': (0.0, 0.272),
     'L2_ffn_bs2': (0.0, 0.286),
     'L2_ffn_bs3': (0.0, 0.287),
     'L3_xattn_bk': (0.0, 2.0),
     'L3_xattn_bv': (0.0, 0.731),
     'L3_xattn_bq': (0.0, 0.8),
     'L3_xattn_boff': (0.0, 0.8),
     'L3_xattn_bo': (0.0, 0.333),
     'L3_ffn_bg': (0.0, 0.1),
     'L3_ffn_b1': (0.0, 0.475),
     'L3_ffn_b2': (0.0, 0.3)}
    factors = {'L0_ffn_Wr': 4.908,
     'L0_ffn_W1': 4.333,
     'L0_ffn_W3': 4.609,
     'L0_ffn_W2': 4.705,
     'L0_ffn_W1s': 3.111,
     'L0_ffn_W3s': 3.241,
     'L0_ffn_W2s': 3.179,
     'L3_xattn_Wk': 8.0,
     'L3_xattn_Wv': 5.099,
     'L3_xattn_Wq': 8.0,
     'L3_xattn_Woff': 8.0,
     'L3_xattn_Wo': 4.737}
    for name, (base, spread) in spreads.items():
        noise = np.random.default_rng([zlib.crc32(name.encode()), seed]).standard_normal(out[name].shape)
        drawn = base * np.exp(spread * noise) if base else spread * noise
        out[name] = jnp.asarray(drawn.astype(out[name].dtype))
    for name, factor in factors.items():
        out[name] = (out[name] * factor).astype(out[name].dtype)
    return out
```

```python
from contextlib import ExitStack

import concourse.bass as bass
from concourse import mybir
import numpy as np

F32 = mybir.dt.float32
I32 = mybir.dt.int32
U32 = mybir.dt.uint32
ALU = mybir.AluOpType
ACT = mybir.ActivationFunctionType
X_AX = mybir.AxisListType.X

P = 128
B, S, D = 32, 64, 128
NT = B * S // P
GT = 4
NG = NT // GT
GW = GT * P
GB = GW // S
H = 16
HD = D // H
NK = 5
F = 512
FB = F // P
E = 8
EG, EI = 16, 64
CAP0 = -(-125 * 2 * 1024 // (100 * 7))
CAP1 = -(-12 * B * S // (10 * 8))
NEG = -1.0e30
STAGES = 8

CONST = {}
_at = 0
for _name, _w in (("ident", P), ("ones", P), ("upto", P), ("causal2", P), ("same2", P), ("offdiag", P),
                  ("causal", S), ("headpair", P), ("headhalf", P), ("headquad", 4), ("spread", P), ("negm", 1), ("iota", 16),
                  ("neghalf", 1), ("ref", 1), ("loc", GW), ("bits", 30)):
    CONST[_name] = (_at, _w)
    _at += _w
NCONST = _at


def constants():
    t = np.zeros((P, NCONST), np.float32)

    def put(name, a):
        t[:, CONST[name][0]:CONST[name][0] + CONST[name][1]] = a

    p, c = np.arange(P)[:, None], np.arange(P)[None, :]
    same = p // S == c // S
    put("ident", p == c)
    put("ones", np.ones((P, P)))
    put("upto", p <= c)
    put("causal2", np.where(same & (c <= p), 0.0, NEG))
    put("same2", np.where(same, 0.0, NEG))
    put("offdiag", same)
    put("causal", np.where(np.arange(S)[None, :] > p % S, -1.0e9, 0.0))
    put("headpair", (c // HD) % 2 == p // S)
    put("headhalf", ((c // HD) % 2 == p // S) * -0.5)
    put("headquad", (p // HD) % 4 == np.arange(4)[None, :])
    put("spread", (c // HD == p // HD + 2) & ((c // HD) % 4 >= 2))
    put("negm", -(p % S))
    put("iota", np.arange(16)[None, :])
    put("neghalf", np.full((P, 1), -0.5))
    put("ref", p % NK - 3.0)
    put("loc", np.arange(GW)[None, :] % S)
    put("bits", (2 ** np.arange(29, -1, -1, dtype=np.int32)).view(np.float32)[None, :])
    return t


_NORM = dict(var_ready=1, rstd_ready=1)
_TURN = dict(rows_ready=1, turned=1, cols_ready=1)
_SOFT = dict(sc_ps=1, sm_in=1, ex_ready=1, pt_ps=1, pt_ready=1, av_ps=1)


def _times(n, d):
    return {k: v * n for k, v in d.items()}


PLAN = [
    ("pre", NG, dict(turned=1, cols_ready=1)),
    ("a0", NG, dict(**_NORM, **_times(2, _TURN), ct_staged=1, qk_ps=1, q_ready=1, kb_ready=1, v_ps=1, vb_ready=1,
                    **_times(GT, _SOFT), sc_read=GT, out_ps=1, x_ready=1, dve=18)),
    ("r0", NG, dict(**_times(2, _NORM), **_TURN, ht_ready=1, lg_ps=1, lg_ready=1, dve=7)),
    ("g0", 1, dict(exp_in=1, exp_ready=1, cum_in=1, cum_ps=1, c_ready=1, dve=18)),
    ("f0", NT, dict(h_staged=1, h_ps=E, act_ready=E, mid_ready=E, mid_ps=E, midT_ready=E, y_ps=1, x_ready=1)),
    ("a1", NG, dict(**_times(4, _NORM), **_times(3, _TURN), **_times(2, _SOFT), h_ps=1, mid_ready=1, y_ps=1,
                    x_ready=1, dve=27)),
    ("r1", NG, dict(**_NORM, **_TURN, ht_ready=1, lg_ps=1, exp_in=1, exp_ready=1, lg_ready=1, dve=6)),
    ("t1", 1, dict(dve=7)),
    ("b1", 30, dict(cum_in=1, cum_ps=1, dve=4)),
    ("g1", 1, dict(cum_in=1, cum_ps=1, c_ready=1, dve=12)),
    ("f1", NT, dict(h_staged=1, c_in=1, c_turned=1, cT_ready=1, h_ps=E, act_in=E, act_ready=E, mid_ready=E, mid_ps=E,
                    midT_ready=E, y_ps=1, x_ready=1)),
    ("a2", NG, dict(**_times(2, _NORM), **_TURN, **_SOFT, x_ready=1, dve=17)),
    ("r2", NG, dict(**_NORM, **_TURN, ht_ready=1, lg_ps=1, exp_in=1, exp_ready=1, lg_ready=1, dve=5)),
    ("g2", 1, dict(c_ready=1, dve=17)),
    ("f2", NT, dict(h_staged=1, c_in=1, c_turned=1, cT_ready=1, h_ps=3, act_in=3, act_ready=3, mid_ready=3, mid_ps=3,
                    midT_ready=3, y_ps=1, x_ready=1, dve=7)),
    ("m3", 1, dict(dve=6)),
    ("a3", NG, dict(**_NORM, **_TURN, ct_staged=1, q_ps=1, q_ready=1, off_ps=1, ix_ready=1, k_ps=1, k_read=1, v_ps=1,
                    kv_ready=1, gap_ps=48, gap_ready=48, hat_ready=48, skv_ps=16, prod_ready=16, score_ps=16,
                    sm_in=16, ex_ready=16, o_ready=16, out_ps=1, x_ready=1, dve=67)),
    ("r3", NG, dict(**_NORM, **_TURN, ht_ready=1, lg_ps=1, lg_ready=1, dve=3)),
    ("g3", 1, dict(exp_in=1, exp_ready=1, c_ready=1, dve=8)),
    ("f3", NT, dict(h_staged=1, c_in=1, c_turned=1, cT_ready=1, h_ps=E, act_in=E, act_ready=E, mid_ready=E, mid_ps=E,
                    midT_ready=E, y_ps=1, x_ready=1)),
]
EARLY = ("ht_ready", "v_ps", "y_ps", "c_turned")
SIGNALS = sorted({name for _, _, rises in PLAN for name in rises})
LAST = {1: "a0", 2: "f0", 3: "a1", 4: "f1", 5: "a2", 6: "f2", 7: "a3", 8: "f3"}[STAGES]
LOOPS = {stage: turns for stage, turns, _ in PLAN}
ORDER = [stage for stage, _, _ in PLAN][:[stage for stage, _, _ in PLAN].index(LAST) + 1]


def count(stage, name, turn=0, k=0):
    base = int(name in EARLY)
    for s, turns, rises in PLAN:
        if s == stage:
            return turn * rises.get(name, 0) + (base + k)
        base += turns * rises.get(name, 0)


def total(stage, name):
    turns, rises = {s: (t, r) for s, t, r in PLAN}[stage]
    return count(stage, name, turns)


def build(nc, t, out):
    with ExitStack() as ctx:
        def sb(name, shape, dt=F32):
            return ctx.enter_context(nc.sbuf_tensor(name, shape, dt))

        ps = ctx.enter_context(nc.psum_tensor("ps", [P, 8, 512], F32))
        sem = {n: ctx.enter_context(nc.semaphore(n)) for n in SIGNALS}
        loads = {n: ctx.enter_context(nc.semaphore("load_" + n)) for n in
                 ("pre", "a0", "f0", "a1", "f1", "a2", "f2", "a3", "f3")}
        s_out = ctx.enter_context(nc.semaphore("s_out"))
        s_keep = ctx.enter_context(nc.semaphore("s_keep"))
        s_init = ctx.enter_context(nc.semaphore("s_init"))

        xs = sb("xs", [P, NT, D])
        cs = sb("cs", [P, NT, D])
        cT = sb("cT", [P, B * S])
        hT = sb("hT", [P, B * S])
        con = sb("con", [P, NCONST])
        wa = sb("wa", [P, 8 * 1536])
        wb = sb("wb", [P, 8 * 1024 + 8 * 512])
        wsm = sb("wsm", [P, 3200])
        work = sb("work", [P, 11500])
        m0i = sb("m0i", [P, NT], I32)
        m2i = sb("m2i", [P, NT, S], I32)
        qkeep = sb("qkeep", [P, NT])
        slack = sb("slack", [P, 2])
        lg = sb("lg", [P, NT, 16])
        comb = sb("comb", [P, NT, 18])
        ident, ones = [con[:, CONST[n][0]:CONST[n][0] + P] for n in ("ident", "ones")]

        def const(name, rows=P):
            a, w = CONST[name]
            return con[0:rows, a:a + w]

        place = {"wsm": 0}

        def small(name, w, rows=P):
            a = place["wsm"]
            place["wsm"] += w
            return wsm[0:rows, a:a + w]

        wq0, wk0, wv0, wo0 = [small(n, P) for n in ("wq", "wk", "wv", "wo")]
        g_ln, b_ln = small("g", D), small("b", D)
        wr0 = small("wr0", 8)
        w1a = small("w1a", F)
        w2a = small("w2a", F).rearrange("p (f d) -> p f d", f=FB)
        b1a = small("b1a", FB)
        b2a = small("b2a", D)
        ga = [small(f"g{n}", D) for n in range(3)]
        ba = [small(f"b{n}", D) for n in range(3)]
        wr1, br1 = small("wr1", E), small("br1", E)
        b2f1 = small("b2f1", D, E)
        end1 = place["wsm"]
        place["wsm"] = 0
        g2, be2 = small("g2", D), small("be2", D)
        wg2, gb2 = small("wg2", EG), small("gb2", EG)
        b2f2 = small("b2f2", D, 18)
        wq3, wk3, wv3 = [small(n, P) for n in ("wq3", "wk3", "wv3")]
        bk3, bv3, bo3 = [small(n, P) for n in ("bk3", "bv3", "bo3")]
        woff3 = small("woff3", H * NK)
        boff3, bq3, bqx3 = small("boff3", 1), small("bq3", 1), small("bqx3", 2)
        wqx3 = small("wqx3", 2 * P).rearrange("p (h c) -> p h c", h=2)
        wox3 = small("wox3", 2 * P).rearrange("p (h c) -> p h c", h=2)
        wg3, bg3 = small("wg3", E), small("bg3", E)
        b2f3 = small("b2f3", D, E)
        assert max(end1, place["wsm"]) <= 3200, (end1, place["wsm"])

        W1 = wa[:, 0:8 * F].rearrange("p (e f) -> p e f", e=E)
        W3 = wa[:, 8 * F:16 * F].rearrange("p (e f) -> p e f", e=E)
        W2 = wa[:, 16 * F:24 * F].rearrange("p (e f d) -> p e f d", e=E, f=FB)
        V1 = wb[:, 0:8 * F].rearrange("p (e f) -> p e f", e=E)
        V2 = wb[:, 8 * F:16 * F].rearrange("p (e f d) -> p e f d", e=E, f=FB)
        VB1 = wb[:, 16 * F:24 * F].rearrange("p (e f) -> p e f", e=E)
        NU = 18 * EI
        U1, U3 = wa[:, 0:NU], wa[:, NU:2 * NU]
        U2 = wa[:, 2 * NU:3 * NU].rearrange("p (f d) -> p f d", f=9)
        UB1, UB3 = wa[:, 3 * NU:4 * NU], wa[:, 4 * NU:5 * NU]

        def carve(start, *shape):
            n = int(np.prod(shape))
            ap = work[:, start:start + n]
            if len(shape) == 2:
                ap = ap.rearrange("p (a b) -> p a b", a=shape[0])
            if len(shape) == 3:
                ap = ap.rearrange("p (a b c) -> p a b c", a=shape[0], b=shape[1])
            return ap

        stats, mv = carve(0, GT, 6), carve(24, GT, 2)
        var, rstd = carve(32, GT), carve(36, GT)
        mx, sm, rs = carve(40, 4 * H), carve(104, 4 * H), carve(168, 4 * H)
        XH, XT = carve(232, GT, D), carve(744, GW)
        N0 = 1256
        names = {}

        def body(name):
            def wrap(f):
                names[name] = f
                return f
            return wrap

        class Chain:

            def __init__(self, eng):
                self.eng = eng

            def start(self, stage, turn):
                self.stage, self.turn, self.k = stage, turn, 0

            def __call__(self, ins):
                self.k += 1
                ins.then_inc(sem["dve"], 1)
                self.eng.wait_ge(sem["dve"], count(self.stage, "dve", self.turn, self.k))

            def end(self):
                plan = {s: r.get("dve", 0) for s, _, r in PLAN}[self.stage]
                assert plan == self.k, (self.stage, self.k)

        def group(ap, i):
            return ap[:, bass.ds(i * GT, GT)]

        def cols(ap, i, w=GW):
            return ap[:, bass.ds(i * w, w)]

        def norm_dve(eng, link, stage, i, k, src, dst, signal=None):
            for j in range(GT):
                last = eng.bn_stats(stats[:, j, :], src[:, j, :])
            link(last)
            eng.memset(slack[:, 0:1], 0.0)
            for j in range(GT):
                last = eng.bn_aggr(mv[:, j, :], stats[:, j, :])
            link(last)
            eng.tensor_scalar(var, mv[:, :, 1], 1.0e-5, None, ALU.add).then_inc(sem["var_ready"], 1)
            eng.wait_ge(sem["rstd_ready"], count(stage, "rstd_ready", i, k))
            for j in range(GT):
                last = eng.tensor_scalar(dst[:, j, :], src[:, j, :], mv[:, j, 0:1], rstd[:, j:j + 1],
                                         ALU.subtract, ALU.mult)
            if signal is None:
                link(last)
            else:
                last.then_inc(sem[signal], 1)

        def norm_pool(eng, stage, i, k):
            eng.wait_ge(sem["var_ready"], count(stage, "var_ready", i, k))
            eng.tensor_tensor(rstd, var, const("neghalf").to_broadcast([P, GT]), ALU.pow)\
               .then_inc(sem["rstd_ready"], 1)

        def turn_pe(eng, stage, i, k, src, bank=0):
            eng.wait_ge(sem["rows_ready"], count(stage, "rows_ready", i, k))
            for j in range(GT):
                last = eng.transpose(ps[:, bank, j * P:(j + 1) * P], src[:, j, :], ident)
            last.then_inc(sem["turned"], 1)

        def turn_act(eng, stage, i, k, dst, bank=0):
            eng.wait_ge(sem["turned"], count(stage, "turned", i, k))
            eng.activation(dst, ps[:, bank, :], ACT.Copy).then_inc(sem["cols_ready"], 1)

        def wait_loads(eng, *which):
            for n in which:
                eng.wait_ge(loads[n], 16 * len(load_list[n]))

        def heads(ap):
            return ap.rearrange("p (h d) -> p h d", h=H)

        def b3(ap, n, at):
            a = ap.shape[1]
            return ap.unsqueeze(at).to_broadcast([ap.shape[0], a, n] if at == 2 else [ap.shape[0], n, a])

        QT = carve(N0, GW)
        CTD = carve(N0 + 512, GB, 2 * S)
        KB = carve(N0 + 1536, GB, 4, S)
        VB = carve(N0 + 3584, GB, D)
        S0 = carve(N0 + 4608, 2, H * S)
        E0 = carve(N0 + 6656, 2, H * S)
        PT0 = carve(N0 + 8704, 8, P)
        OT = QT
        MT = lg[:, :, :].rearrange("p a b -> p (a b)")
        O0 = XH

        def dup(b):
            return CTD[:, b, :]

        def a0_pe(eng, i):
            st = "a0"
            turn_pe(eng, st, i, 1, XH)
            eng.wait_ge(sem["cols_ready"], count(st, "cols_ready", i, 1))
            eng.wait_ge(sem["ct_staged"], count(st, "ct_staged", i, 1))
            eng.matmul(ps[:, 1, :], wq0, XT, start=True, stop=True)
            eng.matmul(ps[:, 2, :], wk0, cols(cT, i), start=True, stop=True).then_inc(sem["qk_ps"], 1)
            for b in range(GB):
                last = eng.matmul(ps[:, 3 + b // 4, (b % 4) * P:(b % 4 + 1) * P], dup(b), wv0, start=True, stop=True)
            last.then_inc(sem["v_ps"], 1)

            def scores(j):
                if j == 0:
                    eng.wait_ge(sem["q_ready"], count(st, "q_ready", i, 1))
                    eng.wait_ge(sem["kb_ready"], count(st, "kb_ready", i, 1))
                    eng.wait_ge(sem["vb_ready"], count(st, "vb_ready", i, 1))
                else:
                    eng.wait_ge(sem["sc_read"], count(st, "sc_read", i, j))
                for b in range(2):
                    for q in range(4):
                        last = eng.matmul(ps[S * b:S * b + S, 1 + q, (j % 2) * 256:(j % 2) * 256 + 256],
                                          QT[32 * q:32 * q + 32, j * P + S * b:j * P + S * b + S],
                                          KB[32 * q:32 * q + 32, 2 * j + b, :, :],
                                          start=True, stop=True, tile_position=(32 * q, S * b))
                last.then_inc(sem["sc_ps"], 1)

            scores(0)
            for j in range(GT):
                if j + 1 < GT:
                    scores(j + 1)
                eng.wait_ge(sem["ex_ready"], count(st, "ex_ready", i, j + 1))
                if j >= 1:
                    eng.wait_ge(sem["pt_ready"], count(st, "pt_ready", i, j))
                for h in range(8):
                    last = eng.transpose(ps[:, 5 + h // 4, (h % 4) * P:(h % 4 + 1) * P],
                                         E0[:, j % 2, h * P:(h + 1) * P], ident)
                last.then_inc(sem["pt_ps"], 1)
                eng.wait_ge(sem["pt_ready"], count(st, "pt_ready", i, j + 1))
                for b in range(2):
                    for h in range(8):
                        last = eng.matmul(ps[S * b:S * b + S, 7, j * P + 16 * h:j * P + 16 * h + 16],
                                          PT0[:, h, S * b:S * b + S], VB[:, 2 * j + b, 16 * h:16 * h + 16],
                                          start=True, stop=True, tile_position=(0, S * b))
                last.then_inc(sem["av_ps"], 1)
            turn_pe(eng, st, i, 2, O0)
            eng.wait_ge(sem["cols_ready"], count(st, "cols_ready", i, 2))
            for j in range(GT):
                last = eng.matmul(ps[:, 1, j * P:(j + 1) * P], OT[:, j * P:(j + 1) * P], wo0, start=True, stop=True)
            last.then_inc(sem["out_ps"], 1)

        def a0_act(eng, i):
            st = "a0"
            turn_act(eng, st, i, 1, XT)
            eng.wait_ge(sem["qk_ps"], count(st, "qk_ps", i, 1))
            eng.activation(QT, ps[:, 1, :], ACT.Copy).then_inc(sem["q_ready"], 1)

            def exp(j):
                eng.wait_ge(sem["sm_in"], count(st, "sm_in", i, j + 1))
                eng.activation(E0[:, j % 2, :], S0[:, j % 2, :], ACT.Exp, scale=HD ** -0.5)\
                   .then_inc(sem["ex_ready"], 1)

            exp(0)
            for j in range(GT):
                if j + 1 < GT:
                    exp(j + 1)
                eng.wait_ge(sem["pt_ps"], count(st, "pt_ps", i, j + 1))
                eng.activation(PT0.rearrange("p a b -> p (a b)"), ps[:, 5:7, :].rearrange("p a b -> p (a b)"),
                               ACT.Copy).then_inc(sem["pt_ready"], 1)
            turn_act(eng, st, i, 2, OT)

        def a0_dve(eng, link, i):
            st = "a0"
            link.start(st, i)
            norm_dve(eng, link, st, i, 1, group(xs, i), XH, "rows_ready")
            eng.wait_ge(sem["qk_ps"], count(st, "qk_ps", i, 1))
            last = None
            for b in range(GB):
                last = eng.tensor_tensor(KB[:, b, :, :], b3(ps[:, 2, b * S:(b + 1) * S], 4, 1),
                                         b3(const("headquad"), S, 2), ALU.mult)
            last.then_inc(sem["kb_ready"], 1)
            eng.wait_ge(sem["v_ps"], count(st, "v_ps", i, 1))
            last = eng.tensor_tensor(VB, ps[:, 3:5, :].rearrange("p a (b c) -> p (a b) c", b=4),
                                     b3(const("headpair"), GB, 1), ALU.mult)
            last.then_inc(sem["vb_ready"], 1)

            def before(j):
                sj, sh = S0[:, j % 2, :], heads(S0[:, j % 2, :])
                keep = qkeep[:, bass.ds(i * GT + j, 1)]
                link(eng.tensor_scalar(MT.rearrange("p (h s) -> p h s", s=S), b3(const("causal"), 4, 1), keep, None,
                                       ALU.mult))
                eng.wait_ge(sem["sc_ps"], count(st, "sc_ps", i, j + 1))
                half = (j % 2) * 4 * S
                eng.scalar_tensor_tensor(out=sj.rearrange("p (q c) -> p q c", q=4),
                                         in0=ps[:, 1:5, half:half + 4 * S], scalar=keep, in1=b3(MT, 4, 1),
                                         op0=ALU.mult, op1=ALU.add).then_inc(sem["sc_read"], 1)
                eng.wait_ge(sem["sc_read"], count(st, "sc_read", i, j + 1))
                m = mx[:, H * j:H * j + H]
                link(eng.tensor_reduce(m, sh, X_AX, ALU.max))
                eng.tensor_tensor(sh, sh, b3(m, S, 2), ALU.subtract).then_inc(sem["sm_in"], 1)

            before(0)
            for j in range(GT):
                if j + 1 < GT:
                    before(j + 1)
                eng.wait_ge(sem["ex_ready"], count(st, "ex_ready", i, j + 1))
                link(eng.reduce_sum(sm[:, H * j:H * j + H], heads(E0[:, j % 2, :]), X_AX))
                link(eng.reciprocal(rs[:, H * j:H * j + H], sm[:, H * j:H * j + H]))
            eng.wait_ge(sem["av_ps"], count(st, "av_ps", i, GT))
            for j in range(GT):
                last = eng.tensor_tensor(heads(O0[:, j, :]), heads(ps[:, 7, j * P:(j + 1) * P]),
                                         b3(rs[:, H * j:H * j + H], HD, 2), ALU.mult)
            last.then_inc(sem["rows_ready"], 1)
            eng.wait_ge(sem["out_ps"], count(st, "out_ps", i, 1))
            g = group(xs, i)
            eng.tensor_tensor(g, g, ps[:, 1, :].rearrange("p (a b) -> p a b", a=GT), ALU.add)\
               .then_inc(sem["x_ready"], 1)
            link.end()

        def bridge(eng):
            one = const("ref")
            eng.tensor_tensor(slack[:, 1:2], one, one, ALU.add)

        def stage_ct(eng, stage, i):
            eng.wait_ge(sem["v_ps"], count(stage, "v_ps", i, 0))
            bridge(eng)
            src = cols(cT, i).rearrange("p (b s) -> p b s", b=GB).unsqueeze(2).to_broadcast([P, GB, 2, S])
            eng.tensor_copy(CTD.rearrange("p b (r s) -> p b r s", r=2), src).then_inc(sem["ct_staged"], 1)

        def logits_pe(eng, st, i, w, n):
            turn_pe(eng, st, i, 1, XH)
            eng.wait_ge(sem["cols_ready"], count(st, "cols_ready", i, 1))
            for j in range(GT):
                last = eng.matmul(ps[:, 1, j * n:(j + 1) * n], XT[:, j * P:(j + 1) * P], w, start=True, stop=True)
            last.then_inc(sem["lg_ps"], 1)

        def logits_act(eng, st, i, softmax, n):
            if i is not None:
                eng.wait_ge(sem["ht_ready"], count(st, "ht_ready", i, 0))
            turn_act(eng, st, i, 1, XT)
            if softmax:
                eng.wait_ge(sem["exp_in"], count(st, "exp_in", i, 1))
                eng.activation(LS[:, 0:GT * n], LS[:, 0:GT * n], ACT.Exp).then_inc(sem["exp_ready"], 1)

        def logits_pool(eng, st, i):
            eng.wait_ge(sem["cols_ready"], count(st, "cols_ready", i, 1))
            bridge(eng)
            eng.tensor_copy(cols(hT, i), XT).then_inc(sem["ht_ready"], 1)

        LS = carve(N0, 64)

        def logits_dve(eng, link, st, i, n, bias=None, scale=None, softmax=False):
            eng.wait_ge(sem["lg_ps"], count(st, "lg_ps", i, 1))
            raw = ps[:, 1, 0:GT * n].rearrange("p (a b) -> p a b", a=GT)
            to = group(lg, i)[:, :, 0:n]
            ls = LS[:, 0:GT * n].rearrange("p (a b) -> p a b", a=GT)
            if bias is None and not softmax:
                eng.tensor_copy(to, raw).then_inc(sem["lg_ready"], 1)
                return
            if bias is not None:
                link(eng.tensor_tensor(ls, raw, b3(bias, GT, 1), ALU.add))
                raw = ls
            if not softmax:
                eng.tensor_scalar(to, ls, scale, None, ALU.mult).then_inc(sem["lg_ready"], 1)
                return
            link(eng.tensor_reduce(mx[:, 0:GT], raw, X_AX, ALU.max))
            eng.tensor_tensor(ls, raw, b3(mx[:, 0:GT], n, 2), ALU.subtract).then_inc(sem["exp_in"], 1)
            eng.wait_ge(sem["exp_ready"], count(st, "exp_ready", i, 1))
            link(eng.reduce_sum(sm[:, 0:GT], ls, X_AX))
            link(eng.reciprocal(rs[:, 0:GT], sm[:, 0:GT]))
            eng.tensor_tensor(to, ls, b3(rs[:, 0:GT], n, 2), ALU.mult).then_inc(sem["lg_ready"], 1)

        VL, IX = carve(N0, NT, 8), carve(N0 + 128, NT, 8).bitcast(U32)
        IXF = carve(N0 + 256, 2, NT)
        A2 = carve(N0 + 288, 2, NT * 16)
        GATE = carve(N0 + 800, 3, NT)
        T0, T1 = carve(N0 + 1000, 512), carve(N0 + 1512, 512)
        T2, T3 = carve(N0 + 2024, 512), carve(N0 + 2536, 512)
        CUR = carve(N0 + 3048, 8)
        CAND, CNT, SEL = carve(N0 + 3056, 8), carve(N0 + 3064, 8), carve(N0 + 3072, 8)
        GG = carve(N0 + 3080, NT, 8)

        def marks(n):
            return A2[:, :, 0:NT * n].rearrange("p k (t e) -> p k t e", t=NT)

        def top2(eng, link, src, n, wide):
            for q in range(NT):
                last = eng.max(VL[:, q, :], src[:, q, 0:wide])
            link(last)
            for q in range(NT):
                last = eng.max_index(IX[:, q, :], VL[:, q, :], src[:, q, 0:wide])
            link(last)
            link(eng.tensor_copy(IXF, IX[:, :, 0:2].rearrange("p t k -> p k t")))
            for k in range(2):
                last = eng.tensor_tensor(marks(n)[:, k], b3(const("iota")[:, 0:n], NT, 1), b3(IXF[:, k, :], n, 2),
                                         ALU.is_equal)
            return last

        def prefix(eng, link, a, b, n, w):
            step = 1
            while step < n:
                eng.tensor_copy(b[:, 0:step * w], a[:, 0:step * w])
                link(eng.tensor_tensor(b[:, step * w:n * w], a[:, step * w:n * w], a[:, 0:(n - step) * w], ALU.add))
                a, b = b, a
                step *= 2
            return a

        def gates_dve(eng, link, st):
            eng.wait_ge(sem["exp_ready"], count(st, "exp_ready", 0, 1))
            link(eng.tensor_scalar(GATE[:, 0, :], GATE[:, 2, :], 1.0, None, ALU.add))
            link(eng.reciprocal(GATE[:, 0, :], GATE[:, 0, :]))
            link(eng.tensor_tensor(GATE[:, 1, :], GATE[:, 2, :], GATE[:, 0, :], ALU.mult))

        def exp_gate(eng, st):
            eng.wait_ge(sem["exp_in"], count(st, "exp_in", 0, 1))
            eng.activation(GATE[:, 2, :], GATE[:, 2, :], ACT.Exp).then_inc(sem["exp_ready"], 1)

        def tri(t3, n):
            return t3.rearrange("p (t e) -> p t e", e=n)

        def g0_dve(eng, link):
            st = "g0"
            link.start(st, 0)
            eng.wait_ge(sem["lg_ready"], total("r0", "lg_ready"))
            top2(eng, link, lg, 8, 8).then_inc(sem["cum_in"], 1)
            eng.tensor_tensor(GATE[:, 2, :], VL[:, :, 1], VL[:, :, 0], ALU.subtract).then_inc(sem["exp_in"], 1)
            eng.wait_ge(sem["cum_ps"], count(st, "cum_ps", 0, 1))
            link(eng.tensor_copy(T0[:, 0:256], ps[:, 1, 0:256]))
            s = prefix(eng, link, T0, T1, 2 * NT, 8)
            link(eng.tensor_tensor(T2[:, 0:256], s[:, 0:256], ps[:, 1, 0:256], ALU.subtract))
            link(eng.tensor_tensor(T2[:, 0:256], T2[:, 0:256], ps[:, 0, 0:256], ALU.add))
            link(eng.tensor_scalar(T2[:, 0:256], T2[:, 0:256], float(CAP0), None, ALU.is_le))
            gates_dve(eng, link, st)
            eng.wait_ge(sem["cum_in"], count(st, "cum_in", 0, 1))
            link(eng.tensor_tensor(T2[:, 0:256].rearrange("p (k c) -> p k c", k=2),
                                   T2[:, 0:256].rearrange("p (k c) -> p k c", k=2), A2[:, :, 0:128], ALU.mult))
            for k in range(2):
                last = eng.tensor_tensor(tri(T3[:, k * 128:k * 128 + 128], 8), tri(T2[:, k * 128:k * 128 + 128], 8),
                                         b3(GATE[:, k, :], 8, 2), ALU.mult)
            link(last)
            link(eng.tensor_tensor(comb[:, :, 0:8], tri(T3[:, 0:128], 8), tri(T3[:, 128:256], 8), ALU.add))
            eng.memset(comb[:, :, 7:8], 1.0).then_inc(sem["c_ready"], 1)
            link.end()

        def g0_pe(eng):
            eng.wait_ge(sem["cum_in"], count("g0", "cum_in", 0, 1))
            eng.wait_ge(sem["lg_ready"], total("r0", "lg_ready"))
            eng.matmul(ps[:, 0, 0:256], const("upto"), A2[:, :, 0:128], start=True, stop=True)
            eng.matmul(ps[:, 1, 0:256], ones, A2[:, :, 0:128], start=True, stop=True).then_inc(sem["cum_ps"], 1)

        def g3_dve(eng, link):
            st = "g3"
            link.start(st, 0)
            eng.wait_ge(sem["lg_ready"], total("r3", "lg_ready"))
            link(top2(eng, link, lg, 8, 8))
            eng.tensor_tensor(GATE[:, 2, :], VL[:, :, 1], VL[:, :, 0], ALU.subtract).then_inc(sem["exp_in"], 1)
            gates_dve(eng, link, st)
            for k in range(2):
                last = eng.tensor_tensor(tri(T3[:, k * 128:k * 128 + 128], 8), marks(8)[:, k],
                                         b3(GATE[:, k, :], 8, 2), ALU.mult)
            link(last)
            eng.tensor_tensor(comb[:, :, 0:8], tri(T3[:, 0:128], 8), tri(T3[:, 128:256], 8), ALU.add)\
               .then_inc(sem["c_ready"], 1)
            link.end()

        def t1_dve(eng, link):
            link.start("t1", 0)
            eng.wait_ge(sem["lg_ready"], total("r1", "lg_ready"))
            link(top2(eng, link, lg, 8, 8))
            link(eng.tensor_tensor(T0[:, 0:128], A2[:, 0, 0:128], A2[:, 1, 0:128], ALU.add))
            link(eng.tensor_tensor(tri(T1[:, 0:128], 8), lg[:, :, 0:8], tri(T0[:, 0:128], 8), ALU.mult))
            eng.memset(CUR, 0.0)
            link(eng.scalar_tensor_tensor(out=GG.rearrange("p t e -> p (t e)"), in0=T0[:, 0:128], scalar=-1.0,
                                          in1=T1[:, 0:128], op0=ALU.add, op1=ALU.add))
            link.end()

        def b1_dve(eng, link, r):
            st = "b1"
            link.start(st, r)
            bit = con[:, bass.ds(r + CONST["bits"][0], 1)].bitcast(U32)
            link(eng.tensor_tensor(CAND.bitcast(U32), CUR.bitcast(U32), bit.to_broadcast([P, 8]), ALU.bitwise_or))
            ge = T0[:, 0:128].rearrange("p (e t) -> p e t", e=8)
            link(eng.tensor_tensor(ge, GG.rearrange("p t e -> p e t"), b3(CAND, NT, 2), ALU.is_ge))
            eng.reduce_sum(CNT, ge, X_AX).then_inc(sem["cum_in"], 1)
            eng.wait_ge(sem["cum_ps"], count(st, "cum_ps", r, 1))
            link(eng.tensor_scalar(SEL.bitcast(U32), ps[:, 0, 0:8], float(CAP1), None, ALU.is_ge))
            eng.memset(slack[:, 0:1], 0.0)
            link(eng.copy_predicated(CUR.bitcast(U32), SEL.bitcast(U32), CAND.bitcast(U32)))
            link.end()

        def b1_pe(eng, r):
            eng.wait_ge(sem["cum_in"], count("b1", "cum_in", r, 1))
            eng.matmul(ps[:, 0, 0:8], ones, CNT, start=True, stop=True).then_inc(sem["cum_ps"], 1)

        def g1_dve(eng, link):
            st = "g1"
            link.start(st, 0)
            eng.tensor_tensor(tri(T2[:, 0:128], 8), GG, b3(CUR, NT, 1), ALU.is_equal)
            eng.tensor_tensor(tri(T2[:, 128:256], 8), GG, b3(CUR, NT, 1), ALU.is_gt).then_inc(sem["cum_in"], 1)
            eng.wait_ge(sem["cum_ps"], count(st, "cum_ps", 0, 1))
            link(eng.tensor_copy(T0[:, 0:128], ps[:, 1, 0:128]))
            s = prefix(eng, link, T0, T1, NT, 8)
            link(eng.tensor_tensor(T3[:, 0:128], s[:, 0:128], ps[:, 1, 0:128], ALU.subtract))
            link(eng.tensor_tensor(T3[:, 0:128], T3[:, 0:128], ps[:, 0, 0:128], ALU.add))
            link(eng.reduce_sum(CNT, ps[:, 1, 128:256].rearrange("p (t e) -> p e t", e=8), X_AX))
            link(eng.tensor_tensor(tri(T3[:, 0:128], 8), tri(T3[:, 0:128], 8), b3(CNT, NT, 1), ALU.add))
            link(eng.scalar_tensor_tensor(out=T3[:, 0:128], in0=T3[:, 0:128], scalar=float(CAP1), in1=T2[:, 0:128],
                                          op0=ALU.is_le, op1=ALU.mult))
            link(eng.tensor_tensor(T3[:, 0:128], T3[:, 0:128], T2[:, 128:256], ALU.add))
            link(eng.tensor_scalar(T3[:, 0:128], T3[:, 0:128], 1.0, None, ALU.min))
            eng.tensor_tensor(comb[:, :, 0:8], lg[:, :, 0:8], tri(T3[:, 0:128], 8), ALU.mult)\
               .then_inc(sem["c_ready"], 1)
            link.end()

        def g1_pe(eng):
            eng.wait_ge(sem["cum_in"], count("g1", "cum_in", 0, 1))
            eng.matmul(ps[:, 0, 0:256], const("upto"), T2[:, 0:256], start=True, stop=True)
            eng.matmul(ps[:, 1, 0:256], ones, T2[:, 0:256], start=True, stop=True).then_inc(sem["cum_ps"], 1)

        GS = carve(N0 + 3300, NT, 8)

        def g2_dve(eng, link):
            st = "g2"
            link.start(st, 0)
            eng.wait_ge(sem["lg_ready"], total("r2", "lg_ready"))
            eng.memset(GS, NEG)
            link(eng.tensor_tensor(tri(T0[:, 0:256], 16), lg[:, :, :], b3(gb2, NT, 1), ALU.add))
            v = T0[:, 0:256].rearrange("p (g a b) -> p g a b", a=2, b=2)
            hi = T1[:, 0:128].rearrange("p (g a) -> p g a", a=2)
            lo = T1[:, 128:256].rearrange("p (g a) -> p g a", a=2)
            eng.tensor_tensor(hi, v[:, :, :, 0], v[:, :, :, 1], ALU.max)
            link(eng.tensor_tensor(lo, v[:, :, :, 0], v[:, :, :, 1], ALU.min))
            eng.tensor_tensor(T2[:, 0:64], hi[:, :, 0], hi[:, :, 1], ALU.max)
            eng.tensor_tensor(T2[:, 64:128], hi[:, :, 0], hi[:, :, 1], ALU.min)
            link(eng.tensor_tensor(T2[:, 128:192], lo[:, :, 0], lo[:, :, 1], ALU.max))
            link(eng.tensor_tensor(T2[:, 64:128], T2[:, 64:128], T2[:, 128:192], ALU.max))
            link(eng.tensor_tensor(GS[:, :, 0:4], tri(T2[:, 0:64], 4), tri(T2[:, 64:128], 4), ALU.add))
            link(top2(eng, link, GS, 4, 8))
            link(eng.tensor_tensor(T1[:, 0:64], A2[:, 0, 0:64], A2[:, 1, 0:64], ALU.add))
            kept = b3(T1[:, 0:64], 4, 2)
            eng.tensor_scalar(T1[:, 64:128], T1[:, 0:64], 1.0, -NEG, ALU.subtract, ALU.mult)
            link(eng.tensor_tensor(T2[:, 0:256].rearrange("p (g c) -> p g c", c=4),
                                   T0[:, 0:256].rearrange("p (g c) -> p g c", c=4), kept, ALU.mult))
            link(eng.tensor_tensor(T2[:, 0:256].rearrange("p (g c) -> p g c", c=4),
                                   T2[:, 0:256].rearrange("p (g c) -> p g c", c=4), b3(T1[:, 64:128], 4, 2), ALU.add))
            link(top2(eng, link, tri(T2[:, 0:256], 16), 16, 16))
            link(eng.tensor_tensor(T1[:, 0:256], A2[:, 0, 0:256], A2[:, 1, 0:256], ALU.add))
            eng.memset(comb[:, :, 16:18], 1.0)
            eng.tensor_tensor(comb[:, :, 0:16], lg[:, :, :], tri(T1[:, 0:256], 16), ALU.mult).then_inc(sem["c_ready"], 1)
            link.end()

        HS = carve(N0 + 4000, P)
        CSS, CTR = carve(N0 + 4128, 18), carve(N0 + 4146, P)
        SL, G_ = carve(N0 + 4280, 2, F), carve(N0 + 5304, 2, F)
        GTT = carve(N0 + 6328, 2, F)
        S3 = carve(N0 + 7352, 2, F)

        def ffn(st, units, width, w1, w3, w2, bias1, bias3, bias2, nc_, grp):
            nf = width // P

            def hid(ap, u, n=2):
                return ap[:, u % n, 0:width]

            def pe(eng, i):
                eng.wait_ge(sem["h_staged"], count(st, "h_staged", i, 1))
                eng.wait_ge(sem["x_ready"], count(st, "x_ready", i, 0))
                if bias2 is not None:
                    eng.wait_ge(sem["c_in"], count(st, "c_in", i, 1))
                    eng.transpose(ps[0:nc_, 7, 0:P], CSS[:, 0:nc_], ident).then_inc(sem["c_turned"], 1)

                def up(u):
                    b = 2 * (u % 2)
                    last = eng.matmul(ps[:, b, 0:width], HS, w1(u), start=True, stop=True)
                    if w3 is not None:
                        last = eng.matmul(ps[:, b + 1, 0:width], HS, w3(u), start=True, stop=True)
                    last.then_inc(sem["h_ps"], 1)

                up(0)
                for u in range(units):
                    if u + 1 < units:
                        up(u + 1)
                    if u == 0 and bias2 is not None:
                        eng.wait_ge(sem["cT_ready"], count(st, "cT_ready", i, 1))
                        eng.matmul(ps[:, 6, 0:D], CTR[0:nc_, :], bias2, start=True, stop=False)
                    eng.wait_ge(sem["mid_ready"], count(st, "mid_ready", i, u + 1))
                    for f in range(nf):
                        last = eng.transpose(ps[:, 4 + u % 2, f * P:(f + 1) * P], G_[:, u % 2, f * P:(f + 1) * P], ident)
                    last.then_inc(sem["mid_ps"], 1)
                    eng.wait_ge(sem["midT_ready"], count(st, "midT_ready", i, u + 1))
                    for f in range(nf):
                        last = eng.matmul(ps[:, 6, 0:D], GTT[:, u % 2, f * P:(f + 1) * P], w2(u, f),
                                          start=(u == 0 and f == 0 and bias2 is None),
                                          stop=(u == units - 1 and f == nf - 1))
                last.then_inc(sem["y_ps"], 1)

            def act(eng, i):
                if bias2 is not None:
                    eng.wait_ge(sem["c_turned"], count(st, "c_turned", i, 1))
                    eng.activation(CTR[0:nc_, :], ps[0:nc_, 7, 0:P], ACT.Copy).then_inc(sem["cT_ready"], 1)

                def silu(u):
                    if bias1 is None:
                        eng.wait_ge(sem["h_ps"], count(st, "h_ps", i, u + 1))
                        eng.activation(hid(SL, u), ps[:, 2 * (u % 2), 0:width], ACT.Silu)\
                           .then_inc(sem["act_ready"], 1)
                    else:
                        eng.wait_ge(sem["act_in"], count(st, "act_in", i, u + 1))
                        eng.activation(hid(SL, u), hid(SL, u), ACT.Silu).then_inc(sem["act_ready"], 1)

                silu(0)
                for u in range(units):
                    if u + 1 < units:
                        silu(u + 1)
                    eng.wait_ge(sem["mid_ps"], count(st, "mid_ps", i, u + 1))
                    eng.activation(hid(GTT, u), ps[:, 4 + u % 2, 0:width], ACT.Copy).then_inc(sem["midT_ready"], 1)

            def dve(eng, link, i):
                link.start(st, i)
                if bias2 is not None:
                    eng.wait_ge(sem["c_turned"], count(st, "c_turned", i, 0))
                    eng.tensor_scalar(CSS[:, 0:nc_], comb[:, bass.ds(i, 1), 0:nc_].rearrange("p a c -> p (a c)"), 1.0, None,
                                      ALU.mult)\
                       .then_inc(sem["c_in"], 1)

                def weight(u):
                    return comb[:, bass.ds(i, 1), u:u + 1].rearrange("p a c -> p (a c)")

                def add_bias(u):
                    eng.wait_ge(sem["h_ps"], count(st, "h_ps", i, u + 1))
                    eng.tensor_tensor(hid(SL, u), ps[:, 2 * (u % 2), 0:width], bias1(u), ALU.add)\
                       .then_inc(sem["act_in"], 1)
                    if w3 is not None:
                        link(eng.tensor_tensor(hid(S3, u), ps[:, 2 * (u % 2) + 1, 0:width], bias3(u), ALU.add))
                        c = comb[:, bass.ds(i, 1), grp * u:grp * u + grp].rearrange("p a c -> p (a c)")
                        s3 = hid(S3, u).rearrange("p (g c) -> p g c", g=grp)
                        link(eng.tensor_tensor(s3, s3, b3(c, width // grp, 2), ALU.mult))

                if bias1 is not None:
                    add_bias(0)
                for u in range(units):
                    if bias1 is not None and u + 1 < units:
                        add_bias(u + 1)
                    eng.wait_ge(sem["act_ready"], count(st, "act_ready", i, u + 1))
                    if bias1 is None:
                        eng.scalar_tensor_tensor(out=hid(G_, u), in0=hid(SL, u), scalar=weight(u),
                                                 in1=ps[:, 2 * (u % 2) + 1, 0:width], op0=ALU.mult, op1=ALU.mult)\
                           .then_inc(sem["mid_ready"], 1)
                    elif w3 is None:
                        eng.tensor_scalar(hid(G_, u), hid(SL, u), weight(u), None, ALU.mult)\
                           .then_inc(sem["mid_ready"], 1)
                    else:
                        eng.tensor_tensor(hid(G_, u), hid(SL, u), hid(S3, u), ALU.mult)\
                           .then_inc(sem["mid_ready"], 1)
                if st == "f2":
                    link(eng.engine_nop())
                eng.wait_ge(sem["y_ps"], count(st, "y_ps", i, 1))
                x = xs[:, bass.ds(i, 1), :].rearrange("p a d -> p (a d)")
                eng.tensor_tensor(x, x, ps[:, 6, 0:D], ALU.add).then_inc(sem["x_ready"], 1)
                link.end()

            def pool(eng, i):
                eng.wait_ge(sem["y_ps"], count(st, "y_ps", i, 0))
                bridge(eng)
                eng.tensor_copy(HS, cols(hT, i, P)).then_inc(sem["h_staged"], 1)

            return pe, act, dve, pool

        f0 = ffn("f0", E, F, lambda u: W1[:, u, :], lambda u: W3[:, u, :], lambda u, f: W2[:, u, f, :],
                 None, None, None, 0, 1)
        f1 = ffn("f1", E, F, lambda u: V1[:, u, :], None, lambda u, f: V2[:, u, f, :],
                 lambda u: VB1[:, u, :], None, b2f1, E, 1)
        f2 = ffn("f2", 3, 384, lambda u: U1[:, 384 * u:384 * u + 384], lambda u: U3[:, 384 * u:384 * u + 384],
                 lambda u, f: U2[:, 3 * u + f, :], lambda u: UB1[:, 384 * u:384 * u + 384],
                 lambda u: UB3[:, 384 * u:384 * u + 384], b2f2, 18, 6)
        f3 = ffn("f3", E, F, lambda u: V1[:, u, :], None, lambda u, f: V2[:, u, f, :],
                 lambda u: VB1[:, u, :], None, b2f3, E, 1)

        Y1, Y2 = carve(N0, GT, D), carve(N0 + 512, GT, D)
        YT = carve(N0 + 1024, GW)
        SC, PTT = carve(N0 + 1536, GT, P), carve(N0 + 2048, GW)
        R = carve(N0 + 2560, GT, D)
        HID = carve(N0 + 3072, FB, GW)
        MF, MA = carve(N0 + 5120, GT, P), carve(N0 + 5632, GT, P)

        def one_head_pe(eng, st, i, k, qT, keys, vals):
            for j in range(GT):
                last = eng.matmul(ps[:, 1, j * P:(j + 1) * P], qT[:, j * P:(j + 1) * P], keys(j), start=True, stop=True)
            last.then_inc(sem["sc_ps"], 1)
            eng.wait_ge(sem["ex_ready"], count(st, "ex_ready", i, k))
            for j in range(GT):
                last = eng.transpose(ps[:, 2, j * P:(j + 1) * P], SC[:, j, :], ident)
            last.then_inc(sem["pt_ps"], 1)
            eng.wait_ge(sem["pt_ready"], count(st, "pt_ready", i, k))
            for j in range(GT):
                last = eng.matmul(ps[:, 3, j * P:(j + 1) * P], PTT[:, j * P:(j + 1) * P], vals(j), start=True, stop=True)
            last.then_inc(sem["av_ps"], 1)

        def one_head_act(eng, st, i, k):
            eng.wait_ge(sem["sm_in"], count(st, "sm_in", i, k))
            eng.activation(SC, SC, ACT.Exp, scale=D ** -0.5).then_inc(sem["ex_ready"], 1)
            eng.wait_ge(sem["pt_ps"], count(st, "pt_ps", i, k))
            eng.activation(PTT, ps[:, 2, :], ACT.Copy).then_inc(sem["pt_ready"], 1)

        def quad(ap):
            return ap.rearrange("p (a b) -> p a b", a=GT)

        def one_head_dve(eng, link, st, i, k, bias):
            eng.wait_ge(sem["sc_ps"], count(st, "sc_ps", i, k))
            bias(link)
            link(eng.tensor_reduce(mx[:, 0:GT], SC, X_AX, ALU.max))
            eng.tensor_tensor(SC, SC, b3(mx[:, 0:GT], P, 2), ALU.subtract).then_inc(sem["sm_in"], 1)
            eng.wait_ge(sem["ex_ready"], count(st, "ex_ready", i, k))
            link(eng.reduce_sum(sm[:, 0:GT], SC, X_AX))
            link(eng.reciprocal(rs[:, 0:GT], sm[:, 0:GT]))
            eng.wait_ge(sem["av_ps"], count(st, "av_ps", i, k))

        def a1_pe(eng, i):
            st = "a1"
            turn_pe(eng, st, i, 1, XH)
            eng.wait_ge(sem["cols_ready"], count(st, "cols_ready", i, 1))
            one_head_pe(eng, st, i, 1, XT, lambda j: XT[:, j * P:(j + 1) * P], lambda j: XH[:, j, :])
            turn_pe(eng, st, i, 2, Y1)
            eng.wait_ge(sem["cols_ready"], count(st, "cols_ready", i, 2))
            one_head_pe(eng, st, i, 2, YT, lambda j: cT[:, bass.ds(i * GW + j * P, P)],
                        lambda j: cs[:, bass.ds(i * GT + j, 1), :])
            turn_pe(eng, st, i, 3, Y2)
            eng.wait_ge(sem["cols_ready"], count(st, "cols_ready", i, 3))
            for f in range(FB):
                last = eng.matmul(ps[:, 4 + f, :], w1a[:, f * P:(f + 1) * P], XT, start=True, stop=True)
            last.then_inc(sem["h_ps"], 1)
            eng.wait_ge(sem["mid_ready"], count(st, "mid_ready", i, 1))
            for j in range(GT):
                for f in range(FB):
                    last = eng.matmul(ps[:, 1, j * P:(j + 1) * P], HID[:, f, j * P:(j + 1) * P], w2a[:, f, :],
                                      start=(f == 0), stop=(f == FB - 1))
            last.then_inc(sem["y_ps"], 1)

        def a1_act(eng, i):
            st = "a1"
            turn_act(eng, st, i, 1, XT)
            one_head_act(eng, st, i, 1)
            turn_act(eng, st, i, 2, YT)
            one_head_act(eng, st, i, 2)
            turn_act(eng, st, i, 3, XT)

        def affine(eng, link, y, g, b, signal=None, final=None):
            link(eng.tensor_tensor(y, y, b3(g, GT, 1), ALU.mult))
            last = eng.tensor_tensor(y, y, b3(b, GT, 1), ALU.add)
            if signal:
                last.then_inc(sem[signal], 1)
            else:
                link(last)

        def weighted(eng, out_, add):
            for j in range(GT):
                if add is None:
                    last = eng.tensor_scalar(out_[:, j, :], ps[:, 3, j * P:(j + 1) * P], rs[:, j:j + 1], None, ALU.mult)
                else:
                    last = eng.scalar_tensor_tensor(out=out_[:, j, :], in0=ps[:, 3, j * P:(j + 1) * P],
                                                    scalar=rs[:, j:j + 1], in1=add[:, j, :], op0=ALU.mult, op1=ALU.add)
            return last

        def a1_dve(eng, link, i):
            st = "a1"
            link.start(st, i)
            norm_dve(eng, link, st, i, 1, group(xs, i), XH, "rows_ready")
            one_head_dve(eng, link, st, i, 1, lambda ln: ln(eng.tensor_tensor(
                SC, quad(ps[:, 1, :]), b3(const("causal2"), GT, 1), ALU.add)))
            link(weighted(eng, R, XH))
            norm_dve(eng, link, st, i, 2, R, Y1)
            affine(eng, link, Y1, ga[0], ba[0], "rows_ready")
            one_head_dve(eng, link, st, i, 2, lambda ln: ln(eng.tensor_tensor(
                SC, quad(ps[:, 1, :]), b3(const("same2"), GT, 1), ALU.add)))
            link(weighted(eng, R, Y1))
            norm_dve(eng, link, st, i, 3, R, Y2)
            affine(eng, link, Y2, ga[1], ba[1], "rows_ready")
            eng.wait_ge(sem["h_ps"], count(st, "h_ps", i, 1))
            for f in range(FB):
                last = eng.tensor_scalar(HID[:, f, :], ps[:, 4 + f, :], b1a[:, f:f + 1], 0.0, ALU.add, ALU.max)
            last.then_inc(sem["mid_ready"], 1)
            eng.wait_ge(sem["y_ps"], count(st, "y_ps", i, 1))
            link(eng.tensor_tensor(R, quad(ps[:, 1, :]), b3(b2a, GT, 1), ALU.add))
            link(eng.tensor_tensor(R, R, Y2, ALU.add))
            norm_dve(eng, link, st, i, 4, R, Y1)
            affine(eng, link, Y1, ga[2], ba[2])
            g = group(xs, i)
            eng.tensor_tensor(g, g, Y1, ALU.add).then_inc(sem["x_ready"], 1)
            link.end()

        def a2_pe(eng, i):
            st = "a2"
            turn_pe(eng, st, i, 1, XH)
            eng.wait_ge(sem["cols_ready"], count(st, "cols_ready", i, 1))
            one_head_pe(eng, st, i, 1, XT, lambda j: cT[:, bass.ds(i * GW + j * P, P)],
                        lambda j: cs[:, bass.ds(i * GT + j, 1), :])

        def a2_act(eng, i):
            turn_act(eng, "a2", i, 1, XT)
            one_head_act(eng, "a2", i, 1)

        def a2_dve(eng, link, i):
            st = "a2"
            link.start(st, i)
            norm_dve(eng, link, st, i, 1, group(xs, i), XH, "rows_ready")
            link(eng.memset(MF, 0.0))
            for b in range(2):
                r = slice(S * b, S * b + S)
                last = eng.tensor_scalar(MF[r, :, r], m2i[r, bass.ds(i * GT, GT), :], 0.0, None, ALU.not_equal)
            link(last)
            link(eng.tensor_scalar(MA, MF, 9.0e15, 9.0e15, ALU.mult, ALU.subtract))
            link(eng.tensor_tensor(MA, MA, b3(const("same2"), GT, 1), ALU.add))

            def masked(ln):
                ln(eng.tensor_tensor(SC, quad(ps[:, 1, :]), MF, ALU.mult))
                ln(eng.tensor_tensor(SC, SC, MA, ALU.add))

            one_head_dve(eng, link, st, i, 1, masked)
            link(weighted(eng, R, None))
            norm_dve(eng, link, st, i, 2, R, Y1)
            affine(eng, link, Y1, g2, be2)
            g = group(xs, i)
            eng.tensor_tensor(g, g, Y1, ALU.add).then_inc(sem["x_ready"], 1)
            link.end()

        QT3 = carve(N0, GW)
        QX = carve(N0 + 1536, 2, GW)
        IXT, LT1, LT2 = [work[0:H * NK, N0 + 2560 + 512 * n:N0 + 3072 + 512 * n] for n in range(3)]
        KV = carve(N0 + 4096, GB, 8, 32)
        OX = carve(N0 + 6144, 2, GW)
        PRD, TT, EX, WW = [carve(N0 + 7168 + 640 * n, 2, NK, S) for n in range(4)]
        SMQ, RQ, UQ, MQ = [carve(N0 + 9728 + 128 * n, 2, S) for n in range(4)]
        KVT = carve(N0 + 7168, GB, D)
        AH = wa[:, 0:10240].rearrange("p (r j k c) -> p r j k c", r=2, j=4, k=NK)
        AB = wa[:, 10240:11776].rearrange("p (r c) -> p r c", r=3)
        M3 = wa[0:H * NK, 8192:10240].bitcast(I32).rearrange("p (b s) -> p b s", b=B)
        LEN, SGN, INV = [wa[0:H * NK, 11776 + 32 * n:11808 + 32 * n] for n in range(3)]
        SG = GW // 2
        CHUNKS = [(j, ks) for j in range(4) for ks in ((0, 1), (2, 3), (4,))]
        NU3 = 16

        def unit(u):
            n, b = divmod(u, 4)
            return n, n // 2, n % 2, b

        def m3_dve(eng, link):
            link.start("m3", 0)
            link(eng.reduce_sum(LEN, M3, X_AX))
            link(eng.tensor_scalar(LEN, LEN, -1.0, float(S - 1), ALU.mult, ALU.add))
            link(eng.tensor_scalar(SGN, LEN, 0.0, None, ALU.is_ge))
            link(eng.tensor_scalar(SGN, SGN, 2.0, 1.0, ALU.mult, ALU.subtract))
            link(eng.tensor_tensor(LEN, LEN, SGN, ALU.mult))
            link(eng.reciprocal(INV, LEN))
            link.end()

        def a3_pe(eng, i):
            st = "a3"
            turn_pe(eng, st, i, 1, XH)
            eng.wait_ge(sem["cols_ready"], count(st, "cols_ready", i, 1))
            eng.wait_ge(sem["ct_staged"], count(st, "ct_staged", i, 1))
            eng.matmul(ps[:, 1, :], wq3, XT, start=True, stop=True)
            for h in range(2):
                last = eng.matmul(ps[:, 2 + h, :], wqx3[:, h, :], XT, start=True, stop=True)
            last.then_inc(sem["q_ps"], 1)

            def kv(w):
                for b in range(GB):
                    last = eng.matmul(ps[:, 5 + b // 4, (b % 4) * P:(b % 4 + 1) * P], dup(b), w, start=True, stop=True)
                return last

            kv(wk3).then_inc(sem["k_ps"], 1)
            eng.wait_ge(sem["q_ready"], count(st, "q_ready", i, 1))
            eng.matmul(ps[0:H * NK, 4, :], woff3, QT3, start=True, stop=True).then_inc(sem["off_ps"], 1)
            eng.wait_ge(sem["k_read"], count(st, "k_read", i, 1))
            kv(wv3).then_inc(sem["v_ps"], 1)
            eng.wait_ge(sem["ix_ready"], count(st, "ix_ready", i, 1))
            eng.wait_ge(sem["kv_ready"], count(st, "kv_ready", i, 1))

            def gaps(n, c):
                j, ks = CHUNKS[c]
                hp = 4 * (n % 2) + j
                c += 12 * n
                if c >= 3:
                    eng.wait_ge(sem["gap_ready"], count(st, "gap_ready", i, c - 2))
                for m, k in enumerate(ks):
                    r = 2 * NK * hp + k
                    for h in range(2):
                        sel = ident[0:H * NK, r + NK * h:r + NK * h + 1].to_broadcast([H * NK, S])
                        last = eng.matmul(ps[S * h:S * h + S, c % 3, m * SG:(m + 1) * SG], sel,
                                          IXT[:, (n // 2) * SG:(n // 2 + 1) * SG], start=True, stop=True,
                                          tile_position=(0, S * h))
                last.then_inc(sem["gap_ps"], 1)

            for c in range(12):
                gaps(0, c)
            for u in range(NU3):
                n, sg, half, b = unit(u)
                if b == 0:
                    eng.wait_ge(sem["hat_ready"], count(st, "hat_ready", i, 12 * (n + 1)))
                if u >= 2:
                    eng.wait_ge(sem["o_ready"], count(st, "o_ready", i, u - 1))
                for j in range(4):
                    last = eng.matmul(ps[32 * j:32 * j + 32, 3 + u % 2, 0:NK * S], KV[:, 4 * sg + b, 4 * half + j, :],
                                      AH[:, n % 2, j, :, b * S:(b + 1) * S], start=True, stop=True,
                                      tile_position=(0, 32 * j))
                last.then_inc(sem["skv_ps"], 1)
                if n < 3:
                    for c in range(3 * b, 3 * b + 3):
                        gaps(n + 1, c)
                eng.wait_ge(sem["prod_ready"], count(st, "prod_ready", i, u + 1))
                if u >= 2:
                    eng.wait_ge(sem["sm_in"], count(st, "sm_in", i, u - 1))
                eng.matmul(ps[:, 5 + u % 2, 0:NK * S], const("spread"), PRD[:, u % 2, :, :].rearrange("p k q -> p (k q)"),
                           start=True, stop=True).then_inc(sem["score_ps"], 1)
            eng.wait_ge(sem["o_ready"], count(st, "o_ready", i, NU3))
            for j in range(GT):
                for h in range(2):
                    last = eng.matmul(ps[:, 7, j * P:(j + 1) * P], OX[:, h, j * P:(j + 1) * P], wox3[:, h, :],
                                      start=(h == 0), stop=(h == 1))
            last.then_inc(sem["out_ps"], 1)

        def chunk_width(c):
            return SG * len(CHUNKS[c % 12][1])

        def a3_act(eng, i):
            st = "a3"
            turn_act(eng, st, i, 1, XT)
            eng.wait_ge(sem["q_ps"], count(st, "q_ps", i, 1))
            eng.activation(QT3, ps[:, 1, :], ACT.Identity, bias=bq3).then_inc(sem["q_ready"], 1)

            def gap(c):
                eng.wait_ge(sem["gap_ps"], count(st, "gap_ps", i, c + 1))
                if c >= 3:
                    eng.wait_ge(sem["hat_ready"], count(st, "hat_ready", i, c - 2))
                w = chunk_width(c)
                eng.activation(AB[:, c % 3, 0:w], ps[:, c % 3, 0:w], ACT.Abs, bias=const("negm"))\
                   .then_inc(sem["gap_ready"], 1)

            for c in range(12):
                gap(c)
            for u in range(NU3):
                n, _, _, b = unit(u)
                if n < 3:
                    for c in range(3 * b, 3 * b + 3):
                        gap(12 * (n + 1) + c)
                eng.wait_ge(sem["sm_in"], count(st, "sm_in", i, u + 1))
                eng.activation(EX[:, u % 2, :, :].rearrange("p k q -> p (k q)"), TT[:, u % 2, :, :].rearrange("p k q -> p (k q)"),
                               ACT.Exp).then_inc(sem["ex_ready"], 1)

        def a3_dve(eng, link, i):
            st = "a3"
            link.start(st, i)
            norm_dve(eng, link, st, i, 1, group(xs, i), XH, "rows_ready")
            eng.wait_ge(sem["q_ps"], count(st, "q_ps", i, 1))
            for h in range(2):
                eng.tensor_scalar(QX[:, h, :], ps[:, 2 + h, :], bqx3[:, h:h + 1], HD ** -0.5, ALU.add, ALU.mult)
            eng.wait_ge(sem["k_ps"], count(st, "k_ps", i, 1))
            for n, bias in ((0, bk3), (1, bv3)):
                if n == 1:
                    eng.wait_ge(sem["v_ps"], count(st, "v_ps", i, 1))
                last = eng.tensor_tensor(KVT, ps[:, 5:7, :].rearrange("p a (b c) -> p (a b) c", b=4),
                                         b3(bias, GB, 1), ALU.add)
                if n == 0:
                    last.then_inc(sem["k_read"], 1)
                    eng.wait_ge(sem["k_read"], count(st, "k_read", i, 1))
                else:
                    link(last)
                for b in range(GB):
                    last = eng.tensor_tensor(KV[:, b, :, 16 * n:16 * n + 16],
                                             KVT[:, b, :].rearrange("p (h c) -> p h c", h=8),
                                             const("headhalf").rearrange("p (h c) -> p h c", h=8), ALU.mult)
                if n == 0:
                    link(last)
            last.then_inc(sem["kv_ready"], 1)
            eng.wait_ge(sem["off_ps"], count(st, "off_ps", i, 1))

            def by_batch(ap):
                return ap.rearrange("p (b s) -> p b s", b=GB)

            def of_batch(ap):
                return b3(ap[:, bass.ds(i * GB, GB)], S, 2)

            v, q = by_batch(LT1), by_batch(LT2)
            link(eng.tensor_scalar(LT1, ps[0:H * NK, 4, :], boff3[0:H * NK, :], const("ref", H * NK), ALU.add, ALU.add))
            link(eng.tensor_tensor(LT1, LT1, const("loc", H * NK), ALU.add))
            link(eng.tensor_tensor(v, v, of_batch(SGN), ALU.mult))
            link(eng.tensor_tensor(q, v, of_batch(INV), ALU.mult))
            link(eng.tensor_scalar(LT2, LT2, 12582912.0, None, ALU.add))
            link(eng.tensor_scalar(LT2, LT2, 12582912.0, None, ALU.subtract))
            link(eng.tensor_tensor(q, q, of_batch(LEN), ALU.mult))
            link(eng.tensor_tensor(LT1, LT1, LT2, ALU.subtract))
            link(eng.tensor_scalar(LT2, LT1, 0.0, None, ALU.is_lt))
            link(eng.tensor_tensor(q, q, of_batch(LEN), ALU.mult))
            link(eng.tensor_tensor(LT1, LT1, LT2, ALU.add))
            link(eng.tensor_tensor(v, v, of_batch(SGN), ALU.mult))
            link(eng.tensor_scalar(LT1, LT1, 2.0 / (S - 1), 1.0, ALU.mult, ALU.subtract))
            link(eng.tensor_scalar(LT1, LT1, 1.0, float(S // 2), ALU.add, ALU.mult))
            eng.tensor_scalar(IXT, LT1, 0.5, None, ALU.subtract).then_inc(sem["ix_ready"], 1)

            def hat(c):
                n, (j, ks) = c // 12, CHUNKS[c % 12]
                eng.wait_ge(sem["gap_ready"], count(st, "gap_ready", i, c + 1))
                w = chunk_width(c)
                eng.tensor_scalar(AH[:, n % 2, j, ks[0]:ks[-1] + 1, :],
                                  AB[:, c % 3, 0:w].rearrange("p (k c) -> p k c", k=len(ks)), 1.0, 0.0,
                                  ALU.subtract, ALU.min).then_inc(sem["hat_ready"], 1)

            def by_place(ap):
                return ap.rearrange("p k q -> p q k")

            def skv(u):
                return ps[:, 3 + u % 2, 0:NK * S].rearrange("p (k q) -> p k q", k=NK)

            def finish(u):
                _, sg, half, b = unit(u)
                r = u % 2
                eng.wait_ge(sem["ex_ready"], count(st, "ex_ready", i, u + 1))
                eng.reduce_sum(SMQ[:, r, :], by_place(EX[:, r, :, :]), X_AX)
                link(eng.tensor_tensor(WW[:, r, :, :], EX[:, r, :, :], skv(u), ALU.mult))
                eng.reciprocal(RQ[:, r, :], SMQ[:, r, :])
                link(eng.reduce_sum(UQ[:, r, :], by_place(WW[:, r, :, :]), X_AX))
                at = sg * SG + b * S
                eng.tensor_tensor(OX[:, half, at:at + S], UQ[:, r, :], RQ[:, r, :], ALU.mult).then_inc(sem["o_ready"], 1)

            for c in range(12):
                hat(c)
            for u in range(NU3):
                n, sg, half, b = unit(u)
                r = u % 2
                eng.wait_ge(sem["skv_ps"], count(st, "skv_ps", i, u + 1))
                at = sg * SG + b * S
                eng.tensor_tensor(PRD[:, r, :, :], skv(u), b3(QX[:, half, at:at + S], NK, 1), ALU.mult)\
                   .then_inc(sem["prod_ready"], 1)
                if n < 3:
                    for c in range(3 * b, 3 * b + 3):
                        hat(12 * (n + 1) + c)
                if u >= 1:
                    finish(u - 1)
                eng.wait_ge(sem["score_ps"], count(st, "score_ps", i, u + 1))
                score = ps[:, 5 + r, 0:NK * S].rearrange("p (k q) -> p k q", k=NK)
                link(eng.tensor_reduce(MQ[:, r, :], by_place(score), X_AX, ALU.max))
                eng.tensor_tensor(TT[:, r, :, :], score, b3(MQ[:, r, :], NK, 1), ALU.subtract).then_inc(sem["sm_in"], 1)
            finish(NU3 - 1)
            eng.wait_ge(sem["out_ps"], count(st, "out_ps", i, 1))
            link(eng.tensor_tensor(XH, quad(ps[:, 7, :]), b3(bo3, GT, 1), ALU.add))
            g = group(xs, i)
            eng.tensor_tensor(g, g, XH, ALU.add).then_inc(sem["x_ready"], 1)
            link.end()

        def row(a, n=P):
            return a.rearrange("(o n) -> o n", o=1).to_broadcast([n, a.shape[0]])

        def column(a):
            return a.rearrange("(p o) -> p o", o=1)

        def tok(a):
            return a.rearrange("b s d -> (b s) d").rearrange("(t p) d -> p t d", p=P)

        def hidden(a):
            return a.rearrange("(f p) d -> p f d", p=P)

        load_list = {
            "pre": [(con[:, :], t["constants"]), (xs[:, :, :], tok(t["x"])), (cs[:, :, :], tok(t["ctx_1024"])),
                    (m0i[:, :], t["mask_BxS2_ik0"]),
                    (m2i[:, :, :], tok(t["mask_BxSxS2_ik1"]))],
            "a0": [(wq0, t["L0_xattn_WQ"]), (wk0, t["L0_xattn_WK"]), (wv0, t["L0_xattn_WV"]), (wo0, t["L0_xattn_WO"]),
                   (g_ln, row(t["L0_ffn_ln_g"])), (b_ln, row(t["L0_ffn_ln_b"])), (wr0[:, 0:7], t["L0_ffn_Wr"])],
            "f0": [(W1[:, 0:7, :], t["L0_ffn_W1"].rearrange("e p f -> p e f")), (W1[:, 7, :], t["L0_ffn_W1s"]),
                   (W3[:, 0:7, :], t["L0_ffn_W3"].rearrange("e p f -> p e f")), (W3[:, 7, :], t["L0_ffn_W3s"])]
            + [(W2[:, e, :, :], hidden(t["L0_ffn_W2"][e, :, :])) for e in range(7)]
            + [(W2[:, 7, :, :], hidden(t["L0_ffn_W2s"]))],
            "a1": [(w1a, t["L1_xattn_w1"]), (w2a, hidden(t["L1_xattn_w2"])),
                   (b1a, t["L1_xattn_b1"]), (b2a, row(t["L1_xattn_b2"]))]
            + [(ga[n], row(t[f"L1_xattn_g{n + 1}"])) for n in range(3)]
            + [(ba[n], row(t[f"L1_xattn_beta{n + 1}"])) for n in range(3)]
            + [(wr1, t["L1_ffn_Wr"]), (br1, row(t["L1_ffn_br"])), (b2f1, t["L1_ffn_b2"])],
            "a2": [(g2, row(t["L2_xattn_gamma"])), (be2, row(t["L2_xattn_beta"])), (wg2, t["L2_ffn_gate_wT"]),
                   (gb2, row(t["L2_ffn_gate_b"])), (b2f2[0:16, :], t["L2_ffn_be2"]),
                   (b2f2[16:17, :], row(t["L2_ffn_bs2"], 1))],
            "a3": [(wq3, t["L3_xattn_WqT"]), (wk3, t["L3_xattn_WkT"]), (wv3, t["L3_xattn_WvT"]),
                   (bk3, row(t["L3_xattn_bk"])), (bv3, row(t["L3_xattn_bv"])), (bo3, row(t["L3_xattn_bo"])),
                   (woff3, t["L3_xattn_WoffT"]), (boff3[0:H * NK, :], column(t["L3_xattn_boff"])),
                   (bq3, column(t["L3_xattn_bq"])), (wg3, t["L3_ffn_Wg"]), (bg3, row(t["L3_ffn_bg"])),
                   (b2f3, t["L3_ffn_b2"])]
            + [(wqx3[:, h, 32 * j:32 * j + 16], t["L3_xattn_WqT"][:, 16 * (4 * h + j):16 * (4 * h + j) + 16])
               for h in range(2) for j in range(4)]
            + [(bqx3[32 * j:32 * j + 16, h:h + 1], column(t["L3_xattn_bq"][16 * (4 * h + j):16 * (4 * h + j) + 16]))
               for h in range(2) for j in range(4)]
            + [(wox3[32 * j + 16:32 * j + 32, h, :], t["L3_xattn_WoT"][16 * (4 * h + j):16 * (4 * h + j) + 16, :])
               for h in range(2) for j in range(4)],
            "f2": [(U1[:, 0:1024].rearrange("p (e f) -> p e f", e=EG), t["L2_ffn_We1"].rearrange("e p f -> p e f")),
                   (U1[:, 1024:NU], t["L2_ffn_ws1"]),
                   (U3[:, 0:1024].rearrange("p (e f) -> p e f", e=EG), t["L2_ffn_We3"].rearrange("e p f -> p e f")),
                   (U3[:, 1024:NU], t["L2_ffn_ws3"]),
                   (U2[:, 0:8, :], hidden(t["L2_ffn_We2"].rearrange("e f d -> (e f) d"))),
                   (U2[:, 8, :], t["L2_ffn_ws2"]),
                   (UB1[:, 0:1024], row(t["L2_ffn_be1"].rearrange("e f -> (e f)"))), (UB1[:, 1024:NU], row(t["L2_ffn_bs1"])),
                   (UB3[:, 0:1024], row(t["L2_ffn_be3"].rearrange("e f -> (e f)"))), (UB3[:, 1024:NU], row(t["L2_ffn_bs3"])),
                   (M3, t["mask_BxS2_if0"].rearrange("(o b) s -> o b s", o=1).to_broadcast([H * NK, B, S]))],
        }
        for n, layer in (("f1", "L1"), ("f3", "L3")):
            load_list[n] = [(V1, t[layer + "_ffn_W1"].rearrange("e p f -> p e f"))]\
                + [(V2[:, e, :, :], hidden(t[layer + "_ffn_W2"][e, :, :])) for e in range(E)]\
                + [(VB1[:, e, :], row(t[layer + "_ffn_b1"][e, :])) for e in range(E)]

        block = ctx.enter_context(nc.Block())

        @block.sync
        def _(eng):
            def load(name):
                for dst, src in load_list[name]:
                    eng.dma_start(dst, src).then_inc(loads[name], 16)

            for name in ("pre", "a0", "f0", "a1", "f1"):
                load(name)
            if "f2" in ORDER:
                eng.wait_ge(sem["x_ready"], total("f0", "x_ready"))
                load("f2")
            if "a2" in ORDER:
                eng.wait_ge(s_init, 1)
                load("a2")
                load("a3")
                load("f3")
            eng.wait_ge(sem["x_ready"], total(LAST, "x_ready"))
            eng.dma_start(tok(out), xs[:, :, :]).then_inc(s_out, 16)
            for name in loads:
                if name in ("pre", "a0", "f0", "a1", "f1") or "f2" in ORDER or ("a2" in ORDER and name in ("a2", "a3", "f3")):
                    eng.wait_ge(loads[name], 16 * len(load_list[name]))
            eng.wait_ge(s_out, 16)

        needs = {"pre": ["pre"], "a0": ["a0"], "f0": ["f0"], "a1": ["a1"], "f1": ["f1"], "a2": ["a2"], "f2": ["f2"],
                 "a3": ["a3"], "f3": ["f3"], "m3": ["f2"]}

        @block.tensor
        def _(eng):
            for n in EARLY:
                eng.sem_inc(sem[n], 1)
            turns = {"a0": a0_pe, "a1": a1_pe, "a2": a2_pe, "a3": a3_pe, "f0": f0[0], "f1": f1[0], "f2": f2[0],
                     "f3": f3[0], "r0": lambda eng, i: logits_pe(eng, "r0", i, wr0[:, 0:7], 7),
                     "r1": lambda eng, i: logits_pe(eng, "r1", i, wr1, 8),
                     "r2": lambda eng, i: logits_pe(eng, "r2", i, wg2, EG),
                     "r3": lambda eng, i: logits_pe(eng, "r3", i, wg3, E), "b1": b1_pe}
            for st in ORDER:
                wait_loads(eng, *needs.get(st, []))
                if st == "pre":
                    for g in range(NG):
                        if g >= 1:
                            eng.wait_ge(sem["cols_ready"], count(st, "cols_ready", g, 0))
                        for j in range(GT):
                            last = eng.transpose(ps[:, 0, j * P:(j + 1) * P], cs[:, g * GT + j, :], ident)
                        last.then_inc(sem["turned"], 1)
                elif st in turns:
                    with eng.Fori(0, LOOPS[st]) as i:
                        turns[st](eng, i)
                elif st == "g0":
                    g0_pe(eng)
                elif st == "g1":
                    g1_pe(eng)

        @block.scalar
        def _(eng):
            turns = {"a0": a0_act, "a1": a1_act, "a2": a2_act, "a3": a3_act, "f0": f0[1], "f1": f1[1], "f2": f2[1],
                     "f3": f3[1], "r0": lambda eng, i: logits_act(eng, "r0", i, False, 7),
                     "r1": lambda eng, i: logits_act(eng, "r1", i, True, 8),
                     "r2": lambda eng, i: logits_act(eng, "r2", i, True, EG),
                     "r3": lambda eng, i: logits_act(eng, "r3", i, False, E)}
            for st in ORDER:
                wait_loads(eng, *needs.get(st, []))
                if st == "pre":
                    for g in range(NG):
                        turn_act(eng, st, g, 1, cT[:, g * GW:(g + 1) * GW])
                elif st in turns:
                    with eng.Fori(0, LOOPS[st]) as i:
                        turns[st](eng, i)
                elif st in ("g0", "g3"):
                    exp_gate(eng, st)

        @block.gpsimd
        def _(eng):
            def a(st, norms, ct=False):
                def f(eng, i):
                    if ct:
                        stage_ct(eng, st, i)
                    for k in range(norms):
                        norm_pool(eng, st, i, k + 1)
                return f

            def r(st, norms):
                def f(eng, i):
                    for k in range(norms):
                        norm_pool(eng, st, i, k + 1)
                    logits_pool(eng, st, i)
                return f

            turns = {"a0": a("a0", 1, True), "a1": a("a1", 4), "a2": a("a2", 2), "a3": a("a3", 1, True),
                     "f0": f0[3], "f1": f1[3], "f2": f2[3], "f3": f3[3],
                     "r0": r("r0", 2), "r1": r("r1", 1), "r2": r("r2", 1), "r3": r("r3", 1)}
            for st in ORDER:
                wait_loads(eng, *needs.get(st, []))
                if st == "a0":
                    eng.wait_ge(sem["cols_ready"], total("pre", "cols_ready"))
                if st == "a3":
                    eng.wait_ge(sem["x_ready"], count("a3", "x_ready"))
                if st[0] == "f":
                    eng.wait_ge(sem["ht_ready"], total("r" + st[1], "ht_ready"))
                    eng.wait_ge(sem["c_ready"], total("g" + st[1], "c_ready"))
                if st in turns:
                    with eng.Fori(0, LOOPS[st]) as i:
                        turns[st](eng, i)

        @block.vector
        def _(eng):
            link = Chain(eng)

            def router(st, norms, n, **kw):
                def f(eng, link, i):
                    link.start(st, i)
                    if norms == 2:
                        norm_dve(eng, link, st, i, 1, group(xs, i), XH)
                        norm_dve(eng, link, st, i, 2, XH, XH)
                        link(eng.tensor_tensor(XH, XH, b3(g_ln, GT, 1), ALU.mult))
                        eng.tensor_tensor(XH, XH, b3(b_ln, GT, 1), ALU.add).then_inc(sem["rows_ready"], 1)
                    else:
                        norm_dve(eng, link, st, i, 1, group(xs, i), XH, "rows_ready")
                    logits_dve(eng, link, st, i, n, **kw)
                    link.end()
                return f

            turns = {"a0": a0_dve, "a1": a1_dve, "a2": a2_dve, "a3": a3_dve, "f0": f0[2], "f1": f1[2], "f2": f2[2],
                     "f3": f3[2], "b1": b1_dve, "r0": router("r0", 2, 7), "r1": router("r1", 1, E, bias=br1, softmax=True),
                     "r2": router("r2", 1, EG, softmax=True),
                     "r3": router("r3", 1, E, bias=bg3, scale=1.0 / (1.0 + 1e-6))}
            once = {"g0": g0_dve, "t1": t1_dve, "g1": g1_dve, "g2": g2_dve, "g3": g3_dve, "m3": m3_dve}
            for st in ORDER:
                if st == "a2":
                    eng.wait_ge(sem["x_ready"], count(st, "x_ready"))
                    eng.memset(wsm[:, :], 0.0).then_inc(s_init, 1)
                wait_loads(eng, *needs.get(st, []))
                if st[0] in "ar" and st != "a0":
                    eng.wait_ge(sem["x_ready"], count(st, "x_ready"))
                if st == "a0":
                    link.start("a0", 0)
                    eng.tensor_scalar(qkeep[:, :], m0i[:, :], 0.0, None, ALU.is_equal).then_inc(s_keep, 1)
                    eng.wait_ge(s_keep, 1)
                if st == "r0":
                    eng.memset(lg[:, :, 7:8], NEG)
                if st[0] == "f":
                    eng.wait_ge(sem["c_ready"], total("g" + st[1], "c_ready"))
                if st in turns:
                    with eng.Fori(0, LOOPS[st]) as i:
                        turns[st](eng, link, i)
                elif st in once:
                    once[st](eng, link)


TURNED = {"L2_ffn_gate_w": "L2_ffn_gate_wT", "L3_xattn_Wq": "L3_xattn_WqT", "L3_xattn_Wk": "L3_xattn_WkT",
          "L3_xattn_Wv": "L3_xattn_WvT", "L3_xattn_Wo": "L3_xattn_WoT", "L3_xattn_Woff": "L3_xattn_WoffT"}


def kernel(**inputs):
    import concourse.bacc as bacc
    from concourse.bass_utils import run_bass_kernel_spmd

    nc = bacc.Bacc("TRN2", target_bir_lowering=False, num_devices=1)
    laid = {}
    for name, a in inputs.items():
        a = np.asarray(a)
        if name in ("mask_BxS2_ik0", "L1_xattn_b1"):
            a = a.reshape(-1, P).T
        laid[TURNED.get(name, name)] = np.ascontiguousarray(a.T if name in TURNED else a)
    laid["constants"] = constants()
    arrays, t = {}, {}
    for name, a in laid.items():
        arrays[f"in_{name}"] = a
        t[name] = nc.dram_tensor(f"in_{name}", a.shape, mybir.dt.from_np(a.dtype), kind="ExternalInput").ap()
    out = nc.dram_tensor("out_x", (B, S, D), F32, kind="ExternalOutput").ap()
    build(nc, t, out)
    r = run_bass_kernel_spmd(nc, [arrays], core_ids=[0])
    return r.results[0]["out_x"]
```

```python
from contextlib import ExitStack

import concourse.bass as bass
from concourse import mybir
import numpy as np

F32 = mybir.dt.float32
I32 = mybir.dt.int32
BF16 = mybir.dt.bfloat16
U32 = mybir.dt.uint32
ALU = mybir.AluOpType
ACT = mybir.ActivationFunctionType
X_AX = mybir.AxisListType.X

P = 128
B, S, D = 32, 64, 128
NT = B * S // P
GT = 4
NG = NT // GT
GW = GT * P
GB = GW // S
H = 16
HD = D // H
NK = 5
F = 512
FB = F // P
E = 8
EG, EI = 16, 64
CAP0 = -(-125 * 2 * 1024 // (100 * 7))
CAP1 = -(-12 * B * S // (10 * 8))
NEG = -1.0e30
SLOTS = 384
KB_ = 8
PLACES = {"s0": (8, 2), "f0": (7, 3), "f1": (8, 3), "f3": (8, 5)}
ROWS = 40 * 128

CONST = {}
_at = 0
for _name, _w in (("ident", P), ("ones", P), ("upto", P), ("causal2", P), ("same2", P), ("offdiag", P),
                  ("causal", S), ("headpair", P), ("headhalf", P), ("headquad", 4), ("spread", P), ("negm", 1), ("iota", 16),
                  ("neghalf", 1), ("ref", 1), ("loc", GW), ("bits", 45),
                  ("place", 8), ("blocks", 40), ("experts", 24)):
    CONST[_name] = (_at, _w)
    _at += _w
NCONST = _at


def constants():
    t = np.zeros((P, NCONST), np.float32)

    def put(name, a):
        t[:, CONST[name][0]:CONST[name][0] + CONST[name][1]] = a

    p, c = np.arange(P)[:, None], np.arange(P)[None, :]
    same = p // S == c // S
    put("ident", p == c)
    put("ones", np.ones((P, P)))
    put("upto", p <= c)
    put("causal2", np.where(same & (c <= p), 0.0, NEG))
    put("same2", np.where(same, 0.0, NEG))
    put("offdiag", same)
    put("causal", np.where(np.arange(S)[None, :] > p % S, -1.0e9, 0.0))
    put("headpair", (c // HD) % 2 == p // S)
    put("headhalf", ((c // HD) % 2 == p // S) * np.where((c // HD) % 8 >= 4, -0.5, 0.5))
    put("headquad", (p // HD) % 4 == np.arange(4)[None, :])
    put("spread", (c // HD == p // HD + 2) & ((c // HD) % 4 >= 2))
    put("negm", -(p % S))
    put("iota", np.arange(16)[None, :])
    put("neghalf", np.full((P, 1), -0.5))
    put("ref", p // H - 3.0)
    put("loc", np.arange(GW)[None, :] % S)
    put("place", np.arange(8)[None, :] * SLOTS - 1.0)
    put("blocks", np.arange(40)[None, :])
    put("experts", np.arange(24)[None, :] // (SLOTS // P))
    bits = 4 ** np.arange(14, -1, -1, dtype=np.int32)[:, None] * np.arange(1, 4, dtype=np.int32)[None, :]
    put("bits", bits.reshape(1, 45).view(np.float32))
    return t


_NORM = dict(var_ready=1, rstd_ready=1)
_TURN = dict(rows_ready=1, turned=1, cols_ready=1)
_SOFT = dict(sc_ps=1, sm_in=1, ex_ready=1, pt_ps=1, pt_ready=1, av_ps=1)


def _times(n, d):
    return {k: v * n for k, v in d.items()}


def _blocks(st, deep):
    n = PLACES[st][0]
    names = ["xt_ps", "xt_ready", "h_ps", "act_in" if deep else "act_ready", "mid_ready", "mid_ps", "midT_ready", "y_ps",
             "y_read"] + (["ys_free"] if st != "s0" else [])
    rises = {name: n for name in names}
    for k in range(n):
        rises[f"xe{k}"] = 16
        if st != "s0":
            rises[f"ys{k}"] = 16
    return rises


PLAN = [
    ("pre", NG, dict(turned=1, cols_ready=1)),
    ("a0", NG, dict(**_NORM, **_times(2, _TURN), ct_staged=1, k_ps=1, q_ps=1, q_ready=1, kb_ready=1, v_ps=1, vb_ready=1,
                    **_times(GT, _SOFT), sc_read=GT, out_ps=1, x_ready=1, dve=18)),
    ("r0", NG // 2, dict(**_times(2, dict(**_times(2, _NORM), **_TURN, ht_ready=1, lg_ps=1, lg_ready=1)), dve=14)),
    ("g0", 1, dict(exp_in=1, exp_ready=1, cum_in=1, cum_ps=1, slot_ready=1, dve=25)),
    ("s0", PLACES["s0"][1], dict(**_blocks("s0", False), dve=0)),
    ("f0", PLACES["f0"][1], dict(**_blocks("f0", False), dve=0)),
    ("a1", NG // 2, dict(**_times(2, dict(gathered=1, combined=1, **_times(4, _NORM), **_times(3, _TURN), **_times(2, _SOFT), h_ps=1, mid_ready=1, y_ps=1,
                    x_ready=1)), dve=56)),
    ("r1", NG // 2, dict(**_times(2, dict(**_NORM, **_TURN, ht_ready=1, lg_ps=1, exp_in=1, exp_ready=1, lg_ready=1)), dve=12)),
    ("t1", 1, dict(dve=7)),
    ("b1", 15, dict(cum_in=1, cum_ps=1, dve=6)),
    ("g1", 1, dict(cum_in=2, cum_ps=2, slot_ready=1, dve=29)),
    ("f1", PLACES["f1"][1], dict(**_blocks("f1", True), dve=0)),
    ("a2", NG // 2, dict(**_times(2, dict(gathered=1, combined=1, **_times(2, _NORM), **_TURN, **_SOFT, x_ready=1)), dve=36)),
    ("r2", NG // 2, dict(**_times(2, dict(**_NORM, **_TURN, ht_ready=1, lg_ps=1, exp_in=1, exp_ready=1, lg_ready=1)), dve=10)),
    ("g2", 1, dict(c_ready=1, dve=17)),
    ("f2", NG, dict(h_staged=1, c_in=1, c_turned=1, cT_ready=1, h_ps=12, act_in=12, act_ready=12, mid_ready=12,
                    mid_ps=12, midT_ready=12, y_ps=GT, x_ready=GT, dve=24)),
    ("m3", 1, dict(dve=7)),
    ("a3", NG, dict(**_NORM, **_TURN, ct_staged=1, q_ps=1, q_ready=1, off_ps=1, ix_ready=1, k_ps=1, k_read=1, v_ps=1,
                    kv_ready=1, gap_ps=48, gap_ready=48, hat_ready=24, odd_hat_ready=24, skv_ps=16, prod_ready=16, score_ps=16,
                    sm_in=16, ex_ready=16, skv_read=16, sum_step=64, sum_ready=16, values_ready=16, o_ready=16, out_ps=1, x_ready=1, dve=56)),
    ("r3", NG // 2, dict(**_times(2, dict(**_NORM, **_TURN, ht_ready=1, lg_ps=1, lg_ready=1)), dve=6)),
    ("g3", 1, dict(exp_in=1, exp_ready=1, cum_in=1, cum_ps=1, slot_ready=1, dve=31)),
    ("f3", PLACES["f3"][1], dict(**_blocks("f3", True), dve=0)),
    ("c3", 1, dict(x_ready=NG, dve=4)),
]
EARLY = {"ht_ready": 1, "v_ps": 1, "y_ps": 1, "c_turned": 1, "y_read": 1, "xt_ps": KB_, "ys_free": KB_}
SIGNALS = sorted({name for _, _, rises in PLAN for name in rises})
ORDER = [stage for stage, _, _ in PLAN]
LOOPS = {stage: turns for stage, turns, _ in PLAN}


def count(stage, name, turn=0, k=0):
    base = EARLY.get(name, 0)
    for s, turns, rises in PLAN:
        if s == stage:
            return turn * rises.get(name, 0) + (base + k)
        base += turns * rises.get(name, 0)


def total(stage, name):
    turns, rises = {s: (t, r) for s, t, r in PLAN}[stage]
    return count(stage, name, turns)


def build(nc, t, out):
    with ExitStack() as ctx:
        def sb(name, shape, dt=F32):
            return ctx.enter_context(nc.sbuf_tensor(name, shape, dt))

        ps = ctx.enter_context(nc.psum_tensor("ps", [P, 8, 512], F32))
        sem = {n: ctx.enter_context(nc.semaphore(n)) for n in SIGNALS}
        loads = {n: ctx.enter_context(nc.semaphore("load_" + n)) for n in
                 ("pre", "a0", "f0", "a1", "f1", "a2", "f2", "a3", "f3")}
        s_zero, s_sent = [ctx.enter_context(nc.semaphore(n)) for n in ("s_zero", "s_sent")]
        s_back = [ctx.enter_context(nc.semaphore(f"s_back{g}")) for g in range(NG)]
        s_zeros = ctx.enter_context(nc.semaphore("s_zeros"))
        s_out = ctx.enter_context(nc.semaphore("s_out"))
        s_keep = ctx.enter_context(nc.semaphore("s_keep"))
        s_init = ctx.enter_context(nc.semaphore("s_init"))

        xs = sb("xs", [P, NT, D])
        cs = sb("cs", [P, NT, D])
        cT = sb("cT", [P, B * S])
        hT = sb("hT", [P, B * S])
        hr = hT[:, :].rearrange("p (t d) -> p t d", t=NT)
        con = sb("con", [P, NCONST])
        wa = sb("wa", [P, 8 * 1536])
        wb = sb("wb", [P, 8 * 1024 + 8 * 512])
        wsm = sb("wsm", [P, 3200])
        work = sb("work", [P, 11500])
        m0i = sb("m0i", [P, NT], I32)
        m2i = sb("m2i", [P, NT, S], I32)
        qkeep = sb("qkeep", [P, NT])
        slack = sb("slack", [P, 28])
        lg = sb("lg", [P, NT, 16])
        slots = sb("slots", [P, 2, 2 * NT], U32)
        gate = sb("gate", [P, 2, NT])
        etab = sb("etab", [P, 3, 40], I32)
        b2r = sb("b2r", [P, E, D])
        xe = nc.dram_tensor("xe", [ROWS, D], F32, kind="Internal").ap()
        ye = nc.dram_tensor("ye", [ROWS, D], F32, kind="Internal").ap()
        comb = sb("comb", [P, NT, 18])
        ident, ones = [con[:, CONST[n][0]:CONST[n][0] + P] for n in ("ident", "ones")]

        def const(name, rows=P):
            a, w = CONST[name]
            return con[0:rows, a:a + w]

        place = {"wsm": 0}

        def small(name, w, rows=P):
            a = place["wsm"]
            place["wsm"] += w
            return wsm[0:rows, a:a + w]

        wq0, wk0, wv0, wo0 = [small(n, P) for n in ("wq", "wk", "wv", "wo")]
        g_ln, b_ln = small("g", D), small("b", D)
        wr0 = small("wr0", 8)
        w1a = small("w1a", F)
        w2a = small("w2a", F).rearrange("p (f d) -> p f d", f=FB)
        b1a = small("b1a", FB)
        b2a = small("b2a", D)
        ga = [small(f"g{n}", D) for n in range(3)]
        ba = [small(f"b{n}", D) for n in range(3)]
        wr1, br1 = small("wr1", E), small("br1", E)
        end1 = place["wsm"]
        place["wsm"] = 0
        g2, be2 = small("g2", D), small("be2", D)
        wg2, gb2 = small("wg2", EG), small("gb2", EG)
        b2f2 = small("b2f2", D, 18)
        wq3, wk3, wv3 = [small(n, P) for n in ("wq3", "wk3", "wv3")]
        bk3, bv3, bo3 = [small(n, P) for n in ("bk3", "bv3", "bo3")]
        woff3 = small("woff3", 96)
        boff3, bq3, bqx3 = small("boff3", 1), small("bq3", 1), small("bqx3", 2)
        wqx3 = small("wqx3", 2 * P).rearrange("p (h c) -> p h c", h=2)
        wox3 = small("wox3", 2 * P).rearrange("p (h c) -> p h c", h=2)
        wg3, bg3 = small("wg3", E), small("bg3", E)
        assert max(end1, place["wsm"]) <= 3200, (end1, place["wsm"])

        W1 = wa[:, 0:8 * F].rearrange("p (e f) -> p e f", e=E)
        W3 = wa[:, 8 * F:16 * F].rearrange("p (e f) -> p e f", e=E)
        W2 = wa[:, 16 * F:24 * F].rearrange("p (e f d) -> p e f d", e=E, f=FB)
        V1 = wb[:, 0:8 * F].rearrange("p (e f) -> p e f", e=E)
        V2 = wb[:, 8 * F:16 * F].rearrange("p (e f d) -> p e f d", e=E, f=FB)
        VB1 = wb[:, 16 * F:24 * F].rearrange("p (e f) -> p e f", e=E)
        NU = 18 * EI
        U1, U3 = wa[:, 0:NU], wa[:, NU:2 * NU]
        U2 = wa[:, 2 * NU:3 * NU].rearrange("p (f d) -> p f d", f=9)
        UB1, UB3 = wa[:, 3 * NU:4 * NU], wa[:, 4 * NU:5 * NU]

        def carve(start, *shape):
            n = int(np.prod(shape))
            ap = work[:, start:start + n]
            if len(shape) == 2:
                ap = ap.rearrange("p (a b) -> p a b", a=shape[0])
            if len(shape) == 3:
                ap = ap.rearrange("p (a b c) -> p a b c", a=shape[0], b=shape[1])
            return ap

        stats, mv = carve(0, GT, 6), carve(24, GT, 2)
        var, rstd = carve(32, GT), carve(36, GT)
        mx, sm, rs = carve(40, 4 * H), carve(104, 4 * H), carve(168, 4 * H)
        XH, XT = carve(232, GT, D), carve(744, GW)
        N0 = 1256
        SIDES = (0, 1)

        def part(side, n, width=1):
            a = 232 + 5120 * side + 512 * n
            return work[:, a:a + 512 * width]

        def tiles(ap):
            return ap.rearrange("p (t d) -> p t d", d=P)

        stats_, mv_ = [stats, carve(11400, GT, 6)], [mv, carve(11424, GT, 2)]
        var_, rstd_ = [var, carve(11432, GT)], [rstd, carve(11436, GT)]
        XH_, XT_, R_, Y2_ = [[tiles(part(q, n)) if n != 1 else part(q, n) for q in SIDES] for n in range(4)]
        Y1_, SC_ = [[tiles(part(q, n)) for q in SIDES] for n in (4, 5)]
        PTT_, MA_ = [part(q, 6) for q in SIDES], [tiles(part(q, 7)) for q in SIDES]
        HID_ = [part(q, 4, 4).rearrange("p (f c) -> p f c", f=FB) for q in SIDES]
        MF_ = Y2_

        def nth(k, side):
            return 2 * (k - 1) + side + 1

        def of_side(ap, i, side):
            return ap[:, bass.ds(i * 2 * GT + side * GT, GT)]

        names = {}

        def body(name):
            def wrap(f):
                names[name] = f
                return f
            return wrap

        class Chain:

            def __init__(self, eng):
                self.eng = eng

            def start(self, stage, turn):
                self.stage, self.turn, self.k = stage, turn, 0

            def __call__(self, ins):
                self.k += 1
                ins.then_inc(sem["dve"], 1)
                self.eng.wait_ge(sem["dve"], count(self.stage, "dve", self.turn, self.k))

            def end(self):
                plan = {s: r.get("dve", 0) for s, _, r in PLAN}[self.stage]
                assert plan == self.k, (self.stage, self.k)

        def group(ap, i):
            return ap[:, bass.ds(i * GT, GT)]

        def cols(ap, i, w=GW):
            return ap[:, bass.ds(i * w, w)]

        def norm_dve(eng, link, stage, i, k, src, dst, signal=None):
            for j in range(GT):
                last = eng.bn_stats(stats[:, j, :], src[:, j, :])
            link(last)
            eng.memset(slack[:, 0:1], 0.0)
            for j in range(GT):
                last = eng.bn_aggr(mv[:, j, :], stats[:, j, :])
            link(last)
            eng.tensor_scalar(var, mv[:, :, 1], 1.0e-5, None, ALU.add).then_inc(sem["var_ready"], 1)
            eng.wait_ge(sem["rstd_ready"], count(stage, "rstd_ready", i, k))
            for j in range(GT):
                last = eng.tensor_scalar(dst[:, j, :], src[:, j, :], mv[:, j, 0:1], rstd[:, j:j + 1],
                                         ALU.subtract, ALU.mult)
            if signal is None:
                link(last)
            else:
                last.then_inc(sem[signal], 1)

        def norm_in(eng, link, side, src):
            for j in range(GT):
                last = eng.bn_stats(stats_[side][:, j, :], src[:, j, :])
            link(last)
            eng.memset(slack[:, 0:1], 0.0)
            for j in range(GT):
                last = eng.bn_aggr(mv_[side][:, j, :], stats_[side][:, j, :])
            link(last)
            eng.tensor_scalar(var_[side], mv_[side][:, :, 1], 1.0e-5, None, ALU.add).then_inc(sem["var_ready"], 1)

        def norm_out(eng, stage, i, k, side, src, dst):
            eng.wait_ge(sem["rstd_ready"], count(stage, "rstd_ready", i, nth(k, side)))
            for j in range(GT):
                last = eng.tensor_scalar(dst[:, j, :], src[:, j, :], mv_[side][:, j, 0:1], rstd_[side][:, j:j + 1],
                                         ALU.subtract, ALU.mult)
            return last

        def norm_side_pool(eng, stage, i, k, side):
            eng.wait_ge(sem["var_ready"], count(stage, "var_ready", i, nth(k, side)))
            eng.tensor_tensor(rstd_[side], var_[side], const("neghalf").to_broadcast([P, GT]), ALU.pow)\
               .then_inc(sem["rstd_ready"], 1)

        def turn_side_pe(eng, stage, i, k, side, src):
            eng.wait_ge(sem["rows_ready"], count(stage, "rows_ready", i, nth(k, side)))
            for j in range(GT):
                last = eng.transpose(ps[:, 4 * side, j * P:(j + 1) * P], src[:, j, :], ident)
            last.then_inc(sem["turned"], 1)

        def turn_side_act(eng, stage, i, k, side):
            eng.wait_ge(sem["turned"], count(stage, "turned", i, nth(k, side)))
            eng.activation(XT_[side], ps[:, 4 * side, :], ACT.Copy).then_inc(sem["cols_ready"], 1)

        def norm_pool(eng, stage, i, k):
            eng.wait_ge(sem["var_ready"], count(stage, "var_ready", i, k))
            eng.tensor_tensor(rstd, var, const("neghalf").to_broadcast([P, GT]), ALU.pow)\
               .then_inc(sem["rstd_ready"], 1)

        def turn_pe(eng, stage, i, k, src, bank=0):
            eng.wait_ge(sem["rows_ready"], count(stage, "rows_ready", i, k))
            for j in range(GT):
                last = eng.transpose(ps[:, bank, j * P:(j + 1) * P], src[:, j, :], ident)
            last.then_inc(sem["turned"], 1)

        def turn_act(eng, stage, i, k, dst, bank=0):
            eng.wait_ge(sem["turned"], count(stage, "turned", i, k))
            eng.activation(dst, ps[:, bank, :], ACT.Copy).then_inc(sem["cols_ready"], 1)

        def wait_loads(eng, *which):
            for n in which:
                eng.wait_ge(loads[n], 16 * len(load_list[n]))

        def heads(ap):
            return ap.rearrange("p (h d) -> p h d", h=H)

        def b3(ap, n, at):
            a = ap.shape[1]
            return ap.unsqueeze(at).to_broadcast([ap.shape[0], a, n] if at == 2 else [ap.shape[0], n, a])

        QT = carve(N0, GW)
        CTD = carve(N0 + 512, GB, 2 * S)
        KB = carve(N0 + 1536, GB, 4, S)
        VB = carve(N0 + 3584, GB, D)
        S0 = carve(N0 + 4608, 2, H * S)
        E0 = carve(N0 + 6656, 2, H * S)
        PT0 = carve(N0 + 8704, 8, P)
        OT = QT
        MT = lg[:, :, :].rearrange("p a b -> p (a b)")
        O0 = XH

        def dup(b):
            return CTD[:, b, :]

        def a0_pe(eng, i):
            st = "a0"
            eng.wait_ge(sem["x_ready"], count(st, "x_ready", i))
            eng.matmul(ps[:, 2, :], wk0, cols(cT, i), start=True, stop=True).then_inc(sem["k_ps"], 1)
            eng.wait_ge(sem["ct_staged"], count(st, "ct_staged", i, 1))
            for b in range(GB):
                last = eng.matmul(ps[:, 5 + b // 4, (b % 4) * P:(b % 4 + 1) * P], dup(b), wv0, start=True, stop=True)
            last.then_inc(sem["v_ps"], 1)
            turn_pe(eng, st, i, 1, XH)
            eng.wait_ge(sem["cols_ready"], count(st, "cols_ready", i, 1))
            eng.matmul(ps[:, 1, :], wq0, XT, start=True, stop=True).then_inc(sem["q_ps"], 1)

            def scores(j):
                if j == 0:
                    eng.wait_ge(sem["q_ready"], count(st, "q_ready", i, 1))
                    eng.wait_ge(sem["kb_ready"], count(st, "kb_ready", i, 1))
                    eng.wait_ge(sem["vb_ready"], count(st, "vb_ready", i, 1))
                else:
                    eng.wait_ge(sem["sc_read"], count(st, "sc_read", i, j))
                for b in range(2):
                    for q in range(4):
                        last = eng.matmul(ps[S * b:S * b + S, 1 + q, (j % 2) * 256:(j % 2) * 256 + 256],
                                          QT[32 * q:32 * q + 32, j * P + S * b:j * P + S * b + S],
                                          KB[32 * q:32 * q + 32, 2 * j + b, :, :],
                                          start=True, stop=True, tile_position=(32 * q, S * b))
                last.then_inc(sem["sc_ps"], 1)

            scores(0)
            scores(1)
            for j in range(GT):
                eng.wait_ge(sem["ex_ready"], count(st, "ex_ready", i, j + 1))
                if j >= 1:
                    eng.wait_ge(sem["pt_ready"], count(st, "pt_ready", i, j))
                for h in range(8):
                    last = eng.transpose(ps[:, 5 + h // 4, (h % 4) * P:(h % 4 + 1) * P],
                                         E0[:, j % 2, h * P:(h + 1) * P], ident)
                last.then_inc(sem["pt_ps"], 1)
                if j + 2 < GT:
                    scores(j + 2)
                eng.wait_ge(sem["pt_ready"], count(st, "pt_ready", i, j + 1))
                for b in range(2):
                    for h in range(8):
                        last = eng.matmul(ps[S * b:S * b + S, 7, j * P + 16 * h:j * P + 16 * h + 16],
                                          PT0[:, h, S * b:S * b + S], VB[:, 2 * j + b, 16 * h:16 * h + 16],
                                          start=True, stop=True, tile_position=(0, S * b))
                last.then_inc(sem["av_ps"], 1)
            turn_pe(eng, st, i, 2, O0)
            eng.wait_ge(sem["cols_ready"], count(st, "cols_ready", i, 2))
            for j in range(GT):
                last = eng.matmul(ps[:, 1, j * P:(j + 1) * P], OT[:, j * P:(j + 1) * P], wo0, start=True, stop=True)
            last.then_inc(sem["out_ps"], 1)

        def a0_act(eng, i):
            st = "a0"
            turn_act(eng, st, i, 1, XT)
            eng.wait_ge(sem["q_ps"], count(st, "q_ps", i, 1))
            eng.activation(QT, ps[:, 1, :], ACT.Copy).then_inc(sem["q_ready"], 1)

            def exp(j):
                eng.wait_ge(sem["sm_in"], count(st, "sm_in", i, j + 1))
                eng.activation(E0[:, j % 2, :], S0[:, j % 2, :], ACT.Exp, scale=HD ** -0.5)\
                   .then_inc(sem["ex_ready"], 1)

            exp(0)
            exp(1)
            for j in range(GT):
                eng.wait_ge(sem["pt_ps"], count(st, "pt_ps", i, j + 1))
                eng.activation(PT0.rearrange("p a b -> p (a b)"), ps[:, 5:7, :].rearrange("p a b -> p (a b)"),
                               ACT.Copy).then_inc(sem["pt_ready"], 1)
                if j + 2 < GT:
                    exp(j + 2)
            turn_act(eng, st, i, 2, OT)

        def a0_dve(eng, link, i):
            st = "a0"
            link.start(st, i)
            norm_dve(eng, link, st, i, 1, group(xs, i), XH, "rows_ready")
            eng.wait_ge(sem["k_ps"], count(st, "k_ps", i, 1))
            last = None
            for b in range(GB):
                last = eng.tensor_tensor(KB[:, b, :, :], b3(ps[:, 2, b * S:(b + 1) * S], 4, 1),
                                         b3(const("headquad"), S, 2), ALU.mult)
            last.then_inc(sem["kb_ready"], 1)
            eng.wait_ge(sem["v_ps"], count(st, "v_ps", i, 1))
            last = eng.tensor_tensor(VB, ps[:, 5:7, :].rearrange("p a (b c) -> p (a b) c", b=4),
                                     b3(const("headpair"), GB, 1), ALU.mult)
            last.then_inc(sem["vb_ready"], 1)

            def before(j):
                sj, sh = S0[:, j % 2, :], heads(S0[:, j % 2, :])
                keep = qkeep[:, bass.ds(i * GT + j, 1)]
                link(eng.tensor_scalar(MT.rearrange("p (h s) -> p h s", s=S), b3(const("causal"), 4, 1), keep, None,
                                       ALU.mult))
                eng.wait_ge(sem["sc_ps"], count(st, "sc_ps", i, j + 1))
                half = (j % 2) * 4 * S
                eng.scalar_tensor_tensor(out=sj.rearrange("p (q c) -> p q c", q=4),
                                         in0=ps[:, 1:5, half:half + 4 * S], scalar=keep, in1=b3(MT, 4, 1),
                                         op0=ALU.mult, op1=ALU.add).then_inc(sem["sc_read"], 1)
                eng.wait_ge(sem["sc_read"], count(st, "sc_read", i, j + 1))
                m = mx[:, H * j:H * j + H]
                link(eng.tensor_reduce(m, sh, X_AX, ALU.max))
                eng.tensor_tensor(sh, sh, b3(m, S, 2), ALU.subtract).then_inc(sem["sm_in"], 1)

            before(0)
            before(1)
            for j in range(GT):
                eng.wait_ge(sem["ex_ready"], count(st, "ex_ready", i, j + 1))
                link(eng.reduce_sum(sm[:, H * j:H * j + H], heads(E0[:, j % 2, :]), X_AX))
                link(eng.reciprocal(rs[:, H * j:H * j + H], sm[:, H * j:H * j + H]))
                if j + 2 < GT:
                    before(j + 2)
            eng.wait_ge(sem["av_ps"], count(st, "av_ps", i, GT))
            for j in range(GT):
                last = eng.tensor_tensor(heads(O0[:, j, :]), heads(ps[:, 7, j * P:(j + 1) * P]),
                                         b3(rs[:, H * j:H * j + H], HD, 2), ALU.mult)
            last.then_inc(sem["rows_ready"], 1)
            eng.wait_ge(sem["out_ps"], count(st, "out_ps", i, 1))
            g = group(xs, i)
            eng.tensor_tensor(g, g, ps[:, 1, :].rearrange("p (a b) -> p a b", a=GT), ALU.add)\
               .then_inc(sem["x_ready"], 1)
            link.end()

        def bridge(eng, at=0):
            one = const("ref")
            return eng.tensor_tensor(slack[:, at + 1:at + 2], one, one, ALU.add)

        def stage_ct(eng, stage, i):
            eng.wait_ge(sem["v_ps"], count(stage, "v_ps", i, 0))
            bridge(eng)
            src = cols(cT, i).rearrange("p (b s) -> p b s", b=GB).unsqueeze(2).to_broadcast([P, GB, 2, S])
            eng.tensor_copy(CTD.rearrange("p b (r s) -> p b r s", r=2), src).then_inc(sem["ct_staged"], 1)

        def logits_pe(eng, st, i, w, n):
            for q in SIDES:
                turn_side_pe(eng, st, i, 1, q, XH_[q])
            for q in SIDES:
                eng.wait_ge(sem["cols_ready"], count(st, "cols_ready", i, nth(1, q)))
                for j in range(GT):
                    last = eng.matmul(ps[:, 4 * q + 1, j * n:(j + 1) * n], XT_[q][:, j * P:(j + 1) * P], w,
                                      start=True, stop=True)
                last.then_inc(sem["lg_ps"], 1)

        def logits_act(eng, st, i, softmax, n):
            eng.wait_ge(sem["ht_ready"], count(st, "ht_ready", i, 0))
            for q in SIDES:
                turn_side_act(eng, st, i, 1, q)
            if softmax:
                for q in SIDES:
                    eng.wait_ge(sem["exp_in"], count(st, "exp_in", i, nth(1, q)))
                    eng.activation(R_[q].rearrange("p a b -> p (a b)")[:, 0:GT * n],
                                   R_[q].rearrange("p a b -> p (a b)")[:, 0:GT * n], ACT.Exp)\
                       .then_inc(sem["exp_ready"], 1)

        def rows_pool(eng, st, i):
            for q in SIDES:
                eng.wait_ge(sem["rows_ready"], count(st, "rows_ready", i, nth(1, q)))
                bridge(eng, (0, 17)[q])
                eng.tensor_copy(of_side(hr, i, q), XH_[q]).then_inc(sem["ht_ready"], 1)

        def logits_pool(eng, st, i):
            for q in SIDES:
                eng.wait_ge(sem["cols_ready"], count(st, "cols_ready", i, nth(1, q)))
                bridge(eng, (0, 17)[q])
                eng.tensor_copy(hT[:, bass.ds(i * 2 * GW + q * GW, GW)], XT_[q]).then_inc(sem["ht_ready"], 1)

        def logits_dve(eng, link, st, i, n, bias=None, scale=None, softmax=False):
            def logits(q):
                return R_[q].rearrange("p a b -> p (a b)")[:, 0:GT * n].rearrange("p (a b) -> p a b", a=GT)

            for q in SIDES:
                eng.wait_ge(sem["lg_ps"], count(st, "lg_ps", i, nth(1, q)))
                raw = ps[:, 4 * q + 1, 0:GT * n].rearrange("p (a b) -> p a b", a=GT)
                to = of_side(lg, i, q)[:, :, 0:n]
                ls = logits(q)
                if bias is None and not softmax:
                    eng.tensor_copy(to, raw).then_inc(sem["lg_ready"], 1)
                    continue
                if bias is not None:
                    link(eng.tensor_tensor(ls, raw, b3(bias, GT, 1), ALU.add))
                    raw = ls
                if not softmax:
                    eng.tensor_scalar(to, ls, scale, None, ALU.mult).then_inc(sem["lg_ready"], 1)
                    continue
                m = mx[:, GT * q:GT * q + GT]
                link(eng.tensor_reduce(m, raw, X_AX, ALU.max))
                eng.tensor_tensor(ls, raw, b3(m, n, 2), ALU.subtract).then_inc(sem["exp_in"], 1)
            if softmax:
                for q in SIDES:
                    total_, inverse = sm[:, GT * q:GT * q + GT], rs[:, GT * q:GT * q + GT]
                    eng.wait_ge(sem["exp_ready"], count(st, "exp_ready", i, nth(1, q)))
                    link(eng.reduce_sum(total_, logits(q), X_AX))
                    link(eng.reciprocal(inverse, total_))
                    eng.tensor_tensor(of_side(lg, i, q)[:, :, 0:n], logits(q), b3(inverse, n, 2), ALU.mult)\
                       .then_inc(sem["lg_ready"], 1)

        VL, IX = carve(N0, NT, 8), carve(N0 + 128, NT, 8).bitcast(U32)
        IXF = carve(N0 + 256, 2, NT)
        A2 = carve(N0 + 288, 2, NT * 16)
        GATE = carve(N0 + 800, 3, NT)
        T0, T1 = carve(N0 + 1000, 512), carve(N0 + 1512, 512)
        T2, T3 = carve(N0 + 2024, 512), carve(N0 + 2536, 512)
        CUR = carve(N0 + 3048, 8)
        CAND, CNT = carve(N0 + 3056, 8), carve(N0 + 3064, 8)
        CANDS, CNTS, SELS = carve(N0 + 3210, 3, 8), carve(N0 + 3240, 3, 8), carve(N0 + 3270, 24)
        GG = carve(N0 + 3080, NT, 8)

        def marks(n):
            return A2[:, :, 0:NT * n].rearrange("p k (t e) -> p k t e", t=NT)

        def top2(eng, link, src, n, wide):
            for q in range(NT):
                last = eng.max(VL[:, q, :], src[:, q, 0:wide])
            link(last)
            for q in range(NT):
                last = eng.max_index(IX[:, q, :], VL[:, q, :], src[:, q, 0:wide])
            link(last)
            link(eng.tensor_copy(IXF, IX[:, :, 0:2].rearrange("p t k -> p k t")))
            for k in range(2):
                last = eng.tensor_tensor(marks(n)[:, k], b3(const("iota")[:, 0:n], NT, 1), b3(IXF[:, k, :], n, 2),
                                         ALU.is_equal)
            return last

        def prefix(eng, link, a, b, n, w):
            step = 1
            while step < n:
                eng.tensor_copy(b[:, 0:step * w], a[:, 0:step * w])
                link(eng.tensor_tensor(b[:, step * w:n * w], a[:, step * w:n * w], a[:, 0:(n - step) * w], ALU.add))
                a, b = b, a
                step *= 2
            return a

        def exp_gate(eng, st):
            eng.wait_ge(sem["exp_in"], count(st, "exp_in", 0, 1))
            eng.activation(GATE[:, 2, :], GATE[:, 2, :], ACT.Exp).then_inc(sem["exp_ready"], 1)

        def tri(t3, n):
            return t3.rearrange("p (t e) -> p t e", e=n)

        A3 = carve(N0 + 3400, 256)
        SL_ = carve(N0 + 3700, 2, 2 * NT)
        KEPT = carve(N0 + 3764, 2 * NT)

        def choices(ap):
            return ap.rearrange("p (q e) -> p q e", e=8)

        def slots_dve(eng, link, place, kept):
            t2, all_gates = choices(T2[:, 0:256]), gate[:, :, :].rearrange("p k t -> p (k t)")
            link(eng.tensor_tensor(t2, t2, b3(place, 2 * NT, 1), ALU.add))
            link(eng.tensor_tensor(t2, t2, choices(A3), ALU.mult))
            link(eng.reduce_sum(SL_[:, 0, :], t2, X_AX))
            if kept is None:
                link(eng.tensor_copy(SL_[:, 1, :], SL_[:, 0, :]))
            else:
                link(eng.tensor_tensor(T3[:, 0:256], A3, kept, ALU.mult))
                link(eng.reduce_sum(KEPT, choices(T3[:, 0:256]), X_AX))
                link(eng.tensor_tensor(SL_[:, 1, :], SL_[:, 0, :], KEPT, ALU.mult))
                link(eng.tensor_tensor(all_gates, all_gates, KEPT, ALU.mult))
                link(eng.tensor_scalar(KEPT, KEPT, 1.0, -65536.0, ALU.subtract, ALU.mult))
                link(eng.tensor_tensor(SL_[:, 0, :], SL_[:, 0, :], KEPT, ALU.add))
            return eng.tensor_copy(slots[:, :, :], SL_)

        def gates_dve(eng, link, st):
            eng.wait_ge(sem["exp_ready"], count(st, "exp_ready", 0, 1))
            link(eng.tensor_scalar(gate[:, 0, :], GATE[:, 2, :], 1.0, None, ALU.add))
            link(eng.reciprocal(gate[:, 0, :], gate[:, 0, :]))
            link(eng.tensor_tensor(gate[:, 1, :], GATE[:, 2, :], gate[:, 0, :], ALU.mult))

        def places_dve(eng, link, n):
            w = 8 * n
            link(eng.tensor_copy(T0[:, 0:w], ps[:, 1, 0:w]))
            s = prefix(eng, link, T0, T1, n, 8)
            link(eng.tensor_tensor(T2[:, 0:w], s[:, 0:w], ps[:, 1, 0:w], ALU.subtract))
            link(eng.tensor_tensor(T2[:, 0:w], T2[:, 0:w], ps[:, 0, 0:w], ALU.add))
            return s[:, w - 8:w]

        def cum_pe(eng, st, k, src):
            eng.wait_ge(sem["cum_in"], count(st, "cum_in", 0, k))
            n = src.shape[1]
            eng.matmul(ps[:, 0, 0:n], const("upto"), src, start=True, stop=True)
            eng.matmul(ps[:, 1, 0:n], ones, src, start=True, stop=True).then_inc(sem["cum_ps"], 1)

        def g0_dve(eng, link):
            st = "g0"
            link.start(st, 0)
            eng.wait_ge(sem["lg_ready"], total("r0", "lg_ready"))
            link(top2(eng, link, lg, 8, 8))
            eng.tensor_copy(A3.rearrange("p (k c) -> p k c", k=2), A2[:, :, 0:128]).then_inc(sem["cum_in"], 1)
            eng.tensor_tensor(GATE[:, 2, :], VL[:, :, 1], VL[:, :, 0], ALU.subtract).then_inc(sem["exp_in"], 1)
            eng.tensor_copy(etab[:, 0, 0:24], const("experts"))
            eng.wait_ge(sem["cum_ps"], count(st, "cum_ps", 0, 1))
            places_dve(eng, link, 2 * NT)
            kept = T3[:, 256:512]
            link(eng.tensor_scalar(kept, T2[:, 0:256], float(CAP0), None, ALU.is_le))
            gates_dve(eng, link, st)
            slots_dve(eng, link, const("place"), kept).then_inc(sem["slot_ready"], 1)
            link.end()

        def g3_dve(eng, link):
            st = "g3"
            link.start(st, 0)
            eng.wait_ge(sem["lg_ready"], total("r3", "lg_ready"))
            link(top2(eng, link, lg, 8, 8))
            eng.tensor_copy(A3.rearrange("p (k c) -> p k c", k=2), A2[:, :, 0:128]).then_inc(sem["cum_in"], 1)
            eng.tensor_tensor(GATE[:, 2, :], VL[:, :, 1], VL[:, :, 0], ALU.subtract).then_inc(sem["exp_in"], 1)
            eng.wait_ge(sem["cum_ps"], count(st, "cum_ps", 0, 1))
            rows = places_dve(eng, link, 2 * NT)
            link(eng.tensor_scalar(CAND, rows, 1.0 / P, 127.0 / 256.0, ALU.mult, ALU.add))
            link(eng.tensor_scalar(CAND, CAND, 12582912.0, None, ALU.add))
            link(eng.tensor_scalar(CAND, CAND, 12582912.0, None, ALU.subtract))
            link(eng.tensor_copy(T0[:, 0:8], CAND))
            ends = prefix(eng, link, T0, T1, 8, 1)[:, 0:8]
            link(eng.tensor_tensor(CNT, ends, CAND, ALU.subtract))
            link(eng.tensor_scalar(CNT, CNT, float(P), 1.0, ALU.mult, ALU.subtract))
            past = T3[:, 0:320].rearrange("p (n e) -> p n e", e=8)
            link(eng.tensor_tensor(past, b3(const("blocks"), 8, 2), b3(ends, 40, 1), ALU.is_ge))
            link(eng.reduce_sum(T3[:, 400:440], past, X_AX))
            link(eng.tensor_scalar(etab[:, 2, :], T3[:, 400:440], 7.0, None, ALU.min))
            gates_dve(eng, link, st)
            slots_dve(eng, link, CNT, None).then_inc(sem["slot_ready"], 1)
            link.end()

        def t1_dve(eng, link):
            link.start("t1", 0)
            eng.tensor_copy(etab[:, 1, 0:24], const("experts"))
            eng.wait_ge(sem["lg_ready"], total("r1", "lg_ready"))
            link(top2(eng, link, lg, 8, 8))
            eng.tensor_copy(A3.rearrange("p (k c) -> p k c", k=2), A2[:, :, 0:128])
            eng.tensor_copy(gate[:, :, :], VL[:, :, 0:2].rearrange("p t k -> p k t"))
            link(eng.tensor_tensor(T0[:, 0:128], A2[:, 0, 0:128], A2[:, 1, 0:128], ALU.add))
            link(eng.tensor_tensor(tri(T1[:, 0:128], 8), lg[:, :, 0:8], tri(T0[:, 0:128], 8), ALU.mult))
            eng.memset(CUR, 0.0)
            link(eng.scalar_tensor_tensor(out=GG.rearrange("p t e -> p (t e)"), in0=T0[:, 0:128], scalar=-1.0,
                                          in1=T1[:, 0:128], op0=ALU.add, op1=ALU.add))
            link.end()

        def b1_dve(eng, link, r):
            st = "b1"
            link.start(st, r)
            bits = con[:, bass.ds(r * 3 + CONST["bits"][0], 3)].bitcast(U32)
            link(eng.tensor_tensor(CANDS.bitcast(U32), b3(CUR.bitcast(U32), 3, 1), b3(bits, 8, 2), ALU.bitwise_or))
            ge = T0[:, 0:384].rearrange("p (m e t) -> p m e t", m=3, e=8)
            gates = GG.rearrange("p t e -> p e t").unsqueeze(1).to_broadcast([P, 3, 8, NT])
            link(eng.tensor_tensor(ge, gates, CANDS.unsqueeze(3).to_broadcast([P, 3, 8, NT]), ALU.is_ge))
            eng.reduce_sum(CNTS.rearrange("p m e -> p (m e)"), T0[:, 0:384].rearrange("p (c t) -> p c t", t=NT), X_AX)\
               .then_inc(sem["cum_in"], 1)
            eng.wait_ge(sem["cum_ps"], count(st, "cum_ps", r, 1))
            link(eng.tensor_scalar(SELS.bitcast(U32), ps[:, 0, 0:24], float(CAP1), None, ALU.is_ge))
            for m in range(3):
                eng.memset(slack[:, 0:1], 0.0)
                link(eng.copy_predicated(CUR.bitcast(U32), SELS[:, 8 * m:8 * m + 8].bitcast(U32),
                                         CANDS[:, m, :].bitcast(U32)))
            link.end()

        def b1_pe(eng, r):
            eng.wait_ge(sem["cum_in"], count("b1", "cum_in", r, 1))
            eng.matmul(ps[:, 0, 0:24], ones, CNTS.rearrange("p m e -> p (m e)"), start=True, stop=True)\
               .then_inc(sem["cum_ps"], 1)

        def g1_dve(eng, link):
            st = "g1"
            link.start(st, 0)
            eng.tensor_tensor(tri(T2[:, 0:128], 8), GG, b3(CUR, NT, 1), ALU.is_equal)
            eng.tensor_tensor(tri(T2[:, 128:256], 8), GG, b3(CUR, NT, 1), ALU.is_gt).then_inc(sem["cum_in"], 1)
            eng.wait_ge(sem["cum_ps"], count(st, "cum_ps", 0, 1))
            link(eng.tensor_copy(T0[:, 0:128], ps[:, 1, 0:128]))
            s = prefix(eng, link, T0, T1, NT, 8)
            link(eng.tensor_tensor(T3[:, 0:128], s[:, 0:128], ps[:, 1, 0:128], ALU.subtract))
            link(eng.tensor_tensor(T3[:, 0:128], T3[:, 0:128], ps[:, 0, 0:128], ALU.add))
            link(eng.reduce_sum(CNT, ps[:, 1, 128:256].rearrange("p (t e) -> p e t", e=8), X_AX))
            link(eng.tensor_tensor(tri(T3[:, 0:128], 8), tri(T3[:, 0:128], 8), b3(CNT, NT, 1), ALU.add))
            link(eng.scalar_tensor_tensor(out=T3[:, 0:128], in0=T3[:, 0:128], scalar=float(CAP1), in1=T2[:, 0:128],
                                          op0=ALU.is_le, op1=ALU.mult))
            link(eng.tensor_tensor(T3[:, 0:128], T3[:, 0:128], T2[:, 128:256], ALU.add))
            kept = T3[:, 256:512]
            link(eng.tensor_scalar(kept[:, 0:128], T3[:, 0:128], 1.0, None, ALU.min))
            eng.tensor_copy(kept[:, 128:256], kept[:, 0:128]).then_inc(sem["cum_in"], 1)
            eng.wait_ge(sem["cum_ps"], count(st, "cum_ps", 0, 2))
            places_dve(eng, link, NT)
            link(eng.tensor_copy(T2[:, 128:256], T2[:, 0:128]))
            slots_dve(eng, link, const("place"), kept).then_inc(sem["slot_ready"], 1)
            link.end()

        GS = carve(N0 + 3300, NT, 8)

        def g2_dve(eng, link):
            st = "g2"
            link.start(st, 0)
            eng.wait_ge(sem["lg_ready"], total("r2", "lg_ready"))
            eng.memset(GS, NEG)
            link(eng.tensor_tensor(tri(T0[:, 0:256], 16), lg[:, :, :], b3(gb2, NT, 1), ALU.add))
            v = T0[:, 0:256].rearrange("p (g a b) -> p g a b", a=2, b=2)
            hi = T1[:, 0:128].rearrange("p (g a) -> p g a", a=2)
            lo = T1[:, 128:256].rearrange("p (g a) -> p g a", a=2)
            eng.tensor_tensor(hi, v[:, :, :, 0], v[:, :, :, 1], ALU.max)
            link(eng.tensor_tensor(lo, v[:, :, :, 0], v[:, :, :, 1], ALU.min))
            eng.tensor_tensor(T2[:, 0:64], hi[:, :, 0], hi[:, :, 1], ALU.max)
            eng.tensor_tensor(T2[:, 64:128], hi[:, :, 0], hi[:, :, 1], ALU.min)
            link(eng.tensor_tensor(T2[:, 128:192], lo[:, :, 0], lo[:, :, 1], ALU.max))
            link(eng.tensor_tensor(T2[:, 64:128], T2[:, 64:128], T2[:, 128:192], ALU.max))
            link(eng.tensor_tensor(GS[:, :, 0:4], tri(T2[:, 0:64], 4), tri(T2[:, 64:128], 4), ALU.add))
            link(top2(eng, link, GS, 4, 8))
            link(eng.tensor_tensor(T1[:, 0:64], A2[:, 0, 0:64], A2[:, 1, 0:64], ALU.add))
            kept = b3(T1[:, 0:64], 4, 2)
            eng.tensor_scalar(T1[:, 64:128], T1[:, 0:64], 1.0, -NEG, ALU.subtract, ALU.mult)
            link(eng.tensor_tensor(T2[:, 0:256].rearrange("p (g c) -> p g c", c=4),
                                   T0[:, 0:256].rearrange("p (g c) -> p g c", c=4), kept, ALU.mult))
            link(eng.tensor_tensor(T2[:, 0:256].rearrange("p (g c) -> p g c", c=4),
                                   T2[:, 0:256].rearrange("p (g c) -> p g c", c=4), b3(T1[:, 64:128], 4, 2), ALU.add))
            link(top2(eng, link, tri(T2[:, 0:256], 16), 16, 16))
            link(eng.tensor_tensor(T1[:, 0:256], A2[:, 0, 0:256], A2[:, 1, 0:256], ALU.add))
            eng.memset(comb[:, :, 16:18], 1.0)
            eng.tensor_tensor(comb[:, :, 0:16], lg[:, :, :], tri(T1[:, 0:256], 16), ALU.mult).then_inc(sem["c_ready"], 1)
            link.end()

        UW, UN, UG = 384, 3, 6
        NUN = GT * UN
        HS = carve(N0, GW)
        CSS, CTR = carve(N0 + 512, GT, 18), carve(N0 + 600, GW)
        SLU, S3U, GU = carve(N0 + 1200, 2, UW), carve(N0 + 2000, 2, UW), carve(N0 + 2800, 2, UW)
        GTU = carve(N0 + 3600, 2, UW)

        def f2_pe(eng, i):
            st = "f2"
            eng.wait_ge(sem["h_staged"], count(st, "h_staged", i, 1))
            eng.wait_ge(sem["c_in"], count(st, "c_in", i, 1))
            eng.wait_ge(sem["x_ready"], count(st, "x_ready", i))
            for j in range(GT):
                last = eng.transpose(ps[0:18, 7, j * P:(j + 1) * P], CSS[:, j, :], ident)
            last.then_inc(sem["c_turned"], 1)

            def up(u):
                if u < NUN:
                    j, c = divmod(u, UN)
                    for n, w in enumerate((U1, U3)):
                        last = eng.matmul(ps[:, 2 * (u % 2) + n, 0:UW], HS[:, j * P:(j + 1) * P],
                                          w[:, UW * c:UW * c + UW], start=True, stop=True)
                    last.then_inc(sem["h_ps"], 1)

            up(0)
            up(1)
            for u in range(NUN):
                j, c = divmod(u, UN)
                eng.wait_ge(sem["mid_ready"], count(st, "mid_ready", i, u + 1))
                for f in range(UW // P):
                    last = eng.transpose(ps[:, 4 + u % 2, f * P:(f + 1) * P], GU[:, u % 2, f * P:(f + 1) * P], ident)
                last.then_inc(sem["mid_ps"], 1)
                up(u + 2)
                if c == 0:
                    if j == 0:
                        eng.wait_ge(sem["cT_ready"], count(st, "cT_ready", i, 1))
                    if j >= 2:
                        eng.wait_ge(sem["x_ready"], count(st, "x_ready", i, j - 1))
                    eng.matmul(ps[:, 6 + j % 2, 0:D], CTR[0:18, j * P:(j + 1) * P], b2f2, start=True, stop=False)
                eng.wait_ge(sem["midT_ready"], count(st, "midT_ready", i, u + 1))
                for f in range(UW // P):
                    last = eng.matmul(ps[:, 6 + j % 2, 0:D], GTU[:, u % 2, f * P:(f + 1) * P], U2[:, 3 * c + f, :],
                                      start=False, stop=(c == UN - 1 and f == UW // P - 1))
                if c == UN - 1:
                    last.then_inc(sem["y_ps"], 1)

        def f2_act(eng, i):
            st = "f2"
            eng.wait_ge(sem["c_turned"], count(st, "c_turned", i, 1))
            eng.activation(CTR[0:18, :], ps[0:18, 7, :], ACT.Copy).then_inc(sem["cT_ready"], 1)

            def silu(u):
                if u < NUN:
                    eng.wait_ge(sem["act_in"], count(st, "act_in", i, u + 1))
                    eng.activation(SLU[:, u % 2, :], SLU[:, u % 2, :], ACT.Silu).then_inc(sem["act_ready"], 1)

            silu(0)
            silu(1)
            for u in range(NUN):
                eng.wait_ge(sem["mid_ps"], count(st, "mid_ps", i, u + 1))
                eng.activation(GTU[:, u % 2, :], ps[:, 4 + u % 2, 0:UW], ACT.Copy).then_inc(sem["midT_ready"], 1)
                silu(u + 2)

        def f2_dve(eng, link, i):
            st = "f2"
            link.start(st, i)
            eng.wait_ge(sem["c_turned"], count(st, "c_turned", i))
            eng.tensor_scalar(CSS, group(comb, i), 1.0, None, ALU.mult).then_inc(sem["c_in"], 1)

            def before(u):
                if u < NUN:
                    j, c = divmod(u, UN)
                    eng.wait_ge(sem["h_ps"], count(st, "h_ps", i, u + 1))
                    eng.tensor_tensor(SLU[:, u % 2, :], ps[:, 2 * (u % 2), 0:UW], UB1[:, UW * c:UW * c + UW], ALU.add)\
                       .then_inc(sem["act_in"], 1)
                    link(eng.tensor_tensor(S3U[:, u % 2, :], ps[:, 2 * (u % 2) + 1, 0:UW], UB3[:, UW * c:UW * c + UW],
                                           ALU.add))
                    s3 = S3U[:, u % 2, :].rearrange("p (g c) -> p g c", g=UG)
                    link(eng.tensor_tensor(s3, s3, b3(CSS[:, j, UG * c:UG * c + UG], UW // UG, 2), ALU.mult))

            def add(j):
                eng.wait_ge(sem["y_ps"], count(st, "y_ps", i, j + 1))
                x = xs[:, bass.ds(i * GT + j, 1), :].rearrange("p a d -> p (a d)")
                eng.tensor_tensor(x, x, ps[:, 6 + j % 2, 0:D], ALU.add).then_inc(sem["x_ready"], 1)

            eng.wait_ge(sem["c_in"], count(st, "c_in", i, 1))
            def gated(u):
                if u < NUN:
                    eng.wait_ge(sem["act_ready"], count(st, "act_ready", i, u + 1))
                    eng.tensor_tensor(GU[:, u % 2, :], SLU[:, u % 2, :], S3U[:, u % 2, :], ALU.mult)\
                       .then_inc(sem["mid_ready"], 1)

            before(0)
            before(1)
            gated(0)
            for u in range(NUN):
                gated(u + 1)
                before(u + 2)
                if u >= UN + 1 and (u - 1) % UN == 0:
                    add((u - 1) // UN - 1)
            add(GT - 1)
            link.end()

        def f2_pool(eng, i):
            eng.wait_ge(sem["y_ps"], count("f2", "y_ps", i))
            bridge(eng)
            eng.tensor_copy(HS, cols(hT, i)).then_inc(sem["h_staged"], 1)

        f2 = (f2_pe, f2_act, f2_dve, f2_pool)

        XE = carve(N0, KB_, D)
        XTS = carve(N0 + 1024, 2, P)
        SLB = carve(N0 + 1280, 3, F)
        GB_, GTB = carve(N0 + 2816, 2, F), carve(N0 + 3840, 2, F)
        YS = carve(N0 + 4864, KB_, D)
        GATH = carve(N0, 2 * NT, D)

        def moe(st, layer, w1, w3, w2, b1):
            shared = layer is None
            KB = PLACES[st][0]

            def expert(eng, i, k):
                if shared:
                    return E - 1
                return eng.value_load(etab[0:1, layer, bass.ds(i * KB + k, 1)], min_val=0, max_val=E - 1)

            deep = w3 is None

            def sp(eng, i):
                for k in range(KB):
                    eng.wait_ge(sem["xt_ps"], count(st, "xt_ps", i, k + 1 - KB))
                    rows = hr[:, bass.ds(i * KB + k, 1), :].rearrange("p a d -> p (a d)") if shared\
                        else xe[bass.ds((i * KB + k) * P, P), :]
                    eng.dma_start(XE[:, k, :], rows).then_inc(sem[f"xe{k}"], 16)

            def pe(eng, i):
                which = {}

                def turn(k):
                    if k < KB:
                        eng.wait_ge(sem[f"xe{k}"], count(st, f"xe{k}", i, 16))
                        if k >= 1:
                            eng.wait_ge(sem["xt_ready"], count(st, "xt_ready", i, k))
                        eng.transpose(ps[:, 6, 0:P], XE[:, k, :], ident).then_inc(sem["xt_ps"], 1)

                def up(k):
                    if k < KB:
                        which[k] = expert(eng, i, k)
                        eng.wait_ge(sem["xt_ready"], count(st, "xt_ready", i, k + 1))
                        b = k % 3 if deep else 2 * (k % 2)
                        last = eng.matmul(ps[:, b, :], XTS[:, k % 2, :], w1[:, bass.ds(which[k], 1), :],
                                          start=True, stop=True)
                        if w3 is not None:
                            last = eng.matmul(ps[:, b + 1, :], XTS[:, k % 2, :], w3[:, bass.ds(which[k], 1), :],
                                              start=True, stop=True)
                        last.then_inc(sem["h_ps"], 1)

                turn(0)
                up(0)
                turn(1)
                up(1)
                turn(2)
                for k in range(KB):
                    eng.wait_ge(sem["mid_ready"], count(st, "mid_ready", i, k + 1))
                    for f in range(FB):
                        last = eng.transpose(ps[:, 4 + k % 2, f * P:(f + 1) * P], GB_[:, k % 2, f * P:(f + 1) * P], ident)
                    last.then_inc(sem["mid_ps"], 1)
                    up(k + 2)
                    turn(k + 3)
                    eng.wait_ge(sem["y_read"], count(st, "y_read", i, k))
                    eng.wait_ge(sem["midT_ready"], count(st, "midT_ready", i, k + 1))
                    for f in range(FB):
                        last = eng.matmul(ps[:, 7, 0:D], GTB[:, k % 2, f * P:(f + 1) * P],
                                          w2[:, bass.ds(which[k] * FB + f, 1), :], start=(f == 0), stop=(f == FB - 1))
                    last.then_inc(sem["y_ps"], 1)

            def act(eng, i):
                def turned(k):
                    if k < KB:
                        eng.wait_ge(sem["xt_ps"], count(st, "xt_ps", i, k + 1))
                        eng.activation(XTS[:, k % 2, :], ps[:, 6, 0:P], ACT.Copy).then_inc(sem["xt_ready"], 1)

                def silu(k):
                    if k < KB:
                        if deep:
                            eng.wait_ge(sem["act_in"], count(st, "act_in", i, k + 1))
                            eng.activation(GB_[:, k % 2, :], SLB[:, k % 3, :], ACT.Silu).then_inc(sem["mid_ready"], 1)
                        else:
                            eng.wait_ge(sem["h_ps"], count(st, "h_ps", i, k + 1))
                            eng.activation(SLB[:, k % 3, :], ps[:, 2 * (k % 2), :], ACT.Silu)\
                               .then_inc(sem["act_ready"], 1)

                def mid(k):
                    eng.wait_ge(sem["mid_ps"], count(st, "mid_ps", i, k + 1))
                    eng.activation(GTB[:, k % 2, :], ps[:, 4 + k % 2, :], ACT.Copy).then_inc(sem["midT_ready"], 1)

                turned(0)
                turned(1)
                silu(0)
                turned(2)
                silu(1)
                for k in range(KB):
                    mid(k)
                    turned(k + 3)
                    silu(k + 2)

            def dve(eng, link, i):
                link.start(st, i)
                which = {}

                def hidden_in(k):
                    if k >= KB:
                        return
                    if deep:
                        which[k] = expert(eng, i, k)
                        eng.wait_ge(sem["h_ps"], count(st, "h_ps", i, k + 1))
                        eng.tensor_tensor(SLB[:, k % 3, :], ps[:, k % 3, :], b1[:, bass.ds(which[k], 1), :], ALU.add)\
                           .then_inc(sem["act_in"], 1)
                    else:
                        eng.wait_ge(sem["act_ready"], count(st, "act_ready", i, k + 1))
                        eng.tensor_tensor(GB_[:, k % 2, :], SLB[:, k % 3, :], ps[:, 2 * (k % 2) + 1, :], ALU.mult)\
                           .then_inc(sem["mid_ready"], 1)

                hidden_in(0)
                hidden_in(1)
                for k in range(KB):
                    if k + 2 < KB or deep:
                        hidden_in(k + 2)
                    if not shared:
                        eng.wait_ge(sem["ys_free"], count(st, "ys_free", i, k + 1 - KB))
                    eng.wait_ge(sem["y_ps"], count(st, "y_ps", i, k + 1))
                    if shared:
                        x = xs[:, bass.ds(i * KB + k, 1), :].rearrange("p a d -> p (a d)")
                        eng.tensor_tensor(x, x, ps[:, 7, 0:D], ALU.add).then_inc(sem["y_read"], 1)
                    elif deep:
                        eng.tensor_tensor(YS[:, k, :], ps[:, 7, 0:D], b2r[:, bass.ds(which[k], 1), :], ALU.add)\
                           .then_inc(sem["y_read"], 1)
                    else:
                        eng.tensor_scalar(YS[:, k, :], ps[:, 7, 0:D], 1.0, None, ALU.mult).then_inc(sem["y_read"], 1)
                link.end()

            def pool(eng, i):
                for k in range(KB):
                    eng.wait_ge(sem["y_read"], count(st, "y_read", i, k + 1))
                    bridge(eng, 1 + k)
                    eng.dma_start(ye[bass.ds((i * KB + k) * P, P), :], YS[:, k, :]).then_inc(sem[f"ys{k}"], 16)
                    for done in ([k - 2] if k >= 2 else []) + ([k - 1, k] if k == KB - 1 else []):
                        eng.wait_ge(sem[f"ys{done}"], count(st, f"ys{done}", i, 16))
                        bridge(eng, 1 + KB + done).then_inc(sem["ys_free"], 1)

            return pe, act, dve, pool, sp

        def flat_w(w):
            return w.rearrange("p e f d -> p (e f) d")

        s0 = moe("s0", None, W1, W3, flat_w(W2), None)
        f0 = moe("f0", 0, W1, W3, flat_w(W2), None)
        f1 = moe("f1", 1, V1, None, flat_w(V2), VB1)
        f3 = moe("f3", 2, V1, None, flat_w(V2), VB1)

        def row_index(way, n):
            return bass.IndirectOffsetOnAxis(ap=slots[:, way, n:n + 1], axis=0)

        def dispatch_pool(eng, layer):
            eng.wait_ge(sem["slot_ready"], total("g" + layer, "slot_ready"))
            eng.wait_ge(sem["ht_ready"], total("r" + layer, "ht_ready"))
            eng.wait_ge(s_zero, 16 * 2)
            for n in range(2 * NT):
                eng.indirect_dma_start(xe, row_index(0, n), hr[:, n % NT, :], None,
                                       bounds_check=ROWS - 1, oob_is_err=False).then_inc(s_sent, 16)

        def gather(eng, g, k, j, to):
            eng.indirect_dma_start(to, None, ye, row_index(1, NT * k + GT * g + j),
                                   bounds_check=ROWS - 1, oob_is_err=False).then_inc(s_back[g], 16)

        def experts_done(eng, st):
            for k in range(PLACES[st][0]):
                eng.wait_ge(sem[f"ys{k}"], total(st, f"ys{k}"))

        def gather_pool(eng):
            experts_done(eng, "f3")
            for g in range(NG):
                for j in range(GT):
                    for k in range(2):
                        gather(eng, g, k, j, GATH[:, NT * k + GT * g + j, :])

        def gather_turns_pool(eng, st, layer, norms):
            def rows(g):
                q = g % 2
                if g >= 2:
                    eng.wait_ge(sem["combined"], count(st, "combined", g // 2 - 1, q + 1))
                for j in range(GT):
                    for k in range(2):
                        gather(eng, g, k, j, hr[:, 2 * GT * q + GT * k + j, :])

            def relay(g):
                eng.wait_ge(s_back[g], 16 * 2 * GT * (layer + 1))
                bridge(eng, 18 + NG * layer + g).then_inc(sem["gathered"], 1)

            experts_done(eng, f"f{layer}")
            rows(0)
            rows(1)
            relay(0)
            relay(1)
            for i in range(LOOPS[st]):
                for k in range(norms):
                    for q in SIDES:
                        norm_side_pool(eng, st, i, k + 1, q)
                    if i == 0 and k < 2:
                        rows(2 + k)
                    if i == 0 and k == 1:
                        relay(2)
                        relay(3)

        def combine_turn_dve(eng, link, st, i):
            for q in SIDES:
                eng.wait_ge(sem["gathered"], count(st, "gathered", i, q + 1))
                for k in range(2):
                    for j in range(GT):
                        tile = i * 2 * GT + q * GT + j
                        x = xs[:, bass.ds(tile, 1), :].rearrange("p a d -> p (a d)")
                        last = eng.scalar_tensor_tensor(out=x, in0=hr[:, 2 * GT * q + GT * k + j, :],
                                                        scalar=gate[:, k, bass.ds(tile, 1)], in1=x,
                                                        op0=ALU.mult, op1=ALU.add)
                    if k == 0:
                        link(last)
                last.then_inc(sem["combined"], 1)
                eng.wait_ge(sem["combined"], count(st, "combined", i, q + 1))
            eng.memset(slack[:, 0:1], 0.0)

        def combine_dve(eng, link):
            link.start("c3", 0)
            for g in range(NG):
                eng.wait_ge(s_back[g], 16 * 2 * GT * 3)
                for k in range(2):
                    for j in range(GT):
                        q = GT * g + j
                        last = eng.scalar_tensor_tensor(out=xs[:, q, :], in0=GATH[:, NT * k + q, :],
                                                        scalar=gate[:, k, q:q + 1], in1=xs[:, q, :],
                                                        op0=ALU.mult, op1=ALU.add)
                    if k == 0:
                        link(last)
                last.then_inc(sem["x_ready"], 1)
            link.end()

        def scores_pe(eng, st, i, k, q, qT, keys):
            for j in range(GT):
                last = eng.matmul(ps[:, 4 * q + 1, j * P:(j + 1) * P], qT[:, j * P:(j + 1) * P], keys(j),
                                  start=True, stop=True)
            last.then_inc(sem["sc_ps"], 1)

        def weights_pe(eng, st, i, k, q):
            eng.wait_ge(sem["ex_ready"], count(st, "ex_ready", i, nth(k, q)))
            for j in range(GT):
                last = eng.transpose(ps[:, 4 * q + 2, j * P:(j + 1) * P], SC_[q][:, j, :], ident)
            last.then_inc(sem["pt_ps"], 1)

        def values_pe(eng, st, i, k, q, vals):
            eng.wait_ge(sem["pt_ready"], count(st, "pt_ready", i, nth(k, q)))
            for j in range(GT):
                last = eng.matmul(ps[:, 4 * q + 3, j * P:(j + 1) * P], PTT_[q][:, j * P:(j + 1) * P], vals(j),
                                  start=True, stop=True)
            last.then_inc(sem["av_ps"], 1)

        def attend_act(eng, st, i, k):
            for q in SIDES:
                eng.wait_ge(sem["sm_in"], count(st, "sm_in", i, nth(k, q)))
                eng.activation(SC_[q], SC_[q], ACT.Exp, scale=D ** -0.5).then_inc(sem["ex_ready"], 1)
            for q in SIDES:
                eng.wait_ge(sem["pt_ps"], count(st, "pt_ps", i, nth(k, q)))
                eng.activation(PTT_[q], ps[:, 4 * q + 2, :], ACT.Copy).then_inc(sem["pt_ready"], 1)

        def quad(ap):
            return ap.rearrange("p (a b) -> p a b", a=GT)

        def attend_dve(eng, link, st, i, k, bias):
            for q in SIDES:
                eng.wait_ge(sem["sc_ps"], count(st, "sc_ps", i, nth(k, q)))
                bias(q)
                m = mx[:, GT * q:GT * q + GT]
                link(eng.tensor_reduce(m, SC_[q], X_AX, ALU.max))
                eng.tensor_tensor(SC_[q], SC_[q], b3(m, P, 2), ALU.subtract).then_inc(sem["sm_in"], 1)
            for q in SIDES:
                eng.wait_ge(sem["ex_ready"], count(st, "ex_ready", i, nth(k, q)))
                link(eng.reduce_sum(sm[:, GT * q:GT * q + GT], SC_[q], X_AX))
                link(eng.reciprocal(rs[:, GT * q:GT * q + GT], sm[:, GT * q:GT * q + GT]))

        def context_keys(i, q):
            return lambda j: cT[:, bass.ds(i * 2 * GW + q * GW + j * P, P)]

        def context_rows(i, q):
            return lambda j: cs[:, bass.ds(i * 2 * GT + q * GT + j, 1), :]

        def a1_pe(eng, i):
            st = "a1"
            for k in (1, 2):
                for q in SIDES:
                    turn_side_pe(eng, st, i, k, q, XH_[q] if k == 1 else Y1_[q])
                for q in SIDES:
                    eng.wait_ge(sem["cols_ready"], count(st, "cols_ready", i, nth(k, q)))
                    scores_pe(eng, st, i, k, q, XT_[q], (lambda j: XT_[q][:, j * P:(j + 1) * P]) if k == 1
                              else context_keys(i, q))
                for q in SIDES:
                    weights_pe(eng, st, i, k, q)
                for q in SIDES:
                    values_pe(eng, st, i, k, q, (lambda j: XH_[q][:, j, :]) if k == 1 else context_rows(i, q))
            for q in SIDES:
                turn_side_pe(eng, st, i, 3, q, Y2_[q])
            for q in SIDES:
                eng.wait_ge(sem["cols_ready"], count(st, "cols_ready", i, nth(3, q)))
                for f in range(FB):
                    last = eng.matmul(ps[:, 4 * q + f, :], w1a[:, f * P:(f + 1) * P], XT_[q], start=True, stop=True)
                last.then_inc(sem["h_ps"], 1)
            for q in SIDES:
                eng.wait_ge(sem["mid_ready"], count(st, "mid_ready", i, nth(1, q)))
                for j in range(GT):
                    for f in range(FB):
                        last = eng.matmul(ps[:, 4 * q + 1, j * P:(j + 1) * P], HID_[q][:, f, j * P:(j + 1) * P],
                                          w2a[:, f, :], start=(f == 0), stop=(f == FB - 1))
                last.then_inc(sem["y_ps"], 1)

        def a1_act(eng, i):
            st = "a1"
            for k in (1, 2, 3):
                for q in SIDES:
                    turn_side_act(eng, st, i, k, q)
                if k < 3:
                    attend_act(eng, st, i, k)

        def affine(eng, link, y, g, b, signal=None):
            link(eng.tensor_tensor(y, y, b3(g, GT, 1), ALU.mult))
            last = eng.tensor_tensor(y, y, b3(b, GT, 1), ALU.add)
            if signal:
                last.then_inc(sem[signal], 1)
            else:
                link(last)

        def weighted(eng, q, add):
            for j in range(GT):
                value, inverse = ps[:, 4 * q + 3, j * P:(j + 1) * P], rs[:, GT * q + j:GT * q + j + 1]
                if add is None:
                    last = eng.tensor_scalar(R_[q][:, j, :], value, inverse, None, ALU.mult)
                else:
                    last = eng.scalar_tensor_tensor(out=R_[q][:, j, :], in0=value, scalar=inverse, in1=add[:, j, :],
                                                    op0=ALU.mult, op1=ALU.add)
            return last

        def a1_dve(eng, link, i):
            st = "a1"
            link.start(st, i)
            combine_turn_dve(eng, link, st, i)
            for q in SIDES:
                norm_in(eng, link, q, of_side(xs, i, q))
            for q in SIDES:
                norm_out(eng, st, i, 1, q, of_side(xs, i, q), XH_[q]).then_inc(sem["rows_ready"], 1)
            for k, masks, before, after in ((1, "causal2", XH_, Y1_), (2, "same2", Y1_, Y2_)):
                attend_dve(eng, link, st, i, k, lambda q: link(eng.tensor_tensor(
                    SC_[q], quad(ps[:, 4 * q + 1, :]), b3(const(masks), GT, 1), ALU.add)))
                for q in SIDES:
                    eng.wait_ge(sem["av_ps"], count(st, "av_ps", i, nth(k, q)))
                    link(weighted(eng, q, before[q]))
                    norm_in(eng, link, q, R_[q])
                for q in SIDES:
                    link(norm_out(eng, st, i, k + 1, q, R_[q], after[q]))
                    affine(eng, link, after[q], ga[k - 1], ba[k - 1], "rows_ready")
            for q in SIDES:
                eng.wait_ge(sem["h_ps"], count(st, "h_ps", i, nth(1, q)))
                for f in range(FB):
                    last = eng.tensor_scalar(HID_[q][:, f, :], ps[:, 4 * q + f, :], b1a[:, f:f + 1], 0.0, ALU.add,
                                             ALU.max)
                last.then_inc(sem["mid_ready"], 1)
            for q in SIDES:
                eng.wait_ge(sem["y_ps"], count(st, "y_ps", i, nth(1, q)))
                link(eng.tensor_tensor(R_[q], quad(ps[:, 4 * q + 1, :]), b3(b2a, GT, 1), ALU.add))
                link(eng.tensor_tensor(R_[q], R_[q], Y2_[q], ALU.add))
                norm_in(eng, link, q, R_[q])
            for q in SIDES:
                link(norm_out(eng, st, i, 4, q, R_[q], Y1_[q]))
                affine(eng, link, Y1_[q], ga[2], ba[2])
                g = of_side(xs, i, q)
                eng.tensor_tensor(g, g, Y1_[q], ALU.add).then_inc(sem["x_ready"], 1)
            link.end()

        def a2_pe(eng, i):
            st = "a2"
            for q in SIDES:
                turn_side_pe(eng, st, i, 1, q, XH_[q])
            for q in SIDES:
                eng.wait_ge(sem["cols_ready"], count(st, "cols_ready", i, nth(1, q)))
                scores_pe(eng, st, i, 1, q, XT_[q], context_keys(i, q))
            for q in SIDES:
                weights_pe(eng, st, i, 1, q)
            for q in SIDES:
                values_pe(eng, st, i, 1, q, context_rows(i, q))

        def a2_act(eng, i):
            for q in SIDES:
                turn_side_act(eng, "a2", i, 1, q)
            attend_act(eng, "a2", i, 1)

        def a2_dve(eng, link, i):
            st = "a2"
            link.start(st, i)
            combine_turn_dve(eng, link, st, i)
            for q in SIDES:
                norm_in(eng, link, q, of_side(xs, i, q))
            for q in SIDES:
                norm_out(eng, st, i, 1, q, of_side(xs, i, q), XH_[q]).then_inc(sem["rows_ready"], 1)
            for q in SIDES:
                link(eng.memset(MF_[q], 0.0))
                for b in range(2):
                    r = slice(S * b, S * b + S)
                    last = eng.tensor_scalar(MF_[q][r, :, r], m2i[r, bass.ds(i * 2 * GT + q * GT, GT), :], 0.0, None,
                                             ALU.not_equal)
                link(last)
                link(eng.tensor_scalar(MA_[q], MF_[q], 9.0e15, 9.0e15, ALU.mult, ALU.subtract))
                link(eng.tensor_tensor(MA_[q], MA_[q], b3(const("same2"), GT, 1), ALU.add))

            def masked(q):
                link(eng.tensor_tensor(SC_[q], quad(ps[:, 4 * q + 1, :]), MF_[q], ALU.mult))
                link(eng.tensor_tensor(SC_[q], SC_[q], MA_[q], ALU.add))

            attend_dve(eng, link, st, i, 1, masked)
            for q in SIDES:
                eng.wait_ge(sem["av_ps"], count(st, "av_ps", i, nth(1, q)))
                link(weighted(eng, q, None))
                norm_in(eng, link, q, R_[q])
            for q in SIDES:
                link(norm_out(eng, st, i, 2, q, R_[q], Y1_[q]))
                affine(eng, link, Y1_[q], g2, be2)
                g = of_side(xs, i, q)
                eng.tensor_tensor(g, g, Y1_[q], ALU.add).then_inc(sem["x_ready"], 1)
            link.end()

        KH = 96
        QT3 = carve(N0, GW)
        QX = carve(N0 + 1536, 2, GW)
        IXT, LT1, LT2 = [work[0:KH, N0 + 2560 + 512 * n:N0 + 3072 + 512 * n] for n in range(3)]
        KV = carve(N0 + 4096, GB, 8, 32)
        OX = carve(N0 + 6144, 2, GW)
        PRD, TT, EX, WW = [carve(N0 + 7168 + 640 * n, 2, NK, S) for n in range(4)]
        SMQ, RQ, UQ, MQ = [carve(N0 + 9728 + 128 * n, 2, S) for n in range(4)]
        KVT = carve(N0 + 7168, GB, D)
        PAIRS = carve(N0 + 2560, 2, 2, S)
        AH = wa[:, 0:10240].rearrange("p (r j k c) -> p r j k c", r=2, j=4, k=NK)
        AB = wa[:, 10240:11776].rearrange("p (r c) -> p r c", r=3)
        windows = wa[0:KH, 10240:12288]
        WIN = hT[0:KH, 0:1024].bitcast(BF16)
        IXB = hT[0:KH, 1024:1792].bitcast(BF16).rearrange("p (n c) -> p n c", n=3)
        PARTS = work[0:KH, N0 + 7168:N0 + 7936].bitcast(BF16).rearrange("p (n c) -> p n c", n=3)
        M3 = wa[0:KH, 8192:10240].bitcast(I32).rearrange("p (b s) -> p b s", b=B)
        LEN, SGN, INV = [wa[0:KH, 11776 + 32 * n:11808 + 32 * n] for n in range(3)]
        SG = GW // 2
        CHUNKS = [(j, ks) for j0 in range(2) for ks in ((0, 1), (2, 3), (4,)) for j in (j0, j0 + 2)]
        SKV_BANK = (3, 4, 7)
        NU3 = 16

        AHEAD = 15

        def with_unit(u):
            return range(min(AHEAD + 3 * u, 48), min(AHEAD + 3 * u + 3, 48)) if u >= 0 else ()

        def unit(u):
            n, b = divmod(u, 4)
            return n, n // 2, n % 2, b

        def m3_dve(eng, link):
            link.start("m3", 0)
            link(eng.tensor_copy(WIN, windows))
            link(eng.reduce_sum(LEN, M3, X_AX))
            link(eng.tensor_scalar(LEN, LEN, -1.0, float(S - 1), ALU.mult, ALU.add))
            link(eng.tensor_scalar(SGN, LEN, 0.0, None, ALU.is_ge))
            link(eng.tensor_scalar(SGN, SGN, 2.0, 1.0, ALU.mult, ALU.subtract))
            link(eng.tensor_tensor(LEN, LEN, SGN, ALU.mult))
            link(eng.reciprocal(INV, LEN))
            link.end()

        def a3_pe(eng, i):
            st = "a3"

            def kv(w):
                for b in range(GB):
                    last = eng.matmul(ps[:, 5 + b // 4, (b % 4) * P:(b % 4 + 1) * P], dup(b), w, start=True, stop=True)
                return last

            eng.wait_ge(sem["ct_staged"], count(st, "ct_staged", i, 1))
            kv(wk3).then_inc(sem["k_ps"], 1)
            turn_pe(eng, st, i, 1, XH)
            eng.wait_ge(sem["cols_ready"], count(st, "cols_ready", i, 1))
            eng.matmul(ps[:, 1, :], wq3, XT, start=True, stop=True)
            for h in range(2):
                last = eng.matmul(ps[:, 2 + h, :], wqx3[:, h, :], XT, start=True, stop=True)
            last.then_inc(sem["q_ps"], 1)
            eng.wait_ge(sem["q_ready"], count(st, "q_ready", i, 1))
            eng.matmul(ps[0:KH, 4, :], woff3, QT3, start=True, stop=True).then_inc(sem["off_ps"], 1)
            eng.wait_ge(sem["k_read"], count(st, "k_read", i, 1))
            kv(wv3).then_inc(sem["v_ps"], 1)
            eng.wait_ge(sem["ix_ready"], count(st, "ix_ready", i, 1))
            eng.wait_ge(sem["kv_ready"], count(st, "kv_ready", i, 1))

            def gaps(c):
                n, (j, ks) = c // 12, CHUNKS[c % 12]
                hp = 4 * (n % 2) + j
                if c >= 3:
                    eng.wait_ge(sem["gap_ready"], count(st, "gap_ready", i, c - 2))
                for m, k in enumerate(ks):
                    first = S * (16 * (k % 2) + 2 * hp)
                    last = eng.matmul(ps[:, c % 3, m * SG:(m + 1) * SG], WIN[:, first:first + 2 * S],
                                      IXB[:, k // 2, (n // 2) * SG:(n // 2 + 1) * SG], start=True, stop=True)
                last.then_inc(sem["gap_ps"], 1)

            def sampled(u):
                n, sg, half, b = unit(u)
                if b == 0:
                    eng.wait_ge(sem["hat_ready"], count(st, "hat_ready", i, 6 * (n + 1)))
                    eng.wait_ge(sem["odd_hat_ready"], count(st, "odd_hat_ready", i, 6 * (n + 1)))
                if u >= 3:
                    eng.wait_ge(sem["skv_read"], count(st, "skv_read", i, u - 2))
                for j in range(4):
                    last = eng.matmul(ps[32 * j:32 * j + 32, SKV_BANK[u % 3], 0:NK * S], KV[:, 4 * sg + b, 4 * half + j, :],
                                      AH[:, n % 2, j, :, b * S:(b + 1) * S], start=True, stop=True,
                                      tile_position=(0, 32 * j))
                last.then_inc(sem["skv_ps"], 1)

            for c in range(AHEAD):
                gaps(c)
            sampled(0)
            for u in range(NU3):
                eng.wait_ge(sem["prod_ready"], count(st, "prod_ready", i, u + 1))
                if u >= 2:
                    eng.wait_ge(sem["sm_in"], count(st, "sm_in", i, u - 1))
                eng.matmul(ps[:, 5 + u % 2, 0:NK * S], const("spread"), PRD[:, u % 2, :, :].rearrange("p k q -> p (k q)"),
                           start=True, stop=True).then_inc(sem["score_ps"], 1)
                for c in with_unit(u):
                    gaps(c)
                if u + 1 < NU3:
                    sampled(u + 1)
            eng.wait_ge(sem["o_ready"], count(st, "o_ready", i, NU3))
            for j in range(GT):
                for h in range(2):
                    last = eng.matmul(ps[:, 7, j * P:(j + 1) * P], OX[:, h, j * P:(j + 1) * P], wox3[:, h, :],
                                      start=(h == 0), stop=(h == 1))
            last.then_inc(sem["out_ps"], 1)

        def chunk_width(c):
            return SG * len(CHUNKS[c % 12][1])

        def a3_act(eng, i):
            st = "a3"
            turn_act(eng, st, i, 1, XT)
            eng.wait_ge(sem["q_ps"], count(st, "q_ps", i, 1))
            eng.activation(QT3, ps[:, 1, :], ACT.Identity, bias=bq3).then_inc(sem["q_ready"], 1)

            def gap(c):
                eng.wait_ge(sem["gap_ps"], count(st, "gap_ps", i, c + 1))
                if c >= 3:
                    made = "hat_ready" if c % 2 else "odd_hat_ready"
                    eng.wait_ge(sem[made], count(st, made, i, (c - 3) // 2 + 1))
                w = chunk_width(c)
                eng.activation(AB[:, c % 3, 0:w], ps[:, c % 3, 0:w], ACT.Abs, bias=const("negm"))\
                   .then_inc(sem["gap_ready"], 1)

            def hats(chunks):
                for c in chunks:
                    gap(c)
                for c in chunks:
                    if c % 2 == 0:
                        j, ks = CHUNKS[c % 12]
                        eng.wait_ge(sem["gap_ready"], count(st, "gap_ready", i, c + 1))
                        eng.activation(AH[:, (c // 12) % 2, j, ks[0]:ks[-1] + 1, :],
                                       AB[:, c % 3, 0:chunk_width(c)].rearrange("p (k c) -> p k c", k=len(ks)),
                                       ACT.Relu, bias=const("ones")[:, 0:1], scale=-1.0)\
                           .then_inc(sem["hat_ready"], 1)

            for c in range(0, AHEAD, 2):
                hats(range(c, min(c + 2, AHEAD)))
            for u in range(NU3):
                hats(with_unit(u)[:2])
                eng.wait_ge(sem["sm_in"], count(st, "sm_in", i, u + 1))
                eng.activation(EX[:, u % 2, :, :].rearrange("p k q -> p (k q)"), TT[:, u % 2, :, :].rearrange("p k q -> p (k q)"),
                               ACT.Exp).then_inc(sem["ex_ready"], 1)
                hats(with_unit(u)[2:])

        def a3_pool(eng, i):
            st = "a3"
            stage_ct(eng, st, i)
            norm_pool(eng, st, i, 1)
            def add_places(steps, r, of, to, signal):
                eng.tensor_tensor(PAIRS[:, r, :, :], of[:, r, 0:2, :], of[:, r, 2:4, :], ALU.add)\
                   .then_inc(sem["sum_step"], 1)
                eng.wait_ge(sem["sum_step"], count(st, "sum_step", i, steps + 1))
                eng.tensor_tensor(to[:, r, :], PAIRS[:, r, 0, :], PAIRS[:, r, 1, :], ALU.add).then_inc(sem["sum_step"], 1)
                eng.wait_ge(sem["sum_step"], count(st, "sum_step", i, steps + 2))
                eng.tensor_tensor(to[:, r, :], to[:, r, :], of[:, r, 4, :], ALU.add).then_inc(sem[signal], 1)

            for u in range(NU3):
                eng.wait_ge(sem["ex_ready"], count(st, "ex_ready", i, u + 1))
                add_places(4 * u, u % 2, EX, SMQ, "sum_ready")
                eng.wait_ge(sem["skv_read"], count(st, "skv_read", i, u + 1))
                add_places(4 * u + 2, u % 2, WW, UQ, "values_ready")

        def a3_dve(eng, link, i):
            st = "a3"
            link.start(st, i)
            norm_dve(eng, link, st, i, 1, group(xs, i), XH, "rows_ready")
            eng.wait_ge(sem["k_ps"], count(st, "k_ps", i, 1))
            for n, bias in ((0, bk3), (1, bv3)):
                if n == 1:
                    eng.wait_ge(sem["q_ps"], count(st, "q_ps", i, 1))
                    for h in range(2):
                        eng.tensor_scalar(QX[:, h, :], ps[:, 2 + h, :], bqx3[:, h:h + 1], HD ** -0.5, ALU.add, ALU.mult)
                    eng.wait_ge(sem["v_ps"], count(st, "v_ps", i, 1))
                last = eng.tensor_tensor(KVT, ps[:, 5:7, :].rearrange("p a (b c) -> p (a b) c", b=4),
                                         b3(bias, GB, 1), ALU.add)
                if n == 0:
                    last.then_inc(sem["k_read"], 1)
                    eng.wait_ge(sem["k_read"], count(st, "k_read", i, 1))
                else:
                    link(last)
                for b in range(GB):
                    last = eng.tensor_tensor(KV[:, b, :, 16 * n:16 * n + 16],
                                             KVT[:, b, :].rearrange("p (h c) -> p h c", h=8),
                                             const("headhalf").rearrange("p (h c) -> p h c", h=8), ALU.mult)
                if n == 0:
                    link(last)
            last.then_inc(sem["kv_ready"], 1)
            eng.wait_ge(sem["off_ps"], count(st, "off_ps", i, 1))

            def by_batch(ap):
                return ap.rearrange("p (b s) -> p b s", b=GB)

            def of_batch(ap):
                return b3(ap[:, bass.ds(i * GB, GB)], S, 2)

            v, q = by_batch(LT1), by_batch(LT2)
            link(eng.tensor_scalar(LT1, ps[0:KH, 4, :], boff3[0:KH, :], const("ref", KH), ALU.add, ALU.add))
            link(eng.tensor_tensor(LT1, LT1, const("loc", KH), ALU.add))
            link(eng.tensor_tensor(v, v, of_batch(SGN), ALU.mult))
            link(eng.tensor_tensor(q, v, of_batch(INV), ALU.mult))
            link(eng.tensor_scalar(LT2, LT2, 12582912.0, None, ALU.add))
            link(eng.tensor_scalar(LT2, LT2, 12582912.0, None, ALU.subtract))
            link(eng.tensor_tensor(q, q, of_batch(LEN), ALU.mult))
            link(eng.tensor_tensor(LT1, LT1, LT2, ALU.subtract))
            link(eng.tensor_scalar(LT2, LT1, 0.0, None, ALU.is_lt))
            link(eng.tensor_tensor(q, q, of_batch(LEN), ALU.mult))
            link(eng.tensor_tensor(LT1, LT1, LT2, ALU.add))
            link(eng.tensor_tensor(v, v, of_batch(SGN), ALU.mult))
            link(eng.tensor_scalar(LT1, LT1, 2.0 / (S - 1), 1.0, ALU.mult, ALU.subtract))
            link(eng.tensor_scalar(LT1, LT1, 1.0, float(S // 2), ALU.add, ALU.mult))
            link(eng.tensor_scalar(IXT, LT1, 0.5, None, ALU.subtract))
            link(eng.tensor_copy(PARTS[:, 0, :], IXT))
            link(eng.tensor_tensor(LT1, IXT, PARTS[:, 0, :], ALU.subtract))
            link(eng.tensor_copy(PARTS[:, 1, :], LT1))
            link(eng.tensor_tensor(PARTS[:, 2, :], LT1, PARTS[:, 1, :], ALU.subtract))
            for n in range(3):
                for part in range(3):
                    last = eng.tensor_copy(IXB[32 * part:32 * part + 32, n, :], PARTS[32 * n:32 * n + 32, part, :])
            last.then_inc(sem["ix_ready"], 1)

            def odd_hat(c):
                j, ks = CHUNKS[c % 12]
                eng.wait_ge(sem["gap_ready"], count(st, "gap_ready", i, c + 1))
                eng.tensor_scalar(AH[:, (c // 12) % 2, j, ks[0]:ks[-1] + 1, :],
                                  AB[:, c % 3, 0:chunk_width(c)].rearrange("p (k c) -> p k c", k=len(ks)), 1.0, 0.0,
                                  ALU.subtract, ALU.min).then_inc(sem["odd_hat_ready"], 1)

            def by_place(ap):
                return ap.rearrange("p k q -> p q k")

            def skv(u):
                return ps[:, SKV_BANK[u % 3], 0:NK * S].rearrange("p (k q) -> p k q", k=NK)

            def weigh(u):
                r = u % 2
                eng.wait_ge(sem["ex_ready"], count(st, "ex_ready", i, u + 1))
                eng.tensor_tensor(WW[:, r, :, :], EX[:, r, :, :], skv(u), ALU.mult).then_inc(sem["skv_read"], 1)

            def finish(u):
                _, sg, half, b = unit(u)
                r = u % 2
                at = sg * SG + b * S
                eng.wait_ge(sem["sum_ready"], count(st, "sum_ready", i, u + 1))
                link(eng.reciprocal(RQ[:, r, :], SMQ[:, r, :]))
                eng.wait_ge(sem["values_ready"], count(st, "values_ready", i, u + 1))
                eng.tensor_tensor(OX[:, half, at:at + S], UQ[:, r, :], RQ[:, r, :], ALU.mult).then_inc(sem["o_ready"], 1)

            for c in range(1, AHEAD, 2):
                odd_hat(c)
            for u in range(NU3):
                n, sg, half, b = unit(u)
                r = u % 2
                eng.wait_ge(sem["skv_ps"], count(st, "skv_ps", i, u + 1))
                at = sg * SG + b * S
                eng.tensor_tensor(PRD[:, r, :, :], skv(u), b3(QX[:, half, at:at + S], NK, 1), ALU.mult)\
                   .then_inc(sem["prod_ready"], 1)
                odd = [c for c in with_unit(u - 1) if c % 2]
                for c in odd[:1]:
                    odd_hat(c)
                if u >= 1:
                    weigh(u - 1)
                for c in odd[1:]:
                    odd_hat(c)
                if u >= 2:
                    finish(u - 2)
                eng.wait_ge(sem["score_ps"], count(st, "score_ps", i, u + 1))
                score = ps[:, 5 + r, 0:NK * S].rearrange("p (k q) -> p k q", k=NK)
                link(eng.tensor_reduce(MQ[:, r, :], by_place(score), X_AX, ALU.max))
                eng.tensor_tensor(TT[:, r, :, :], score, b3(MQ[:, r, :], NK, 1), ALU.subtract).then_inc(sem["sm_in"], 1)
            weigh(NU3 - 1)
            finish(NU3 - 2)
            finish(NU3 - 1)
            eng.wait_ge(sem["out_ps"], count(st, "out_ps", i, 1))
            link(eng.tensor_tensor(XH, quad(ps[:, 7, :]), b3(bo3, GT, 1), ALU.add))
            g = group(xs, i)
            eng.tensor_tensor(g, g, XH, ALU.add).then_inc(sem["x_ready"], 1)
            link.end()

        def row(a, n=P):
            return a.rearrange("(o n) -> o n", o=1).to_broadcast([n, a.shape[0]])

        def column(a):
            return a.rearrange("(p o) -> p o", o=1)

        def tok(a):
            return a.rearrange("b s d -> (b s) d").rearrange("(t p) d -> p t d", p=P)

        def hidden(a):
            return a.rearrange("(f p) d -> p f d", p=P)

        load_list = {
            "pre": [(con[:, :], t["constants"]), (xs[:, :, :], tok(t["x"])), (cs[:, :, :], tok(t["ctx_1024"])),
                    (m0i[:, :], t["mask_BxS2_ik0"]),
                    (m2i[:, :, :], tok(t["mask_BxSxS2_ik1"]))],
            "a0": [(wq0, t["L0_xattn_WQ"]), (wk0, t["L0_xattn_WK"]), (wv0, t["L0_xattn_WV"]), (wo0, t["L0_xattn_WO"]),
                   (g_ln, row(t["L0_ffn_ln_g"])), (b_ln, row(t["L0_ffn_ln_b"])), (wr0[:, 0:7], t["L0_ffn_Wr"])],
            "f0": [(W1[:, 0:7, :], t["L0_ffn_W1"].rearrange("e p f -> p e f")), (W1[:, 7, :], t["L0_ffn_W1s"]),
                   (W3[:, 0:7, :], t["L0_ffn_W3"].rearrange("e p f -> p e f")), (W3[:, 7, :], t["L0_ffn_W3s"])]
            + [(W2[:, e, :, :], hidden(t["L0_ffn_W2"][e, :, :])) for e in range(7)]
            + [(W2[:, 7, :, :], hidden(t["L0_ffn_W2s"]))],
            "a1": [(w1a, t["L1_xattn_w1"]), (w2a, hidden(t["L1_xattn_w2"])),
                   (b1a, t["L1_xattn_b1"]), (b2a, row(t["L1_xattn_b2"]))]
            + [(ga[n], row(t[f"L1_xattn_g{n + 1}"])) for n in range(3)]
            + [(ba[n], row(t[f"L1_xattn_beta{n + 1}"])) for n in range(3)]
            + [(wr1, t["L1_ffn_Wr"]), (br1, row(t["L1_ffn_br"]))],
            "a2": [(g2, row(t["L2_xattn_gamma"])), (be2, row(t["L2_xattn_beta"])), (wg2, t["L2_ffn_gate_wT"]),
                   (gb2, row(t["L2_ffn_gate_b"])), (b2f2[0:16, :], t["L2_ffn_be2"]),
                   (b2f2[16:17, :], row(t["L2_ffn_bs2"], 1))],
            "a3": [(wq3, t["L3_xattn_WqT"]), (wk3, t["L3_xattn_WkT"]), (wv3, t["L3_xattn_WvT"]),
                   (bk3, row(t["L3_xattn_bk"])), (bv3, row(t["L3_xattn_bv"])), (bo3, row(t["L3_xattn_bo"])),
                   (woff3[:, 0:H * NK], t["L3_xattn_WoffT"]), (boff3[0:H * NK, :], column(t["L3_xattn_boff"])),
                   (bq3, column(t["L3_xattn_bq"])), (wg3, t["L3_ffn_Wg"]), (bg3, row(t["L3_ffn_bg"]))]
            + [(wqx3[:, h, 32 * j:32 * j + 16], t["L3_xattn_WqT"][:, 16 * (4 * h + j):16 * (4 * h + j) + 16])
               for h in range(2) for j in range(4)]
            + [(bqx3[32 * j:32 * j + 16, h:h + 1], column(t["L3_xattn_bq"][16 * (4 * h + j):16 * (4 * h + j) + 16]))
               for h in range(2) for j in range(4)]
            + [(wox3[32 * j + 16:32 * j + 32, h, :], t["L3_xattn_WoT"][16 * (4 * h + j):16 * (4 * h + j) + 16, :])
               for h in range(2) for j in range(4)],
            "f2": [(U1[:, 0:1024].rearrange("p (e f) -> p e f", e=EG), t["L2_ffn_We1"].rearrange("e p f -> p e f")),
                   (U1[:, 1024:NU], t["L2_ffn_ws1"]),
                   (U3[:, 0:1024].rearrange("p (e f) -> p e f", e=EG), t["L2_ffn_We3"].rearrange("e p f -> p e f")),
                   (U3[:, 1024:NU], t["L2_ffn_ws3"]),
                   (U2[:, 0:8, :], hidden(t["L2_ffn_We2"].rearrange("e f d -> (e f) d"))),
                   (U2[:, 8, :], t["L2_ffn_ws2"]),
                   (UB1[:, 0:1024], row(t["L2_ffn_be1"].rearrange("e f -> (e f)"))), (UB1[:, 1024:NU], row(t["L2_ffn_bs1"])),
                   (UB3[:, 0:1024], row(t["L2_ffn_be3"].rearrange("e f -> (e f)"))), (UB3[:, 1024:NU], row(t["L2_ffn_bs3"])),
                   (M3, t["mask_BxS2_if0"].rearrange("(o b) s -> o b s", o=1).to_broadcast([KH, B, S])),
                   (windows, t["windows"])],
        }
        for n, layer in (("f1", "L1"), ("f3", "L3")):
            load_list[n] = [(V1, t[layer + "_ffn_W1"].rearrange("e p f -> p e f"))]\
                + [(V2[:, e, :, :], hidden(t[layer + "_ffn_W2"][e, :, :])) for e in range(E)]\
                + [(VB1[:, e, :], row(t[layer + "_ffn_b1"][e, :])) for e in range(E)]\
                + [(b2r[:, e, :], row(t[layer + "_ffn_b2"][e, :])) for e in range(E)]

        block = ctx.enter_context(nc.Block())

        @block.sync
        def _(eng):
            def load(name):
                for dst, src in load_list[name]:
                    eng.dma_start(dst, src).then_inc(loads[name], 16)

            def blocks(st, programs):
                with eng.Fori(0, LOOPS[st]) as i:
                    programs[4](eng, i)

            load("pre")
            load("a0")
            eng.wait_ge(s_zeros, 1)
            for rows in (xe, ye):
                eng.dma_start(rows.rearrange("(n p) d -> p n d", p=P),
                              wb[:, 0:ROWS].rearrange("p (n d) -> p n d", d=D)).then_inc(s_zero, 16)
            load("f0")
            load("a1")
            eng.wait_ge(s_zero, 16 * 2)
            load("f1")
            eng.wait_ge(sem["ht_ready"], total("r0", "ht_ready"))
            eng.wait_ge(sem["slot_ready"], total("g0", "slot_ready"))
            blocks("s0", s0)
            eng.wait_ge(s_sent, 16 * 2 * NT)
            blocks("f0", f0)
            eng.wait_ge(sem["y_read"], total("f0", "y_read"))
            load("f2")
            eng.wait_ge(s_sent, 16 * 2 * NT * 2)
            blocks("f1", f1)
            eng.wait_ge(s_init, 1)
            load("a2")
            load("a3")
            eng.wait_ge(sem["y_read"], total("f1", "y_read"))
            load("f3")
            eng.wait_ge(s_sent, 16 * 2 * NT * 3)
            blocks("f3", f3)
            eng.wait_ge(sem["x_ready"], total("c3", "x_ready"))
            eng.dma_start(tok(out), xs[:, :, :]).then_inc(s_out, 16)
            for name in loads:
                eng.wait_ge(loads[name], 16 * len(load_list[name]))
            eng.wait_ge(s_out, 16)

        needs = {"pre": ["pre"], "a0": ["a0"], "s0": ["f0"], "a1": ["a1"], "f1": ["f1"], "a2": ["a2"], "f2": ["f2"],
                 "a3": ["a3"], "f3": ["f3"], "m3": ["f2"]}

        @block.tensor
        def _(eng):
            for n, value in EARLY.items():
                eng.sem_inc(sem[n], value)
            turns = {"a0": a0_pe, "a1": a1_pe, "a2": a2_pe, "a3": a3_pe, "s0": s0[0], "f0": f0[0], "f1": f1[0], "f2": f2[0],
                     "f3": f3[0], "r0": lambda eng, i: logits_pe(eng, "r0", i, wr0[:, 0:7], 7),
                     "r1": lambda eng, i: logits_pe(eng, "r1", i, wr1, 8),
                     "r2": lambda eng, i: logits_pe(eng, "r2", i, wg2, EG),
                     "r3": lambda eng, i: logits_pe(eng, "r3", i, wg3, E), "b1": b1_pe}
            for st in ORDER:
                wait_loads(eng, *needs.get(st, []))
                if st in ("s0", "f0", "f1", "f3"):
                    eng.wait_ge(sem["slot_ready"], total("g" + st[1], "slot_ready"))
                if st == "pre":
                    for g in range(NG):
                        if g >= 1:
                            eng.wait_ge(sem["cols_ready"], count(st, "cols_ready", g, 0))
                        for j in range(GT):
                            last = eng.transpose(ps[:, 0, j * P:(j + 1) * P], cs[:, g * GT + j, :], ident)
                        last.then_inc(sem["turned"], 1)
                elif st in turns:
                    with eng.Fori(0, LOOPS[st]) as i:
                        turns[st](eng, i)
                elif st in ("g0", "g3"):
                    cum_pe(eng, st, 1, A3)
                elif st == "g1":
                    cum_pe(eng, st, 1, T2[:, 0:256])
                    cum_pe(eng, st, 2, T3[:, 256:384])

        @block.scalar
        def _(eng):
            turns = {"a0": a0_act, "a1": a1_act, "a2": a2_act, "a3": a3_act, "s0": s0[1], "f0": f0[1], "f1": f1[1], "f2": f2[1],
                     "f3": f3[1], "r0": lambda eng, i: logits_act(eng, "r0", i, False, 7),
                     "r1": lambda eng, i: logits_act(eng, "r1", i, True, 8),
                     "r2": lambda eng, i: logits_act(eng, "r2", i, True, EG),
                     "r3": lambda eng, i: logits_act(eng, "r3", i, False, E)}
            for st in ORDER:
                wait_loads(eng, *needs.get(st, []))
                if st == "pre":
                    for g in range(NG):
                        turn_act(eng, st, g, 1, cT[:, g * GW:(g + 1) * GW])
                elif st in turns:
                    with eng.Fori(0, LOOPS[st]) as i:
                        turns[st](eng, i)
                elif st in ("g0", "g3"):
                    exp_gate(eng, st)

        @block.gpsimd
        def _(eng):
            def a(st, norms, ct=False):
                def f(eng, i):
                    if ct:
                        stage_ct(eng, st, i)
                    for k in range(norms):
                        norm_pool(eng, st, i, k + 1)
                return f

            def sides(st, norms, then=None):
                def f(eng, i):
                    for k in range(norms):
                        for q in SIDES:
                            norm_side_pool(eng, st, i, k + 1, q)
                    if then:
                        then(eng, st, i)
                return f

            turns = {"a0": a("a0", 1, True), "a3": a3_pool,
                     "f0": f0[3], "f1": f1[3], "f2": f2[3], "f3": f3[3],
                     "r0": sides("r0", 2, rows_pool), "r1": sides("r1", 1, rows_pool),
                     "r2": sides("r2", 1, logits_pool), "r3": sides("r3", 1, rows_pool)}
            for st in ORDER:
                wait_loads(eng, *needs.get(st, []))
                if st == "a0":
                    eng.wait_ge(sem["cols_ready"], total("pre", "cols_ready"))
                if st == "a3":
                    eng.wait_ge(sem["x_ready"], count("a3", "x_ready"))
                if st == "f2":
                    eng.wait_ge(sem["ht_ready"], total("r2", "ht_ready"))
                    eng.wait_ge(sem["c_ready"], total("g2", "c_ready"))
                if st in ("f0", "f1", "f3"):
                    dispatch_pool(eng, st[1])
                if st in ("a1", "a2"):
                    gather_turns_pool(eng, st, int(st[1]) - 1, {"a1": 4, "a2": 2}[st])
                if st in turns:
                    with eng.Fori(0, LOOPS[st]) as i:
                        turns[st](eng, i)
                if st == "f3":
                    gather_pool(eng)

        @block.vector
        def _(eng):
            link = Chain(eng)
            eng.memset(wb[:, 0:ROWS], 0.0).then_inc(s_zeros, 1)

            def router(st, norms, n, **kw):
                def f(eng, link, i):
                    link.start(st, i)
                    eng.wait_ge(sem["ht_ready"], count(st, "ht_ready", i))
                    for q in SIDES:
                        norm_in(eng, link, q, of_side(xs, i, q))
                    if norms == 1:
                        for q in SIDES:
                            norm_out(eng, st, i, 1, q, of_side(xs, i, q), XH_[q]).then_inc(sem["rows_ready"], 1)
                    else:
                        for q in SIDES:
                            link(norm_out(eng, st, i, 1, q, of_side(xs, i, q), XH_[q]))
                            norm_in(eng, link, q, XH_[q])
                        for q in SIDES:
                            link(norm_out(eng, st, i, 2, q, XH_[q], XH_[q]))
                            link(eng.tensor_tensor(XH_[q], XH_[q], b3(g_ln, GT, 1), ALU.mult))
                            eng.tensor_tensor(XH_[q], XH_[q], b3(b_ln, GT, 1), ALU.add).then_inc(sem["rows_ready"], 1)
                    logits_dve(eng, link, st, i, n, **kw)
                    link.end()
                return f

            turns = {"a0": a0_dve, "a1": a1_dve, "a2": a2_dve, "a3": a3_dve, "s0": s0[2], "f0": f0[2], "f1": f1[2], "f2": f2[2],
                     "f3": f3[2], "b1": b1_dve, "r0": router("r0", 2, 7), "r1": router("r1", 1, E, bias=br1, softmax=True),
                     "r2": router("r2", 1, EG, softmax=True),
                     "r3": router("r3", 1, E, bias=bg3, scale=1.0 / (1.0 + 1e-6))}
            once = {"g0": g0_dve, "t1": t1_dve, "g1": g1_dve, "g2": g2_dve, "g3": g3_dve, "m3": m3_dve}
            for st in ORDER:
                if st == "f1":
                    eng.wait_ge(sem["lg_ps"], total("r1", "lg_ps"))
                    eng.memset(wsm[:, :], 0.0).then_inc(s_init, 1)
                wait_loads(eng, *needs.get(st, []))
                if st[0] in "ar" and st != "a0":
                    eng.wait_ge(sem["x_ready"], count(st, "x_ready"))
                if st == "a0":
                    link.start("a0", 0)
                    eng.tensor_scalar(qkeep[:, :], m0i[:, :], 0.0, None, ALU.is_equal).then_inc(s_keep, 1)
                    eng.wait_ge(s_keep, 1)
                if st == "r0":
                    eng.memset(lg[:, :, 7:8], NEG)
                if st in ("s0", "f0", "f1", "f3"):
                    eng.wait_ge(sem["slot_ready"], total("g" + st[1], "slot_ready"))
                if st == "c3":
                    combine_dve(eng, link)
                if st == "f2":
                    eng.wait_ge(sem["c_ready"], total("g2", "c_ready"))
                if st in turns:
                    with eng.Fori(0, LOOPS[st]) as i:
                        turns[st](eng, link, i)
                elif st in once:
                    once[st](eng, link)


TURNED = {"L2_ffn_gate_w": "L2_ffn_gate_wT", "L3_xattn_Wq": "L3_xattn_WqT", "L3_xattn_Wk": "L3_xattn_WkT",
          "L3_xattn_Wv": "L3_xattn_WvT", "L3_xattn_Wo": "L3_xattn_WoT", "L3_xattn_Woff": "L3_xattn_WoffT"}


def kernel(**inputs):
    import concourse.bacc as bacc
    from concourse.bass_utils import run_bass_kernel_spmd

    nc = bacc.Bacc("TRN2", target_bir_lowering=False, num_devices=1)
    laid = {}
    for name, a in inputs.items():
        a = np.asarray(a)
        if name in ("mask_BxS2_ik0", "L1_xattn_b1"):
            a = a.reshape(-1, P).T
        if name in ("L3_xattn_Woff", "L3_xattn_boff"):
            a = a.reshape(H, NK, -1).transpose(1, 0, 2).reshape(a.shape)
        laid[TURNED.get(name, name)] = np.ascontiguousarray(a.T if name in TURNED else a)
    laid["constants"] = constants()
    laid["windows"] = (np.arange(2048)[None, :] // S == np.arange(96)[:, None] % 32).astype(np.float32)
    arrays, t = {}, {}
    for name, a in laid.items():
        arrays[f"in_{name}"] = a
        t[name] = nc.dram_tensor(f"in_{name}", a.shape, mybir.dt.from_np(a.dtype), kind="ExternalInput").ap()
    out = nc.dram_tensor("out_x", (B, S, D), F32, kind="ExternalOutput").ap()
    build(nc, t, out)
    r = run_bass_kernel_spmd(nc, [arrays], core_ids=[0])
    return r.results[0]["out_x"]
```

```python
from contextlib import ExitStack

import concourse.bass as bass
from concourse import mybir
import numpy as np

F32 = mybir.dt.float32
I32 = mybir.dt.int32
BF16 = mybir.dt.bfloat16
U32 = mybir.dt.uint32
ALU = mybir.AluOpType
ACT = mybir.ActivationFunctionType
X_AX = mybir.AxisListType.X

P = 128
B, S, D = 32, 64, 128
NT = B * S // P
GT = 4
NG = NT // GT
GW = GT * P
GB = GW // S
H = 16
HD = D // H
NK = 5
F = 512
FB = F // P
E = 8
EG, EI = 16, 64
CAP0 = -(-125 * 2 * 1024 // (100 * 7))
CAP1 = -(-12 * B * S // (10 * 8))
NEG = -1.0e30
SLOTS = 384
KB_ = 8
PLACES = {"s0": (1, 8), "f0": (2, 5), "f1": (2, 8), "f3": (4, 8)}
ROWS = 40 * 128

CONST = {}
_at = 0
for _name, _w in (("ident", P), ("causal", S), ("headpair", P), ("headquad", 4), ("neghalf", 1), ("ref", 1),
                  ("ones", P), ("upto", P), ("causal2", P), ("same2", P), ("headhalf", P), ("spread", P), ("negm", 1),
                  ("iota", 16), ("loc", GW), ("bits", 45), ("place", 8), ("blocks", 40), ("experts", 24)):
    CONST[_name] = (_at, _w)
    _at += _w
NCONST = _at
NFIRST = CONST["ones"][0]


def constants():
    t = np.zeros((P, NCONST), np.float32)

    def put(name, a):
        t[:, CONST[name][0]:CONST[name][0] + CONST[name][1]] = a

    p, c = np.arange(P)[:, None], np.arange(P)[None, :]
    same = p // S == c // S
    put("ident", p == c)
    put("ones", np.ones((P, P)))
    put("upto", p <= c)
    put("causal2", np.where(same & (c <= p), 0.0, NEG))
    put("same2", np.where(same, 0.0, NEG))
    put("causal", np.where(np.arange(S)[None, :] > p % S, -1.0e9, 0.0))
    put("headpair", (c // HD) % 2 == p // S)
    put("headhalf", ((c // HD) % 2 == p // S) * np.where((c // HD) % 8 >= 4, -0.5, 0.5))
    put("headquad", (p // HD) % 4 == np.arange(4)[None, :])
    put("spread", (c // HD == p // HD + 2) & ((c // HD) % 4 >= 2))
    put("negm", -(p % S))
    put("iota", np.arange(16)[None, :])
    put("neghalf", np.full((P, 1), -0.5))
    put("ref", p // H - 3.0)
    put("loc", np.arange(GW)[None, :] % S)
    put("place", np.arange(8)[None, :] * SLOTS - 1.0)
    put("blocks", np.arange(40)[None, :])
    put("experts", np.arange(24)[None, :] // (SLOTS // P))
    bits = 4 ** np.arange(14, -1, -1, dtype=np.int32)[:, None] * np.arange(1, 4, dtype=np.int32)[None, :]
    put("bits", bits.reshape(1, 45).view(np.float32))
    return t


_NORM = dict(var_ready=1, rstd_ready=1)
_TURN = dict(rows_ready=1, turned=1, cols_ready=1)
_SOFT = dict(sc_ps=1, sm_in=1, ex_ready=1, pt_ps=1, pt_ready=1, av_ps=1)


def _times(n, d):
    return {k: v * n for k, v in d.items()}


def _blocks(st, n, deep):
    names = ["xt_ps", "xt_ready", "h_ps", "act_in" if deep else "act_ready", "mid_ready", "mid_ps", "midT_ready", "y_ps",
             "y_read"] + (["ys_free"] if st != "s0" else [])
    rises = {name: n for name in names}
    for k in range(n):
        rises[f"xe{k}"] = 16
        if st != "s0":
            rises[f"ys{k}"] = 16
    return rises


PLAN = [
    ("pre", NG, dict(turned=1, cols_ready=1)),
    ("a0", NG, dict(**_NORM, **_times(2, _TURN), ct_staged=1, k_ps=1, q_ps=1, q_ready=1, kb_ready=1, v_ps=1, vb_ready=1,
                    **_times(GT, _SOFT), sc_read=GT, out_ps=1, x_ready=1, dve=18)),
    ("r0", NG // 2, dict(**_times(2, dict(**_times(2, _NORM), **_TURN, ht_ready=1, lg_ps=1, lg_ready=1)), dve=14)),
    ("g0", 1, dict(exp_in=1, exp_ready=1, cum_in=1, cum_ps=1, slot_ready=1, dve=25)),
    ("s0", PLACES["s0"][0], _blocks("s0", KB_, False)),
    ("s0_last", 1, _blocks("s0", PLACES["s0"][1], False)),
    ("f0", PLACES["f0"][0], _blocks("f0", KB_, False)),
    ("f0_last", 1, _blocks("f0", PLACES["f0"][1], False)),
    ("a1", NG // 2, dict(**_times(2, dict(gathered=1, combined=1, **_times(4, _NORM), **_times(3, _TURN), **_times(2, _SOFT),
                                         h_ps=1, mid_ready=1, y_ps=1, x_ready=1)), dve=56)),
    ("r1", NG // 2, dict(**_times(2, dict(**_NORM, **_TURN, ht_ready=1, lg_ps=1, exp_in=1, exp_ready=1,
                                         lg_ready=1)), dve=12)),
    ("t1", 1, dict(dve=7)),
    ("b1", 15, dict(cum_in=1, cum_ps=1, dve=6)),
    ("g1", 1, dict(cum_in=2, cum_ps=2, slot_ready=1, dve=29)),
    ("f1", PLACES["f1"][0], _blocks("f1", KB_, True)),
    ("f1_last", 1, _blocks("f1", PLACES["f1"][1], True)),
    ("a2", NG // 2, dict(**_times(2, dict(gathered=1, combined=1, **_times(2, _NORM), **_TURN, **_SOFT,
                                         x_ready=1)), dve=36)),
    ("r2", NG // 2, dict(**_times(2, dict(**_NORM, **_TURN, ht_ready=1, lg_ps=1, exp_in=1, exp_ready=1,
                                         lg_ready=1)), dve=10)),
    ("g2", 1, dict(c_ready=1, dve=17)),
    ("f2", NG, dict(h_staged=1, c_in=1, c_turned=1, cT_ready=1, h_ps=12, act_in=12, act_ready=12, mid_ready=12,
                    mid_ps=12, midT_ready=12, y_ps=GT, x_ready=GT, dve=24)),
    ("m3", 1, dict(dve=7)),
    ("a3", NG, dict(**_NORM, **_TURN, ct_staged=1, q_ps=1, qx_ps=1, qx_read=1, q_ready=1, off_ps=1, ix_ready=1,
                    k_ps=1, k_read=1, v_ps=1, kv_ready=1, gap_ps=48, gap_ready=48, hat_ready=24, odd_hat_ready=24,
                    skv_ps=16, prod_ready=16, score_ps=16, sm_in=16, ex_ready=16, skv_read=16, sum_step=64,
                    sum_ready=16, values_ready=16, o_ready=16, out_ps=1, x_ready=1, dve=56)),
    ("r3", NG // 2, dict(**_times(2, dict(**_NORM, **_TURN, ht_ready=1, lg_ps=1, lg_ready=1)), dve=6)),
    ("g3", 1, dict(exp_in=1, exp_ready=1, cum_in=1, cum_ps=1, slot_ready=1, dve=31)),
    ("f3", PLACES["f3"][0], _blocks("f3", KB_, True)),
    ("f3_last", 1, _blocks("f3", PLACES["f3"][1], True)),
    ("c3", 1, dict(x_ready=NG, dve=4)),
]
EARLY = {"ht_ready": 1, "v_ps": 1, "y_ps": 1, "c_turned": 1, "y_read": 1, "xt_ps": KB_, "xt_ready": 1, "ys_free": KB_}
SIGNALS = sorted({name for _, _, rises in PLAN for name in rises})
ORDER = [stage for stage, _, _ in PLAN]
LOOPS = {stage: turns for stage, turns, _ in PLAN}


def count(stage, name, turn=0, k=0):
    base = EARLY.get(name, 0)
    for s, turns, rises in PLAN:
        if s == stage:
            return turn * rises.get(name, 0) + (base + k)
        base += turns * rises.get(name, 0)


def total(stage, name):
    turns, rises = {s: (t, r) for s, t, r in PLAN}[stage]
    return count(stage, name, turns)


def build(nc, t, out):
    with ExitStack() as ctx:
        def sb(name, shape, dt=F32):
            return ctx.enter_context(nc.sbuf_tensor(name, shape, dt))

        ps = ctx.enter_context(nc.psum_tensor("ps", [P, 8, 512], F32))
        sem = {n: ctx.enter_context(nc.semaphore(n)) for n in SIGNALS}
        loads = {n: ctx.enter_context(nc.semaphore("load_" + n)) for n in
                 ("pre", "a0", "r0", "f0", "a1", "f1", "a2", "f2", "a3", "f3")}
        s_zero, s_sent = [ctx.enter_context(nc.semaphore(n)) for n in ("s_zero", "s_sent")]
        s_back = [ctx.enter_context(nc.semaphore(f"s_back{g}")) for g in range(NG)]
        s_zeros = ctx.enter_context(nc.semaphore("s_zeros"))
        s_out = ctx.enter_context(nc.semaphore("s_out"))
        s_keep = ctx.enter_context(nc.semaphore("s_keep"))
        s_init = ctx.enter_context(nc.semaphore("s_init"))

        xs = sb("xs", [P, NT, D])
        cs = sb("cs", [P, NT, D])
        cT = sb("cT", [P, B * S])
        hT = sb("hT", [P, B * S])
        hr = hT[:, :].rearrange("p (t d) -> p t d", t=NT)
        con = sb("con", [P, NCONST])
        wa = sb("wa", [P, 8 * 1536])
        wb = sb("wb", [P, 8 * 1024 + 8 * 512])
        wsm = sb("wsm", [P, 3200])
        work = sb("work", [P, 11500])
        m0i = sb("m0i", [P, NT], I32)
        m2i = sb("m2i", [P, NT, S], I32)
        qkeep = sb("qkeep", [P, NT])
        slack = sb("slack", [P, 28])
        lg = sb("lg", [P, NT, 16])
        slots = sb("slots", [P, 2, 2 * NT], U32)
        gate = sb("gate", [P, 2, NT])
        etab = sb("etab", [P, 3, 40], I32)
        b2r = sb("b2r", [P, E, D])
        xe = nc.dram_tensor("xe", [ROWS, D], F32, kind="Internal").ap()
        ye = nc.dram_tensor("ye", [ROWS, D], F32, kind="Internal").ap()
        comb = sb("comb", [P, NT, 18])
        ident, ones = [con[:, CONST[n][0]:CONST[n][0] + P] for n in ("ident", "ones")]

        def const(name, rows=P):
            a, w = CONST[name]
            return con[0:rows, a:a + w]

        place = {"wsm": 0}

        def small(name, w, rows=P):
            a = place["wsm"]
            place["wsm"] += w
            return wsm[0:rows, a:a + w]

        wq0, wk0, wv0, wo0 = [small(n, P) for n in ("wq", "wk", "wv", "wo")]
        g_ln, b_ln = small("g", D), small("b", D)
        wr0 = small("wr0", 8)
        w1a = small("w1a", F)
        w2a = small("w2a", F).rearrange("p (f d) -> p f d", f=FB)
        b1a = small("b1a", FB)
        b2a = small("b2a", D)
        ga = [small(f"g{n}", D) for n in range(3)]
        ba = [small(f"b{n}", D) for n in range(3)]
        wr1, br1 = small("wr1", E), small("br1", E)
        end1 = place["wsm"]
        place["wsm"] = 0
        g2, be2 = small("g2", D), small("be2", D)
        wg2, gb2 = small("wg2", EG), small("gb2", EG)
        b2f2 = small("b2f2", D, 18)
        wq3, wk3, wv3 = [small(n, P) for n in ("wq3", "wk3", "wv3")]
        bk3, bv3, bo3 = [small(n, P) for n in ("bk3", "bv3", "bo3")]
        woff3 = small("woff3", 96)
        boff3, bq3, bqx3 = small("boff3", 1), small("bq3", 1), small("bqx3", 2)
        wqx3 = small("wqx3", 2 * P).rearrange("p (h c) -> p h c", h=2)
        wox3 = small("wox3", 2 * P).rearrange("p (h c) -> p h c", h=2)
        wg3, bg3 = small("wg3", E), small("bg3", E)
        assert max(end1, place["wsm"]) <= 3200, (end1, place["wsm"])

        W1 = wa[:, 0:8 * F].rearrange("p (e f) -> p e f", e=E)
        W3 = wa[:, 8 * F:16 * F].rearrange("p (e f) -> p e f", e=E)
        W2 = wa[:, 16 * F:24 * F].rearrange("p (e f d) -> p e f d", e=E, f=FB)
        V1 = wb[:, 0:8 * F].rearrange("p (e f) -> p e f", e=E)
        V2 = wb[:, 8 * F:16 * F].rearrange("p (e f d) -> p e f d", e=E, f=FB)
        VB1 = wb[:, 16 * F:24 * F].rearrange("p (e f) -> p e f", e=E)
        NU = 18 * EI
        U1, U3 = wa[:, 0:NU], wa[:, NU:2 * NU]
        U2 = wa[:, 2 * NU:3 * NU].rearrange("p (f d) -> p f d", f=9)
        UB1, UB3 = wa[:, 3 * NU:4 * NU], wa[:, 4 * NU:5 * NU]

        def carve(start, *shape):
            n = int(np.prod(shape))
            ap = work[:, start:start + n]
            if len(shape) == 2:
                ap = ap.rearrange("p (a b) -> p a b", a=shape[0])
            if len(shape) == 3:
                ap = ap.rearrange("p (a b c) -> p a b c", a=shape[0], b=shape[1])
            return ap

        stats, mv = carve(0, GT, 6), carve(24, GT, 2)
        var, rstd = carve(32, GT), carve(36, GT)
        mx, sm, rs = carve(40, 4 * H), carve(104, 4 * H), carve(168, 4 * H)
        XH, XT = carve(232, GT, D), carve(744, GW)
        N0 = 1256
        SIDES = (0, 1)

        def part(side, n, width=1):
            a = 232 + 5120 * side + 512 * n
            return work[:, a:a + 512 * width]

        def tiles(ap):
            return ap.rearrange("p (t d) -> p t d", d=P)

        stats_, mv_ = [stats, carve(11400, GT, 6)], [mv, carve(11424, GT, 2)]
        var_, rstd_ = [var, carve(11432, GT)], [rstd, carve(11436, GT)]
        XH_, XT_, R_, Y2_ = [[tiles(part(q, n)) if n != 1 else part(q, n) for q in SIDES] for n in range(4)]
        Y1_, SC_ = [[tiles(part(q, n)) for q in SIDES] for n in (4, 5)]
        PTT_, MA_ = [part(q, 6) for q in SIDES], [tiles(part(q, 7)) for q in SIDES]
        HID_ = [part(q, 4, 4).rearrange("p (f c) -> p f c", f=FB) for q in SIDES]
        MF_ = Y2_

        def nth(k, side):
            return 2 * (k - 1) + side + 1

        def of_side(ap, i, side):
            return ap[:, bass.ds(i * 2 * GT + side * GT, GT)]

        class Chain:

            def __init__(self, eng):
                self.eng = eng

            def start(self, stage, turn):
                self.stage, self.turn, self.k = stage, turn, 0

            def __call__(self, ins):
                self.k += 1
                ins.then_inc(sem["dve"], 1)
                self.eng.wait_ge(sem["dve"], count(self.stage, "dve", self.turn, self.k))

            def end(self):
                plan = {s: r.get("dve", 0) for s, _, r in PLAN}[self.stage]
                assert plan == self.k, (self.stage, self.k)

        def group(ap, i):
            return ap[:, bass.ds(i * GT, GT)]

        def cols(ap, i, w=GW):
            return ap[:, bass.ds(i * w, w)]

        def norm_dve(eng, link, stage, i, k, src, dst, signal=None):
            for j in range(GT):
                last = eng.bn_stats(stats[:, j, :], src[:, j, :])
            link(last)
            eng.memset(slack[:, 0:1], 0.0)
            for j in range(GT):
                last = eng.bn_aggr(mv[:, j, :], stats[:, j, :])
            link(last)
            eng.tensor_scalar(var, mv[:, :, 1], 1.0e-5, None, ALU.add).then_inc(sem["var_ready"], 1)
            eng.wait_ge(sem["rstd_ready"], count(stage, "rstd_ready", i, k))
            for j in range(GT):
                last = eng.tensor_scalar(dst[:, j, :], src[:, j, :], mv[:, j, 0:1], rstd[:, j:j + 1],
                                         ALU.subtract, ALU.mult)
            if signal is None:
                link(last)
            else:
                last.then_inc(sem[signal], 1)

        def norm_in(eng, link, side, src):
            for j in range(GT):
                last = eng.bn_stats(stats_[side][:, j, :], src[:, j, :])
            link(last)
            eng.memset(slack[:, 0:1], 0.0)
            for j in range(GT):
                last = eng.bn_aggr(mv_[side][:, j, :], stats_[side][:, j, :])
            link(last)
            eng.tensor_scalar(var_[side], mv_[side][:, :, 1], 1.0e-5, None, ALU.add).then_inc(sem["var_ready"], 1)

        def norm_out(eng, stage, i, k, side, src, dst):
            eng.wait_ge(sem["rstd_ready"], count(stage, "rstd_ready", i, nth(k, side)))
            for j in range(GT):
                last = eng.tensor_scalar(dst[:, j, :], src[:, j, :], mv_[side][:, j, 0:1], rstd_[side][:, j:j + 1],
                                         ALU.subtract, ALU.mult)
            return last

        def norm_side_pool(eng, stage, i, k, side):
            eng.wait_ge(sem["var_ready"], count(stage, "var_ready", i, nth(k, side)))
            eng.tensor_tensor(rstd_[side], var_[side], const("neghalf").to_broadcast([P, GT]), ALU.pow)\
               .then_inc(sem["rstd_ready"], 1)

        def turn_side_pe(eng, stage, i, k, side, src):
            eng.wait_ge(sem["rows_ready"], count(stage, "rows_ready", i, nth(k, side)))
            for j in range(GT):
                last = eng.transpose(ps[:, 4 * side, j * P:(j + 1) * P], src[:, j, :], ident)
            last.then_inc(sem["turned"], 1)

        def turn_side_act(eng, stage, i, k, side):
            eng.wait_ge(sem["turned"], count(stage, "turned", i, nth(k, side)))
            eng.activation(XT_[side], ps[:, 4 * side, :], ACT.Copy).then_inc(sem["cols_ready"], 1)

        def warm(eng, function):
            eng.activation(slack[:, 27:28], const("neghalf"), function)

        def norm_pool(eng, stage, i, k):
            eng.wait_ge(sem["var_ready"], count(stage, "var_ready", i, k))
            eng.tensor_tensor(rstd, var, const("neghalf").to_broadcast([P, GT]), ALU.pow)\
               .then_inc(sem["rstd_ready"], 1)

        def turn_pe(eng, stage, i, k, src, bank=0):
            eng.wait_ge(sem["rows_ready"], count(stage, "rows_ready", i, k))
            for j in range(GT):
                last = eng.transpose(ps[:, bank, j * P:(j + 1) * P], src[:, j, :], ident)
            last.then_inc(sem["turned"], 1)

        def turn_act(eng, stage, i, k, dst, bank=0):
            eng.wait_ge(sem["turned"], count(stage, "turned", i, k))
            eng.activation(dst, ps[:, bank, :], ACT.Copy).then_inc(sem["cols_ready"], 1)

        def wait_loads(eng, *which):
            for n in which:
                eng.wait_ge(loads[n], 16 * len(load_list[n]))

        def heads(ap):
            return ap.rearrange("p (h d) -> p h d", h=H)

        def b3(ap, n, at):
            a = ap.shape[1]
            return ap.unsqueeze(at).to_broadcast([ap.shape[0], a, n] if at == 2 else [ap.shape[0], n, a])

        QT = carve(N0, GW)
        CTD = carve(N0 + 512, GB, 2 * S)
        KB = carve(N0 + 1536, GB, 4, S)
        VB = carve(N0 + 3584, GB, D)
        S0 = carve(N0 + 4608, 2, H * S)
        E0 = carve(N0 + 6656, 2, H * S)
        PT0 = [carve(N0 + 8704, 8, P), hr[:, 0:8, :]]
        OT = QT
        MT = lg[:, :, :].rearrange("p a b -> p (a b)")
        O0 = XH

        def dup(b):
            return CTD[:, b, :]

        def a0_pe(eng, i):
            st = "a0"
            eng.wait_ge(sem["x_ready"], count(st, "x_ready", i))
            eng.matmul(ps[:, 2, :], wk0, cols(cT, i), start=True, stop=True).then_inc(sem["k_ps"], 1)
            eng.wait_ge(sem["ct_staged"], count(st, "ct_staged", i, 1))
            for b in range(GB):
                last = eng.matmul(ps[:, 5 + b // 4, (b % 4) * P:(b % 4 + 1) * P], dup(b), wv0, start=True, stop=True)
            last.then_inc(sem["v_ps"], 1)
            turn_pe(eng, st, i, 1, XH)
            eng.wait_ge(sem["cols_ready"], count(st, "cols_ready", i, 1))
            eng.matmul(ps[:, 1, :], wq0, XT, start=True, stop=True).then_inc(sem["q_ps"], 1)

            def scores(j):
                if j == 0:
                    eng.wait_ge(sem["q_ready"], count(st, "q_ready", i, 1))
                    eng.wait_ge(sem["kb_ready"], count(st, "kb_ready", i, 1))
                    eng.wait_ge(sem["vb_ready"], count(st, "vb_ready", i, 1))
                else:
                    eng.wait_ge(sem["sc_read"], count(st, "sc_read", i, j))
                for b in range(2):
                    for q in range(4):
                        last = eng.matmul(ps[S * b:S * b + S, 1 + q, (j % 2) * 256:(j % 2) * 256 + 256],
                                          QT[32 * q:32 * q + 32, j * P + S * b:j * P + S * b + S],
                                          KB[32 * q:32 * q + 32, 2 * j + b, :, :],
                                          start=True, stop=True, tile_position=(32 * q, S * b))
                last.then_inc(sem["sc_ps"], 1)

            def weights(j):
                eng.wait_ge(sem["ex_ready"], count(st, "ex_ready", i, j + 1))
                if j >= 1:
                    eng.wait_ge(sem["pt_ready"], count(st, "pt_ready", i, j))
                for h in range(8):
                    last = eng.transpose(ps[:, 5 + h // 4, (h % 4) * P:(h % 4 + 1) * P],
                                         E0[:, j % 2, h * P:(h + 1) * P], ident)
                last.then_inc(sem["pt_ps"], 1)

            def values(j):
                eng.wait_ge(sem["pt_ready"], count(st, "pt_ready", i, j + 1))
                for b in range(2):
                    for h in range(8):
                        last = eng.matmul(ps[S * b:S * b + S, 7, j * P + 16 * h:j * P + 16 * h + 16],
                                          PT0[j % 2][:, h, S * b:S * b + S], VB[:, 2 * j + b, 16 * h:16 * h + 16],
                                          start=True, stop=True, tile_position=(0, S * b))
                last.then_inc(sem["av_ps"], 1)

            scores(0)
            scores(1)
            weights(0)
            for j in range(GT):
                if j + 2 < GT:
                    scores(j + 2)
                if j + 1 < GT:
                    weights(j + 1)
                values(j)
            turn_pe(eng, st, i, 2, O0)
            eng.wait_ge(sem["cols_ready"], count(st, "cols_ready", i, 2))
            for j in range(GT):
                last = eng.matmul(ps[:, 1, j * P:(j + 1) * P], OT[:, j * P:(j + 1) * P], wo0, start=True, stop=True)
            last.then_inc(sem["out_ps"], 1)

        def a0_act(eng, i):
            st = "a0"
            warm(eng, ACT.Exp)
            turn_act(eng, st, i, 1, XT)
            eng.wait_ge(sem["q_ps"], count(st, "q_ps", i, 1))
            eng.activation(QT, ps[:, 1, :], ACT.Copy).then_inc(sem["q_ready"], 1)

            def exp(j):
                eng.wait_ge(sem["sm_in"], count(st, "sm_in", i, j + 1))
                eng.activation(E0[:, j % 2, :], S0[:, j % 2, :], ACT.Exp, scale=HD ** -0.5)\
                   .then_inc(sem["ex_ready"], 1)

            exp(0)
            exp(1)
            for j in range(GT):
                eng.wait_ge(sem["pt_ps"], count(st, "pt_ps", i, j + 1))
                eng.activation(PT0[j % 2].rearrange("p a b -> p (a b)"), ps[:, 5:7, :].rearrange("p a b -> p (a b)"),
                               ACT.Copy).then_inc(sem["pt_ready"], 1)
                if j + 2 < GT:
                    exp(j + 2)
            turn_act(eng, st, i, 2, OT)

        def a0_dve(eng, link, i):
            st = "a0"
            link.start(st, i)
            norm_dve(eng, link, st, i, 1, group(xs, i), XH, "rows_ready")
            eng.wait_ge(sem["k_ps"], count(st, "k_ps", i, 1))
            last = None
            for b in range(GB):
                last = eng.tensor_tensor(KB[:, b, :, :], b3(ps[:, 2, b * S:(b + 1) * S], 4, 1),
                                         b3(const("headquad"), S, 2), ALU.mult)
            last.then_inc(sem["kb_ready"], 1)
            eng.wait_ge(sem["v_ps"], count(st, "v_ps", i, 1))
            last = eng.tensor_tensor(VB, ps[:, 5:7, :].rearrange("p a (b c) -> p (a b) c", b=4),
                                     b3(const("headpair"), GB, 1), ALU.mult)
            last.then_inc(sem["vb_ready"], 1)

            def before(j):
                sj, sh = S0[:, j % 2, :], heads(S0[:, j % 2, :])
                keep = qkeep[:, bass.ds(i * GT + j, 1)]
                link(eng.tensor_scalar(MT.rearrange("p (h s) -> p h s", s=S), b3(const("causal"), 4, 1), keep, None,
                                       ALU.mult))
                eng.wait_ge(sem["sc_ps"], count(st, "sc_ps", i, j + 1))
                half = (j % 2) * 4 * S
                eng.scalar_tensor_tensor(out=sj.rearrange("p (q c) -> p q c", q=4),
                                         in0=ps[:, 1:5, half:half + 4 * S], scalar=keep, in1=b3(MT, 4, 1),
                                         op0=ALU.mult, op1=ALU.add).then_inc(sem["sc_read"], 1)
                eng.wait_ge(sem["sc_read"], count(st, "sc_read", i, j + 1))
                m = mx[:, H * j:H * j + H]
                link(eng.tensor_reduce(m, sh, X_AX, ALU.max))
                eng.tensor_tensor(sh, sh, b3(m, S, 2), ALU.subtract).then_inc(sem["sm_in"], 1)

            before(0)
            before(1)
            for j in range(GT):
                eng.wait_ge(sem["ex_ready"], count(st, "ex_ready", i, j + 1))
                link(eng.reduce_sum(sm[:, H * j:H * j + H], heads(E0[:, j % 2, :]), X_AX))
                link(eng.reciprocal(rs[:, H * j:H * j + H], sm[:, H * j:H * j + H]))
                if j + 2 < GT:
                    before(j + 2)
            eng.wait_ge(sem["av_ps"], count(st, "av_ps", i, GT))
            for j in range(GT):
                last = eng.tensor_tensor(heads(O0[:, j, :]), heads(ps[:, 7, j * P:(j + 1) * P]),
                                         b3(rs[:, H * j:H * j + H], HD, 2), ALU.mult)
            last.then_inc(sem["rows_ready"], 1)
            eng.wait_ge(sem["out_ps"], count(st, "out_ps", i, 1))
            g = group(xs, i)
            eng.tensor_tensor(g, g, ps[:, 1, :].rearrange("p (a b) -> p a b", a=GT), ALU.add)\
               .then_inc(sem["x_ready"], 1)
            link.end()

        def bridge(eng, at=0):
            one = const("ref")
            return eng.tensor_tensor(slack[:, at + 1:at + 2], one, one, ALU.add)

        def stage_ct(eng, stage, i):
            eng.wait_ge(sem["v_ps"], count(stage, "v_ps", i, 0))
            bridge(eng)
            src = cols(cT, i).rearrange("p (b s) -> p b s", b=GB).unsqueeze(2).to_broadcast([P, GB, 2, S])
            eng.tensor_copy(CTD.rearrange("p b (r s) -> p b r s", r=2), src).then_inc(sem["ct_staged"], 1)

        def logits_pe(eng, st, i, w, n):
            for q in SIDES:
                turn_side_pe(eng, st, i, 1, q, XH_[q])
            for q in SIDES:
                eng.wait_ge(sem["cols_ready"], count(st, "cols_ready", i, nth(1, q)))
                for j in range(GT):
                    last = eng.matmul(ps[:, 4 * q + 1, j * n:(j + 1) * n], XT_[q][:, j * P:(j + 1) * P], w,
                                      start=True, stop=True)
                last.then_inc(sem["lg_ps"], 1)

        def logits_act(eng, st, i, softmax, n):
            if softmax:
                warm(eng, ACT.Exp)
            eng.wait_ge(sem["ht_ready"], count(st, "ht_ready", i, 0))
            for q in SIDES:
                turn_side_act(eng, st, i, 1, q)
            if softmax:
                for q in SIDES:
                    eng.wait_ge(sem["exp_in"], count(st, "exp_in", i, nth(1, q)))
                    eng.activation(R_[q].rearrange("p a b -> p (a b)")[:, 0:GT * n],
                                   R_[q].rearrange("p a b -> p (a b)")[:, 0:GT * n], ACT.Exp)\
                       .then_inc(sem["exp_ready"], 1)

        def rows_pool(eng, st, i):
            for q in SIDES:
                eng.wait_ge(sem["rows_ready"], count(st, "rows_ready", i, nth(1, q)))
                bridge(eng, (0, 17)[q])
                eng.tensor_copy(of_side(hr, i, q), XH_[q]).then_inc(sem["ht_ready"], 1)

        def logits_pool(eng, st, i):
            for q in SIDES:
                eng.wait_ge(sem["cols_ready"], count(st, "cols_ready", i, nth(1, q)))
                bridge(eng, (0, 17)[q])
                eng.tensor_copy(hT[:, bass.ds(i * 2 * GW + q * GW, GW)], XT_[q]).then_inc(sem["ht_ready"], 1)

        def logits_dve(eng, link, st, i, n, bias=None, scale=None, softmax=False):
            def logits(q):
                return R_[q].rearrange("p a b -> p (a b)")[:, 0:GT * n].rearrange("p (a b) -> p a b", a=GT)

            for q in SIDES:
                eng.wait_ge(sem["lg_ps"], count(st, "lg_ps", i, nth(1, q)))
                raw = ps[:, 4 * q + 1, 0:GT * n].rearrange("p (a b) -> p a b", a=GT)
                to = of_side(lg, i, q)[:, :, 0:n]
                ls = logits(q)
                if bias is None and not softmax:
                    eng.tensor_copy(to, raw).then_inc(sem["lg_ready"], 1)
                    continue
                if bias is not None:
                    link(eng.tensor_tensor(ls, raw, b3(bias, GT, 1), ALU.add))
                    raw = ls
                if not softmax:
                    eng.tensor_scalar(to, ls, scale, None, ALU.mult).then_inc(sem["lg_ready"], 1)
                    continue
                m = mx[:, GT * q:GT * q + GT]
                link(eng.tensor_reduce(m, raw, X_AX, ALU.max))
                eng.tensor_tensor(ls, raw, b3(m, n, 2), ALU.subtract).then_inc(sem["exp_in"], 1)
            if softmax:
                for q in SIDES:
                    total_, inverse = sm[:, GT * q:GT * q + GT], rs[:, GT * q:GT * q + GT]
                    eng.wait_ge(sem["exp_ready"], count(st, "exp_ready", i, nth(1, q)))
                    link(eng.reduce_sum(total_, logits(q), X_AX))
                    link(eng.reciprocal(inverse, total_))
                    eng.tensor_tensor(of_side(lg, i, q)[:, :, 0:n], logits(q), b3(inverse, n, 2), ALU.mult)\
                       .then_inc(sem["lg_ready"], 1)

        VL, IX = carve(N0, NT, 8), carve(N0 + 128, NT, 8).bitcast(U32)
        IXF = carve(N0 + 256, 2, NT)
        A2 = carve(N0 + 288, 2, NT * 16)
        GATE = carve(N0 + 800, 3, NT)
        T0, T1 = carve(N0 + 1000, 512), carve(N0 + 1512, 512)
        T2, T3 = carve(N0 + 2024, 512), carve(N0 + 2536, 512)
        CUR = carve(N0 + 3048, 8)
        CAND, CNT = carve(N0 + 3056, 8), carve(N0 + 3064, 8)
        CANDS, CNTS, SELS = carve(N0 + 3210, 3, 8), carve(N0 + 3240, 3, 8), carve(N0 + 3270, 24)
        GG = carve(N0 + 3080, NT, 8)

        def marks(n):
            return A2[:, :, 0:NT * n].rearrange("p k (t e) -> p k t e", t=NT)

        def top2(eng, link, src, n, wide):
            for q in range(NT):
                last = eng.max(VL[:, q, :], src[:, q, 0:wide])
            link(last)
            for q in range(NT):
                last = eng.max_index(IX[:, q, :], VL[:, q, :], src[:, q, 0:wide])
            link(last)
            link(eng.tensor_copy(IXF, IX[:, :, 0:2].rearrange("p t k -> p k t")))
            for k in range(2):
                last = eng.tensor_tensor(marks(n)[:, k], b3(const("iota")[:, 0:n], NT, 1), b3(IXF[:, k, :], n, 2),
                                         ALU.is_equal)
            return last

        def prefix(eng, link, a, b, n, w):
            step = 1
            while step < n:
                eng.tensor_copy(b[:, 0:step * w], a[:, 0:step * w])
                link(eng.tensor_tensor(b[:, step * w:n * w], a[:, step * w:n * w], a[:, 0:(n - step) * w], ALU.add))
                a, b = b, a
                step *= 2
            return a

        def exp_gate(eng, st):
            eng.wait_ge(sem["exp_in"], count(st, "exp_in", 0, 1))
            eng.activation(GATE[:, 2, :], GATE[:, 2, :], ACT.Exp).then_inc(sem["exp_ready"], 1)

        def tri(t3, n):
            return t3.rearrange("p (t e) -> p t e", e=n)

        A3 = carve(N0 + 3400, 256)
        SL_ = carve(N0 + 3700, 2, 2 * NT)
        KEPT = carve(N0 + 3764, 2 * NT)

        def choices(ap):
            return ap.rearrange("p (q e) -> p q e", e=8)

        def slots_dve(eng, link, place, kept):
            t2, all_gates = choices(T2[:, 0:256]), gate[:, :, :].rearrange("p k t -> p (k t)")
            link(eng.tensor_tensor(t2, t2, b3(place, 2 * NT, 1), ALU.add))
            link(eng.tensor_tensor(t2, t2, choices(A3), ALU.mult))
            link(eng.reduce_sum(SL_[:, 0, :], t2, X_AX))
            if kept is None:
                link(eng.tensor_copy(SL_[:, 1, :], SL_[:, 0, :]))
            else:
                link(eng.tensor_tensor(T3[:, 0:256], A3, kept, ALU.mult))
                link(eng.reduce_sum(KEPT, choices(T3[:, 0:256]), X_AX))
                link(eng.tensor_tensor(SL_[:, 1, :], SL_[:, 0, :], KEPT, ALU.mult))
                link(eng.tensor_tensor(all_gates, all_gates, KEPT, ALU.mult))
                link(eng.tensor_scalar(KEPT, KEPT, 1.0, -65536.0, ALU.subtract, ALU.mult))
                link(eng.tensor_tensor(SL_[:, 0, :], SL_[:, 0, :], KEPT, ALU.add))
            return eng.tensor_copy(slots[:, :, :], SL_)

        def gates_dve(eng, link, st):
            eng.wait_ge(sem["exp_ready"], count(st, "exp_ready", 0, 1))
            link(eng.tensor_scalar(gate[:, 0, :], GATE[:, 2, :], 1.0, None, ALU.add))
            link(eng.reciprocal(gate[:, 0, :], gate[:, 0, :]))
            link(eng.tensor_tensor(gate[:, 1, :], GATE[:, 2, :], gate[:, 0, :], ALU.mult))

        def places_dve(eng, link, n):
            w = 8 * n
            link(eng.tensor_copy(T0[:, 0:w], ps[:, 1, 0:w]))
            s = prefix(eng, link, T0, T1, n, 8)
            link(eng.tensor_tensor(T2[:, 0:w], s[:, 0:w], ps[:, 1, 0:w], ALU.subtract))
            link(eng.tensor_tensor(T2[:, 0:w], T2[:, 0:w], ps[:, 0, 0:w], ALU.add))
            return s[:, w - 8:w]

        def cum_pe(eng, st, k, src):
            eng.wait_ge(sem["cum_in"], count(st, "cum_in", 0, k))
            n = src.shape[1]
            eng.matmul(ps[:, 0, 0:n], const("upto"), src, start=True, stop=True)
            eng.matmul(ps[:, 1, 0:n], ones, src, start=True, stop=True).then_inc(sem["cum_ps"], 1)

        def g0_dve(eng, link):
            st = "g0"
            link.start(st, 0)
            eng.wait_ge(sem["lg_ready"], total("r0", "lg_ready"))
            link(top2(eng, link, lg, 8, 8))
            eng.tensor_copy(A3.rearrange("p (k c) -> p k c", k=2), A2[:, :, 0:128]).then_inc(sem["cum_in"], 1)
            eng.tensor_tensor(GATE[:, 2, :], VL[:, :, 1], VL[:, :, 0], ALU.subtract).then_inc(sem["exp_in"], 1)
            eng.tensor_copy(etab[:, 0, 0:24], const("experts"))
            eng.wait_ge(sem["cum_ps"], count(st, "cum_ps", 0, 1))
            places_dve(eng, link, 2 * NT)
            kept = T3[:, 256:512]
            link(eng.tensor_scalar(kept, T2[:, 0:256], float(CAP0), None, ALU.is_le))
            gates_dve(eng, link, st)
            slots_dve(eng, link, const("place"), kept).then_inc(sem["slot_ready"], 1)
            link.end()

        def g3_dve(eng, link):
            st = "g3"
            link.start(st, 0)
            eng.wait_ge(sem["lg_ready"], total("r3", "lg_ready"))
            link(top2(eng, link, lg, 8, 8))
            eng.tensor_copy(A3.rearrange("p (k c) -> p k c", k=2), A2[:, :, 0:128]).then_inc(sem["cum_in"], 1)
            eng.tensor_tensor(GATE[:, 2, :], VL[:, :, 1], VL[:, :, 0], ALU.subtract).then_inc(sem["exp_in"], 1)
            eng.wait_ge(sem["cum_ps"], count(st, "cum_ps", 0, 1))
            rows = places_dve(eng, link, 2 * NT)
            link(eng.tensor_scalar(CAND, rows, 1.0 / P, 127.0 / 256.0, ALU.mult, ALU.add))
            link(eng.tensor_scalar(CAND, CAND, 12582912.0, None, ALU.add))
            link(eng.tensor_scalar(CAND, CAND, 12582912.0, None, ALU.subtract))
            link(eng.tensor_copy(T0[:, 0:8], CAND))
            ends = prefix(eng, link, T0, T1, 8, 1)[:, 0:8]
            link(eng.tensor_tensor(CNT, ends, CAND, ALU.subtract))
            link(eng.tensor_scalar(CNT, CNT, float(P), 1.0, ALU.mult, ALU.subtract))
            past = T3[:, 0:320].rearrange("p (n e) -> p n e", e=8)
            link(eng.tensor_tensor(past, b3(const("blocks"), 8, 2), b3(ends, 40, 1), ALU.is_ge))
            link(eng.reduce_sum(T3[:, 400:440], past, X_AX))
            link(eng.tensor_scalar(etab[:, 2, :], T3[:, 400:440], 7.0, None, ALU.min))
            gates_dve(eng, link, st)
            slots_dve(eng, link, CNT, None).then_inc(sem["slot_ready"], 1)
            link.end()

        def t1_dve(eng, link):
            link.start("t1", 0)
            eng.tensor_copy(etab[:, 1, 0:24], const("experts"))
            eng.wait_ge(sem["lg_ready"], total("r1", "lg_ready"))
            link(top2(eng, link, lg, 8, 8))
            eng.tensor_copy(A3.rearrange("p (k c) -> p k c", k=2), A2[:, :, 0:128])
            eng.tensor_copy(gate[:, :, :], VL[:, :, 0:2].rearrange("p t k -> p k t"))
            link(eng.tensor_tensor(T0[:, 0:128], A2[:, 0, 0:128], A2[:, 1, 0:128], ALU.add))
            link(eng.tensor_tensor(tri(T1[:, 0:128], 8), lg[:, :, 0:8], tri(T0[:, 0:128], 8), ALU.mult))
            eng.memset(CUR, 0.0)
            link(eng.scalar_tensor_tensor(out=GG.rearrange("p t e -> p (t e)"), in0=T0[:, 0:128], scalar=-1.0,
                                          in1=T1[:, 0:128], op0=ALU.add, op1=ALU.add))
            link.end()

        def b1_dve(eng, link, r):
            st = "b1"
            link.start(st, r)
            bits = con[:, bass.ds(r * 3 + CONST["bits"][0], 3)].bitcast(U32)
            link(eng.tensor_tensor(CANDS.bitcast(U32), b3(CUR.bitcast(U32), 3, 1), b3(bits, 8, 2), ALU.bitwise_or))
            ge = T0[:, 0:384].rearrange("p (m e t) -> p m e t", m=3, e=8)
            gates = GG.rearrange("p t e -> p e t").unsqueeze(1).to_broadcast([P, 3, 8, NT])
            link(eng.tensor_tensor(ge, gates, CANDS.unsqueeze(3).to_broadcast([P, 3, 8, NT]), ALU.is_ge))
            eng.reduce_sum(CNTS.rearrange("p m e -> p (m e)"), T0[:, 0:384].rearrange("p (c t) -> p c t", t=NT), X_AX)\
               .then_inc(sem["cum_in"], 1)
            eng.wait_ge(sem["cum_ps"], count(st, "cum_ps", r, 1))
            link(eng.tensor_scalar(SELS.bitcast(U32), ps[:, 0, 0:24], float(CAP1), None, ALU.is_ge))
            for m in range(3):
                eng.memset(slack[:, 0:1], 0.0)
                link(eng.copy_predicated(CUR.bitcast(U32), SELS[:, 8 * m:8 * m + 8].bitcast(U32),
                                         CANDS[:, m, :].bitcast(U32)))
            link.end()

        def b1_pe(eng, r):
            eng.wait_ge(sem["cum_in"], count("b1", "cum_in", r, 1))
            eng.matmul(ps[:, 0, 0:24], ones, CNTS.rearrange("p m e -> p (m e)"), start=True, stop=True)\
               .then_inc(sem["cum_ps"], 1)

        def g1_dve(eng, link):
            st = "g1"
            link.start(st, 0)
            eng.tensor_tensor(tri(T2[:, 0:128], 8), GG, b3(CUR, NT, 1), ALU.is_equal)
            eng.tensor_tensor(tri(T2[:, 128:256], 8), GG, b3(CUR, NT, 1), ALU.is_gt).then_inc(sem["cum_in"], 1)
            eng.wait_ge(sem["cum_ps"], count(st, "cum_ps", 0, 1))
            link(eng.tensor_copy(T0[:, 0:128], ps[:, 1, 0:128]))
            s = prefix(eng, link, T0, T1, NT, 8)
            link(eng.tensor_tensor(T3[:, 0:128], s[:, 0:128], ps[:, 1, 0:128], ALU.subtract))
            link(eng.tensor_tensor(T3[:, 0:128], T3[:, 0:128], ps[:, 0, 0:128], ALU.add))
            link(eng.reduce_sum(CNT, ps[:, 1, 128:256].rearrange("p (t e) -> p e t", e=8), X_AX))
            link(eng.tensor_tensor(tri(T3[:, 0:128], 8), tri(T3[:, 0:128], 8), b3(CNT, NT, 1), ALU.add))
            link(eng.scalar_tensor_tensor(out=T3[:, 0:128], in0=T3[:, 0:128], scalar=float(CAP1), in1=T2[:, 0:128],
                                          op0=ALU.is_le, op1=ALU.mult))
            link(eng.tensor_tensor(T3[:, 0:128], T3[:, 0:128], T2[:, 128:256], ALU.add))
            kept = T3[:, 256:512]
            link(eng.tensor_scalar(kept[:, 0:128], T3[:, 0:128], 1.0, None, ALU.min))
            eng.tensor_copy(kept[:, 128:256], kept[:, 0:128]).then_inc(sem["cum_in"], 1)
            eng.wait_ge(sem["cum_ps"], count(st, "cum_ps", 0, 2))
            places_dve(eng, link, NT)
            link(eng.tensor_copy(T2[:, 128:256], T2[:, 0:128]))
            slots_dve(eng, link, const("place"), kept).then_inc(sem["slot_ready"], 1)
            link.end()

        GS = carve(N0 + 3300, NT, 8)

        def g2_dve(eng, link):
            st = "g2"
            link.start(st, 0)
            eng.wait_ge(sem["lg_ready"], total("r2", "lg_ready"))
            eng.memset(GS, NEG)
            link(eng.tensor_tensor(tri(T0[:, 0:256], 16), lg[:, :, :], b3(gb2, NT, 1), ALU.add))
            v = T0[:, 0:256].rearrange("p (g a b) -> p g a b", a=2, b=2)
            hi = T1[:, 0:128].rearrange("p (g a) -> p g a", a=2)
            lo = T1[:, 128:256].rearrange("p (g a) -> p g a", a=2)
            eng.tensor_tensor(hi, v[:, :, :, 0], v[:, :, :, 1], ALU.max)
            link(eng.tensor_tensor(lo, v[:, :, :, 0], v[:, :, :, 1], ALU.min))
            eng.tensor_tensor(T2[:, 0:64], hi[:, :, 0], hi[:, :, 1], ALU.max)
            eng.tensor_tensor(T2[:, 64:128], hi[:, :, 0], hi[:, :, 1], ALU.min)
            link(eng.tensor_tensor(T2[:, 128:192], lo[:, :, 0], lo[:, :, 1], ALU.max))
            link(eng.tensor_tensor(T2[:, 64:128], T2[:, 64:128], T2[:, 128:192], ALU.max))
            link(eng.tensor_tensor(GS[:, :, 0:4], tri(T2[:, 0:64], 4), tri(T2[:, 64:128], 4), ALU.add))
            link(top2(eng, link, GS, 4, 8))
            link(eng.tensor_tensor(T1[:, 0:64], A2[:, 0, 0:64], A2[:, 1, 0:64], ALU.add))
            kept = b3(T1[:, 0:64], 4, 2)
            eng.tensor_scalar(T1[:, 64:128], T1[:, 0:64], 1.0, -NEG, ALU.subtract, ALU.mult)
            link(eng.tensor_tensor(T2[:, 0:256].rearrange("p (g c) -> p g c", c=4),
                                   T0[:, 0:256].rearrange("p (g c) -> p g c", c=4), kept, ALU.mult))
            link(eng.tensor_tensor(T2[:, 0:256].rearrange("p (g c) -> p g c", c=4),
                                   T2[:, 0:256].rearrange("p (g c) -> p g c", c=4), b3(T1[:, 64:128], 4, 2), ALU.add))
            link(top2(eng, link, tri(T2[:, 0:256], 16), 16, 16))
            link(eng.tensor_tensor(T1[:, 0:256], A2[:, 0, 0:256], A2[:, 1, 0:256], ALU.add))
            eng.memset(comb[:, :, 16:18], 1.0)
            eng.tensor_tensor(comb[:, :, 0:16], lg[:, :, :], tri(T1[:, 0:256], 16), ALU.mult).then_inc(sem["c_ready"], 1)
            link.end()

        UW, UN, UG = 384, 3, 6
        NUN = GT * UN
        HS = carve(N0, GW)
        CSS, CTR = carve(N0 + 512, GT, 18), carve(N0 + 600, GW)
        SLU, S3U, GU = carve(N0 + 1200, 2, UW), carve(N0 + 2000, 2, UW), carve(N0 + 2800, 2, UW)
        GTU = carve(N0 + 3600, 2, UW)

        def f2_pe(eng, i):
            st = "f2"
            eng.wait_ge(sem["h_staged"], count(st, "h_staged", i, 1))
            eng.wait_ge(sem["c_in"], count(st, "c_in", i, 1))
            eng.wait_ge(sem["x_ready"], count(st, "x_ready", i))
            for j in range(GT):
                last = eng.transpose(ps[0:18, 7, j * P:(j + 1) * P], CSS[:, j, :], ident)
            last.then_inc(sem["c_turned"], 1)

            def up(u):
                if u < NUN:
                    j, c = divmod(u, UN)
                    for n, w in enumerate((U1, U3)):
                        last = eng.matmul(ps[:, 2 * (u % 2) + n, 0:UW], HS[:, j * P:(j + 1) * P],
                                          w[:, UW * c:UW * c + UW], start=True, stop=True)
                    last.then_inc(sem["h_ps"], 1)

            up(0)
            up(1)
            for u in range(NUN):
                j, c = divmod(u, UN)
                eng.wait_ge(sem["mid_ready"], count(st, "mid_ready", i, u + 1))
                for f in range(UW // P):
                    last = eng.transpose(ps[:, 4 + u % 2, f * P:(f + 1) * P], GU[:, u % 2, f * P:(f + 1) * P], ident)
                last.then_inc(sem["mid_ps"], 1)
                up(u + 2)
                if c == 0:
                    if j == 0:
                        eng.wait_ge(sem["cT_ready"], count(st, "cT_ready", i, 1))
                    if j >= 2:
                        eng.wait_ge(sem["x_ready"], count(st, "x_ready", i, j - 1))
                    eng.matmul(ps[:, 6 + j % 2, 0:D], CTR[0:18, j * P:(j + 1) * P], b2f2, start=True, stop=False)
                eng.wait_ge(sem["midT_ready"], count(st, "midT_ready", i, u + 1))
                for f in range(UW // P):
                    last = eng.matmul(ps[:, 6 + j % 2, 0:D], GTU[:, u % 2, f * P:(f + 1) * P], U2[:, 3 * c + f, :],
                                      start=False, stop=(c == UN - 1 and f == UW // P - 1))
                if c == UN - 1:
                    last.then_inc(sem["y_ps"], 1)

        def f2_act(eng, i):
            st = "f2"
            warm(eng, ACT.Silu)
            eng.wait_ge(sem["c_turned"], count(st, "c_turned", i, 1))
            eng.activation(CTR[0:18, :], ps[0:18, 7, :], ACT.Copy).then_inc(sem["cT_ready"], 1)

            def silu(u):
                if u < NUN:
                    eng.wait_ge(sem["act_in"], count(st, "act_in", i, u + 1))
                    eng.activation(SLU[:, u % 2, :], SLU[:, u % 2, :], ACT.Silu).then_inc(sem["act_ready"], 1)

            silu(0)
            silu(1)
            for u in range(NUN):
                eng.wait_ge(sem["mid_ps"], count(st, "mid_ps", i, u + 1))
                eng.activation(GTU[:, u % 2, :], ps[:, 4 + u % 2, 0:UW], ACT.Copy).then_inc(sem["midT_ready"], 1)
                silu(u + 2)

        def f2_dve(eng, link, i):
            st = "f2"
            link.start(st, i)
            eng.wait_ge(sem["c_turned"], count(st, "c_turned", i))
            eng.tensor_scalar(CSS, group(comb, i), 1.0, None, ALU.mult).then_inc(sem["c_in"], 1)

            def before(u):
                if u < NUN:
                    j, c = divmod(u, UN)
                    eng.wait_ge(sem["h_ps"], count(st, "h_ps", i, u + 1))
                    eng.tensor_tensor(SLU[:, u % 2, :], ps[:, 2 * (u % 2), 0:UW], UB1[:, UW * c:UW * c + UW], ALU.add)\
                       .then_inc(sem["act_in"], 1)
                    link(eng.tensor_tensor(S3U[:, u % 2, :], ps[:, 2 * (u % 2) + 1, 0:UW], UB3[:, UW * c:UW * c + UW],
                                           ALU.add))
                    s3 = S3U[:, u % 2, :].rearrange("p (g c) -> p g c", g=UG)
                    link(eng.tensor_tensor(s3, s3, b3(CSS[:, j, UG * c:UG * c + UG], UW // UG, 2), ALU.mult))

            def add(j):
                eng.wait_ge(sem["y_ps"], count(st, "y_ps", i, j + 1))
                x = xs[:, bass.ds(i * GT + j, 1), :].rearrange("p a d -> p (a d)")
                eng.tensor_tensor(x, x, ps[:, 6 + j % 2, 0:D], ALU.add).then_inc(sem["x_ready"], 1)

            eng.wait_ge(sem["c_in"], count(st, "c_in", i, 1))
            def gated(u):
                if u < NUN:
                    eng.wait_ge(sem["act_ready"], count(st, "act_ready", i, u + 1))
                    eng.tensor_tensor(GU[:, u % 2, :], SLU[:, u % 2, :], S3U[:, u % 2, :], ALU.mult)\
                       .then_inc(sem["mid_ready"], 1)

            before(0)
            before(1)
            gated(0)
            for u in range(NUN):
                gated(u + 1)
                before(u + 2)
                if u >= UN + 1 and (u - 1) % UN == 0:
                    add((u - 1) // UN - 1)
            add(GT - 1)
            link.end()

        def f2_pool(eng, i):
            eng.wait_ge(sem["y_ps"], count("f2", "y_ps", i))
            bridge(eng)
            eng.tensor_copy(HS, cols(hT, i)).then_inc(sem["h_staged"], 1)

        f2 = (f2_pe, f2_act, f2_dve, f2_pool)

        XE = carve(N0, KB_, D)
        XTS = carve(N0 + 1024, 2, P)
        SLB = carve(N0 + 6000, 4, F)
        GB_, GTB = carve(N0 + 2816, 2, F), carve(N0 + 3840, 2, F)
        YS = carve(N0 + 4864, KB_, D)
        GATH = carve(N0, 2 * NT, D)

        def moe(st, layer, w1, w3, w2, b1):
            shared = layer is None
            deep = w3 is None

            def expert(eng, i, k):
                if shared:
                    return E - 1
                return eng.value_load(etab[0:1, layer, bass.ds(i * KB_ + k, 1)], min_val=0, max_val=E - 1)

            def sp(eng, i, n, last):
                for k in range(n):
                    eng.wait_ge(sem["xt_ps"], count(st, "xt_ps", i, k + 1 - KB_))
                    rows = hr[:, bass.ds(i * KB_ + k, 1), :].rearrange("p a d -> p (a d)") if shared\
                        else xe[bass.ds((i * KB_ + k) * P, P), :]
                    eng.dma_start(XE[:, k, :], rows).then_inc(sem[f"xe{k}"], 16)

            def turn(eng, i, k):
                place_ = k % KB_
                eng.wait_ge(sem[f"xe{place_}"], count(st, f"xe{place_}", i, 16 * (k // KB_ + 1)))
                eng.wait_ge(sem["xt_ready"], count(st, "xt_ready", i, k))
                eng.transpose(ps[:, 6, 0:P], XE[:, place_, :], ident).then_inc(sem["xt_ps"], 1)

            def up(eng, i, k, e):
                eng.wait_ge(sem["xt_ready"], count(st, "xt_ready", i, k + 1))
                b = k % 4 if deep else 2 * (k % 2)
                last = eng.matmul(ps[:, b, :], XTS[:, k % 2, :], w1[:, bass.ds(e, 1), :], start=True, stop=True)
                if w3 is not None:
                    last = eng.matmul(ps[:, b + 1, :], XTS[:, k % 2, :], w3[:, bass.ds(e, 1), :], start=True, stop=True)
                last.then_inc(sem["h_ps"], 1)

            def pe_first(eng):
                turn(eng, 0, 0)
                up(eng, 0, 0, expert(eng, 0, 0))
                turn(eng, 0, 1)
                up(eng, 0, 1, expert(eng, 0, 1))
                turn(eng, 0, 2)

            def pe(eng, i, n, last):
                which = {k: expert(eng, i, k) for k in range(2)}
                for k in range(n):
                    eng.wait_ge(sem["mid_ready"], count(st, "mid_ready", i, k + 1))
                    for f in range(FB):
                        done = eng.transpose(ps[:, 4 + k % 2, f * P:(f + 1) * P], GB_[:, k % 2, f * P:(f + 1) * P], ident)
                    done.then_inc(sem["mid_ps"], 1)
                    if k + 2 < n or not last:
                        which[k + 2] = expert(eng, i, k + 2)
                        up(eng, i, k + 2, which[k + 2])
                    if k + 3 < n or not last:
                        turn(eng, i, k + 3)
                    eng.wait_ge(sem["y_read"], count(st, "y_read", i, k))
                    eng.wait_ge(sem["midT_ready"], count(st, "midT_ready", i, k + 1))
                    for f in range(FB):
                        done = eng.matmul(ps[:, 7, 0:D], GTB[:, k % 2, f * P:(f + 1) * P],
                                          w2[:, bass.ds(which[k] * FB + f, 1), :], start=(f == 0), stop=(f == FB - 1))
                    done.then_inc(sem["y_ps"], 1)

            def turned(eng, i, k):
                eng.wait_ge(sem["xt_ps"], count(st, "xt_ps", i, k + 1))
                eng.activation(XTS[:, k % 2, :], ps[:, 6, 0:P], ACT.Copy).then_inc(sem["xt_ready"], 1)

            def silu(eng, i, k):
                if deep:
                    eng.wait_ge(sem["act_in"], count(st, "act_in", i, k + 1))
                    eng.activation(GB_[:, k % 2, :], SLB[:, k % 4, :], ACT.Silu).then_inc(sem["mid_ready"], 1)
                else:
                    eng.wait_ge(sem["h_ps"], count(st, "h_ps", i, k + 1))
                    eng.activation(SLB[:, k % 4, :], ps[:, 2 * (k % 2), :], ACT.Silu).then_inc(sem["act_ready"], 1)

            def act_first(eng):
                warm(eng, ACT.Silu)
                turned(eng, 0, 0)
                turned(eng, 0, 1)
                silu(eng, 0, 0)
                turned(eng, 0, 2)
                silu(eng, 0, 1)

            def act(eng, i, n, last):
                warm(eng, ACT.Silu)
                for k in range(n):
                    eng.wait_ge(sem["mid_ps"], count(st, "mid_ps", i, k + 1))
                    eng.activation(GTB[:, k % 2, :], ps[:, 4 + k % 2, :], ACT.Copy).then_inc(sem["midT_ready"], 1)
                    if k + 3 < n or not last:
                        turned(eng, i, k + 3)
                    if k + 2 < n or not last:
                        silu(eng, i, k + 2)

            def hidden_in(eng, i, k, e):
                if deep:
                    eng.wait_ge(sem["h_ps"], count(st, "h_ps", i, k + 1))
                    eng.tensor_tensor(SLB[:, k % 4, :], ps[:, k % 4, :], b1[:, bass.ds(e, 1), :], ALU.add)\
                       .then_inc(sem["act_in"], 1)
                else:
                    eng.wait_ge(sem["act_ready"], count(st, "act_ready", i, k + 1))
                    eng.tensor_tensor(GB_[:, k % 2, :], SLB[:, k % 4, :], ps[:, 2 * (k % 2) + 1, :], ALU.mult)\
                       .then_inc(sem["mid_ready"], 1)

            def dve_first(eng):
                for k in range(2):
                    hidden_in(eng, 0, k, expert(eng, 0, k) if deep else None)

            def dve(eng, i, n, last):
                which = {k: expert(eng, i, k) for k in range(2)} if deep else {}
                for k in range(n):
                    if k + 2 < n or not last:
                        if deep:
                            which[k + 2] = expert(eng, i, k + 2)
                        hidden_in(eng, i, k + 2, which.get(k + 2))
                    if not shared:
                        eng.wait_ge(sem["ys_free"], count(st, "ys_free", i, k + 1 - KB_))
                    eng.wait_ge(sem["y_ps"], count(st, "y_ps", i, k + 1))
                    if shared:
                        x = xs[:, bass.ds(i * KB_ + k, 1), :].rearrange("p a d -> p (a d)")
                        eng.tensor_tensor(x, x, ps[:, 7, 0:D], ALU.add).then_inc(sem["y_read"], 1)
                    elif deep:
                        eng.tensor_tensor(YS[:, k, :], ps[:, 7, 0:D], b2r[:, bass.ds(which[k], 1), :], ALU.add)\
                           .then_inc(sem["y_read"], 1)
                    else:
                        eng.tensor_scalar(YS[:, k, :], ps[:, 7, 0:D], 1.0, None, ALU.mult).then_inc(sem["y_read"], 1)

            def pool(eng, i, n, last):
                for k in range(n):
                    eng.wait_ge(sem["y_read"], count(st, "y_read", i, k + 1))
                    bridge(eng, 1 + k)
                    eng.dma_start(ye[bass.ds((i * KB_ + k) * P, P), :], YS[:, k, :]).then_inc(sem[f"ys{k}"], 16)
                    for done in ([k - 2] if k >= 2 else []) + ([k - 1, k] if k == n - 1 else []):
                        eng.wait_ge(sem[f"ys{done}"], count(st, f"ys{done}", i, 16))
                        bridge(eng, 1 + KB_ + done).then_inc(sem["ys_free"], 1)

            def run(first, turn_):
                def f(eng):
                    turns, rest = PLACES[st]
                    if first:
                        first(eng)
                    with eng.Fori(0, turns) as i:
                        turn_(eng, i, KB_, False)
                    turn_(eng, turns, rest, True)
                return f

            return run(pe_first, pe), run(act_first, act), run(dve_first, dve), run(None, pool), run(None, sp)

        def flat_w(w):
            return w.rearrange("p e f d -> p (e f) d")

        s0 = moe("s0", None, W1, W3, flat_w(W2), None)
        f0 = moe("f0", 0, W1, W3, flat_w(W2), None)
        f1 = moe("f1", 1, V1, None, flat_w(V2), VB1)
        f3 = moe("f3", 2, V1, None, flat_w(V2), VB1)

        experts_loops = {"s0": s0, "f0": f0, "f1": f1, "f3": f3}

        def row_index(way, n):
            return bass.IndirectOffsetOnAxis(ap=slots[:, way, n:n + 1], axis=0)

        def dispatch_pool(eng, layer):
            eng.wait_ge(sem["slot_ready"], total("g" + layer, "slot_ready"))
            eng.wait_ge(sem["ht_ready"], total("r" + layer, "ht_ready"))
            eng.wait_ge(s_zero, 16 * 2)
            for n in range(2 * NT):
                eng.indirect_dma_start(xe, row_index(0, n), hr[:, n % NT, :], None,
                                       bounds_check=ROWS - 1, oob_is_err=False).then_inc(s_sent, 16)

        def gather(eng, g, k, j, to):
            eng.indirect_dma_start(to, None, ye, row_index(1, NT * k + GT * g + j),
                                   bounds_check=ROWS - 1, oob_is_err=False).then_inc(s_back[g], 16)

        def experts_done(eng, st):
            for k in range(KB_):
                eng.wait_ge(sem[f"ys{k}"], total(st + "_last", f"ys{k}"))

        def gather_pool(eng):
            experts_done(eng, "f3")
            for g in range(NG):
                for j in range(GT):
                    for k in range(2):
                        gather(eng, g, k, j, GATH[:, NT * k + GT * g + j, :])

        def gather_turns_pool(eng, st, layer, norms):
            def rows(g, tiles=range(GT)):
                q = g % 2
                if g >= 2:
                    eng.wait_ge(sem["combined"], count(st, "combined", g // 2 - 1, q + 1))
                for j in tiles:
                    for k in range(2):
                        gather(eng, g, k, j, hr[:, 2 * GT * q + GT * k + j, :])

            def relay(g):
                eng.wait_ge(s_back[g], 16 * 2 * GT * (layer + 1))
                bridge(eng, 18 + NG * layer + g).then_inc(sem["gathered"], 1)

            experts_done(eng, f"f{layer}")
            rows(0)
            rows(1, range(GT // 2))
            relay(0)
            rows(1, range(GT // 2, GT))
            relay(1)
            for i in range(LOOPS[st]):
                for k in range(norms):
                    for q in SIDES:
                        norm_side_pool(eng, st, i, k + 1, q)
                    if i == 0 and k < 2:
                        rows(2 + k)
                    if i == 0 and k == 1:
                        relay(2)
                        relay(3)

        def combine_turn_dve(eng, link, st, i):
            for q in SIDES:
                eng.wait_ge(sem["gathered"], count(st, "gathered", i, q + 1))
                for k in range(2):
                    for j in range(GT):
                        tile = i * 2 * GT + q * GT + j
                        x = xs[:, bass.ds(tile, 1), :].rearrange("p a d -> p (a d)")
                        last = eng.scalar_tensor_tensor(out=x, in0=hr[:, 2 * GT * q + GT * k + j, :],
                                                        scalar=gate[:, k, bass.ds(tile, 1)], in1=x,
                                                        op0=ALU.mult, op1=ALU.add)
                    if k == 0:
                        link(last)
                last.then_inc(sem["combined"], 1)
                eng.wait_ge(sem["combined"], count(st, "combined", i, q + 1))
                eng.memset(slack[:, 0:1], 0.0)
                norm_in(eng, link, q, of_side(xs, i, q))

        def combine_dve(eng, link):
            link.start("c3", 0)
            for g in range(NG):
                eng.wait_ge(s_back[g], 16 * 2 * GT * 3)
                for k in range(2):
                    for j in range(GT):
                        q = GT * g + j
                        last = eng.scalar_tensor_tensor(out=xs[:, q, :], in0=GATH[:, NT * k + q, :],
                                                        scalar=gate[:, k, q:q + 1], in1=xs[:, q, :],
                                                        op0=ALU.mult, op1=ALU.add)
                    if k == 0:
                        link(last)
                last.then_inc(sem["x_ready"], 1)
            link.end()

        def scores_pe(eng, st, i, k, q, qT, keys):
            for j in range(GT):
                last = eng.matmul(ps[:, 4 * q + 1, j * P:(j + 1) * P], qT[:, j * P:(j + 1) * P], keys(j),
                                  start=True, stop=True)
            last.then_inc(sem["sc_ps"], 1)

        def weights_pe(eng, st, i, k, q):
            eng.wait_ge(sem["ex_ready"], count(st, "ex_ready", i, nth(k, q)))
            for j in range(GT):
                last = eng.transpose(ps[:, 4 * q + 2, j * P:(j + 1) * P], SC_[q][:, j, :], ident)
            last.then_inc(sem["pt_ps"], 1)

        def values_pe(eng, st, i, k, q, vals):
            eng.wait_ge(sem["pt_ready"], count(st, "pt_ready", i, nth(k, q)))
            for j in range(GT):
                last = eng.matmul(ps[:, 4 * q + 3, j * P:(j + 1) * P], PTT_[q][:, j * P:(j + 1) * P], vals(j),
                                  start=True, stop=True)
            last.then_inc(sem["av_ps"], 1)

        def attend_act(eng, st, i, k):
            for q in SIDES:
                eng.wait_ge(sem["sm_in"], count(st, "sm_in", i, nth(k, q)))
                eng.activation(SC_[q], SC_[q], ACT.Exp, scale=D ** -0.5).then_inc(sem["ex_ready"], 1)
            for q in SIDES:
                eng.wait_ge(sem["pt_ps"], count(st, "pt_ps", i, nth(k, q)))
                eng.activation(PTT_[q], ps[:, 4 * q + 2, :], ACT.Copy).then_inc(sem["pt_ready"], 1)

        def quad(ap):
            return ap.rearrange("p (a b) -> p a b", a=GT)

        def attend_dve(eng, link, st, i, k, bias):
            for q in SIDES:
                eng.wait_ge(sem["sc_ps"], count(st, "sc_ps", i, nth(k, q)))
                bias(q)
                m = mx[:, GT * q:GT * q + GT]
                link(eng.tensor_reduce(m, SC_[q], X_AX, ALU.max))
                eng.tensor_tensor(SC_[q], SC_[q], b3(m, P, 2), ALU.subtract).then_inc(sem["sm_in"], 1)
            for q in SIDES:
                eng.wait_ge(sem["ex_ready"], count(st, "ex_ready", i, nth(k, q)))
                link(eng.reduce_sum(sm[:, GT * q:GT * q + GT], SC_[q], X_AX))
                link(eng.reciprocal(rs[:, GT * q:GT * q + GT], sm[:, GT * q:GT * q + GT]))

        def context_keys(i, q):
            return lambda j: cT[:, bass.ds(i * 2 * GW + q * GW + j * P, P)]

        def context_rows(i, q):
            return lambda j: cs[:, bass.ds(i * 2 * GT + q * GT + j, 1), :]

        def a1_pe(eng, i):
            st = "a1"
            for k in (1, 2):
                for q in SIDES:
                    turn_side_pe(eng, st, i, k, q, XH_[q] if k == 1 else Y1_[q])
                for q in SIDES:
                    eng.wait_ge(sem["cols_ready"], count(st, "cols_ready", i, nth(k, q)))
                    scores_pe(eng, st, i, k, q, XT_[q], (lambda j: XT_[q][:, j * P:(j + 1) * P]) if k == 1
                              else context_keys(i, q))
                for q in SIDES:
                    weights_pe(eng, st, i, k, q)
                for q in SIDES:
                    values_pe(eng, st, i, k, q, (lambda j: XH_[q][:, j, :]) if k == 1 else context_rows(i, q))
            for q in SIDES:
                turn_side_pe(eng, st, i, 3, q, Y2_[q])
            for q in SIDES:
                eng.wait_ge(sem["cols_ready"], count(st, "cols_ready", i, nth(3, q)))
                for f in range(FB):
                    last = eng.matmul(ps[:, 4 * q + f, :], w1a[:, f * P:(f + 1) * P], XT_[q], start=True, stop=True)
                last.then_inc(sem["h_ps"], 1)
            for q in SIDES:
                eng.wait_ge(sem["mid_ready"], count(st, "mid_ready", i, nth(1, q)))
                for j in range(GT):
                    for f in range(FB):
                        last = eng.matmul(ps[:, 4 * q + 1, j * P:(j + 1) * P], HID_[q][:, f, j * P:(j + 1) * P],
                                          w2a[:, f, :], start=(f == 0), stop=(f == FB - 1))
                last.then_inc(sem["y_ps"], 1)

        def a1_act(eng, i):
            st = "a1"
            warm(eng, ACT.Exp)
            for k in (1, 2, 3):
                for q in SIDES:
                    turn_side_act(eng, st, i, k, q)
                if k < 3:
                    attend_act(eng, st, i, k)

        def affine(eng, link, y, g, b, signal=None):
            link(eng.tensor_tensor(y, y, b3(g, GT, 1), ALU.mult))
            last = eng.tensor_tensor(y, y, b3(b, GT, 1), ALU.add)
            if signal:
                last.then_inc(sem[signal], 1)
            else:
                link(last)

        def weighted(eng, q, add):
            for j in range(GT):
                value, inverse = ps[:, 4 * q + 3, j * P:(j + 1) * P], rs[:, GT * q + j:GT * q + j + 1]
                if add is None:
                    last = eng.tensor_scalar(R_[q][:, j, :], value, inverse, None, ALU.mult)
                else:
                    last = eng.scalar_tensor_tensor(out=R_[q][:, j, :], in0=value, scalar=inverse, in1=add[:, j, :],
                                                    op0=ALU.mult, op1=ALU.add)
            return last

        def a1_dve(eng, link, i):
            st = "a1"
            link.start(st, i)
            combine_turn_dve(eng, link, st, i)
            for q in SIDES:
                norm_out(eng, st, i, 1, q, of_side(xs, i, q), XH_[q]).then_inc(sem["rows_ready"], 1)
            for k, masks, before, after in ((1, "causal2", XH_, Y1_), (2, "same2", Y1_, Y2_)):
                attend_dve(eng, link, st, i, k, lambda q: link(eng.tensor_tensor(
                    SC_[q], quad(ps[:, 4 * q + 1, :]), b3(const(masks), GT, 1), ALU.add)))
                for q in SIDES:
                    eng.wait_ge(sem["av_ps"], count(st, "av_ps", i, nth(k, q)))
                    link(weighted(eng, q, before[q]))
                    norm_in(eng, link, q, R_[q])
                for q in SIDES:
                    link(norm_out(eng, st, i, k + 1, q, R_[q], after[q]))
                    affine(eng, link, after[q], ga[k - 1], ba[k - 1], "rows_ready")
            for q in SIDES:
                eng.wait_ge(sem["h_ps"], count(st, "h_ps", i, nth(1, q)))
                for f in range(FB):
                    last = eng.tensor_scalar(HID_[q][:, f, :], ps[:, 4 * q + f, :], b1a[:, f:f + 1], 0.0, ALU.add,
                                             ALU.max)
                last.then_inc(sem["mid_ready"], 1)
            for q in SIDES:
                eng.wait_ge(sem["y_ps"], count(st, "y_ps", i, nth(1, q)))
                link(eng.tensor_tensor(R_[q], quad(ps[:, 4 * q + 1, :]), b3(b2a, GT, 1), ALU.add))
                link(eng.tensor_tensor(R_[q], R_[q], Y2_[q], ALU.add))
                norm_in(eng, link, q, R_[q])
            for q in SIDES:
                link(norm_out(eng, st, i, 4, q, R_[q], Y1_[q]))
                affine(eng, link, Y1_[q], ga[2], ba[2])
                g = of_side(xs, i, q)
                eng.tensor_tensor(g, g, Y1_[q], ALU.add).then_inc(sem["x_ready"], 1)
            link.end()

        def a2_pe(eng, i):
            st = "a2"
            for q in SIDES:
                turn_side_pe(eng, st, i, 1, q, XH_[q])
            for q in SIDES:
                eng.wait_ge(sem["cols_ready"], count(st, "cols_ready", i, nth(1, q)))
                scores_pe(eng, st, i, 1, q, XT_[q], context_keys(i, q))
            for q in SIDES:
                weights_pe(eng, st, i, 1, q)
            for q in SIDES:
                values_pe(eng, st, i, 1, q, context_rows(i, q))

        def a2_act(eng, i):
            warm(eng, ACT.Exp)
            for q in SIDES:
                turn_side_act(eng, "a2", i, 1, q)
            attend_act(eng, "a2", i, 1)

        def a2_dve(eng, link, i):
            st = "a2"
            link.start(st, i)
            combine_turn_dve(eng, link, st, i)
            for q in SIDES:
                norm_out(eng, st, i, 1, q, of_side(xs, i, q), XH_[q]).then_inc(sem["rows_ready"], 1)
            for q in SIDES:
                link(eng.memset(MF_[q], 0.0))
                for b in range(2):
                    r = slice(S * b, S * b + S)
                    last = eng.tensor_scalar(MF_[q][r, :, r], m2i[r, bass.ds(i * 2 * GT + q * GT, GT), :], 0.0, None,
                                             ALU.not_equal)
                link(last)
                link(eng.tensor_scalar(MA_[q], MF_[q], 9.0e15, 9.0e15, ALU.mult, ALU.subtract))
                link(eng.tensor_tensor(MA_[q], MA_[q], b3(const("same2"), GT, 1), ALU.add))

            def masked(q):
                link(eng.tensor_tensor(SC_[q], quad(ps[:, 4 * q + 1, :]), MF_[q], ALU.mult))
                link(eng.tensor_tensor(SC_[q], SC_[q], MA_[q], ALU.add))

            attend_dve(eng, link, st, i, 1, masked)
            for q in SIDES:
                eng.wait_ge(sem["av_ps"], count(st, "av_ps", i, nth(1, q)))
                link(weighted(eng, q, None))
                norm_in(eng, link, q, R_[q])
            for q in SIDES:
                link(norm_out(eng, st, i, 2, q, R_[q], Y1_[q]))
                affine(eng, link, Y1_[q], g2, be2)
                g = of_side(xs, i, q)
                eng.tensor_tensor(g, g, Y1_[q], ALU.add).then_inc(sem["x_ready"], 1)
            link.end()

        KH = 96
        QT3 = carve(N0, GW)
        QX = carve(N0 + 1536, 2, GW)
        IXT, LT1, LT2 = [work[0:KH, N0 + 2560 + 512 * n:N0 + 3072 + 512 * n] for n in range(3)]
        KV = carve(N0 + 4096, GB, 8, 32)
        OX = carve(N0 + 6144, 2, GW)
        PRD, TT, EX, WW = [carve(N0 + 7168 + 640 * n, 2, NK, S) for n in range(4)]
        SMQ, RQ, UQ, MQ = [carve(N0 + 9728 + 128 * n, 2, S) for n in range(4)]
        KVT = carve(N0 + 7168, GB, D)
        PAIRS = carve(N0 + 2560, 2, 2, S)
        AH = wa[:, 0:10240].rearrange("p (r j k c) -> p r j k c", r=2, j=4, k=NK)
        AB = wa[:, 10240:11776].rearrange("p (r c) -> p r c", r=3)
        windows = wa[0:KH, 10240:12288]
        WIN = hT[0:KH, 0:1024].bitcast(BF16)
        IXB = hT[0:KH, 1024:1792].bitcast(BF16).rearrange("p (n c) -> p n c", n=3)
        PARTS = work[0:KH, N0 + 7168:N0 + 7936].bitcast(BF16).rearrange("p (n c) -> p n c", n=3)
        M3 = wa[0:KH, 8192:10240].bitcast(I32).rearrange("p (b s) -> p b s", b=B)
        LEN, SGN, INV = [wa[0:KH, 11776 + 32 * n:11808 + 32 * n] for n in range(3)]
        SG = GW // 2
        CHUNKS = [(j, ks) for j0 in range(2) for ks in ((0, 1), (2, 3), (4,)) for j in (j0, j0 + 2)]
        SKV_BANK = (3, 4, 7)
        NU3 = 16

        AHEAD = 15

        def with_unit(u):
            return range(min(AHEAD + 3 * u, 48), min(AHEAD + 3 * u + 3, 48)) if u >= 0 else ()

        def unit(u):
            n, b = divmod(u, 4)
            return n, n // 2, n % 2, b

        def m3_dve(eng, link):
            link.start("m3", 0)
            link(eng.tensor_copy(WIN, windows))
            link(eng.reduce_sum(LEN, M3, X_AX))
            link(eng.tensor_scalar(LEN, LEN, -1.0, float(S - 1), ALU.mult, ALU.add))
            link(eng.tensor_scalar(SGN, LEN, 0.0, None, ALU.is_ge))
            link(eng.tensor_scalar(SGN, SGN, 2.0, 1.0, ALU.mult, ALU.subtract))
            link(eng.tensor_tensor(LEN, LEN, SGN, ALU.mult))
            link(eng.reciprocal(INV, LEN))
            link.end()

        def a3_pe(eng, i):
            st = "a3"

            def kv(w):
                for b in range(GB):
                    last = eng.matmul(ps[:, 5 + b // 4, (b % 4) * P:(b % 4 + 1) * P], dup(b), w, start=True, stop=True)
                return last

            eng.wait_ge(sem["ct_staged"], count(st, "ct_staged", i, 1))
            kv(wk3).then_inc(sem["k_ps"], 1)
            turn_pe(eng, st, i, 1, XH)
            eng.wait_ge(sem["cols_ready"], count(st, "cols_ready", i, 1))
            eng.matmul(ps[:, 1, :], wq3, XT, start=True, stop=True).then_inc(sem["q_ps"], 1)
            eng.wait_ge(sem["q_ready"], count(st, "q_ready", i, 1))
            eng.matmul(ps[0:KH, 4, :], woff3, QT3, start=True, stop=True).then_inc(sem["off_ps"], 1)
            for h in range(2):
                last = eng.matmul(ps[:, 2 + h, :], wqx3[:, h, :], XT, start=True, stop=True)
            last.then_inc(sem["qx_ps"], 1)
            eng.wait_ge(sem["k_read"], count(st, "k_read", i, 1))
            kv(wv3).then_inc(sem["v_ps"], 1)
            eng.wait_ge(sem["ix_ready"], count(st, "ix_ready", i, 1))

            def gaps(c):
                n, (j, ks) = c // 12, CHUNKS[c % 12]
                hp = 4 * (n % 2) + j
                if c >= 3:
                    eng.wait_ge(sem["gap_ready"], count(st, "gap_ready", i, c - 2))
                if c == 2:
                    eng.wait_ge(sem["qx_read"], count(st, "qx_read", i, 1))
                for m, place_ in enumerate(ks):
                    first = S * (16 * (place_ % 2) + 2 * hp)
                    last = eng.matmul(ps[:, c % 3, m * SG:(m + 1) * SG], WIN[:, first:first + 2 * S],
                                      IXB[:, place_ // 2, (n // 2) * SG:(n // 2 + 1) * SG], start=True, stop=True)
                last.then_inc(sem["gap_ps"], 1)

            def sampled(u):
                n, sg, half, b = unit(u)
                if b == 0:
                    eng.wait_ge(sem["hat_ready"], count(st, "hat_ready", i, 6 * (n + 1)))
                    eng.wait_ge(sem["odd_hat_ready"], count(st, "odd_hat_ready", i, 6 * (n + 1)))
                if u >= 3:
                    eng.wait_ge(sem["skv_read"], count(st, "skv_read", i, u - 2))
                for j in range(4):
                    last = eng.matmul(ps[32 * j:32 * j + 32, SKV_BANK[u % 3], 0:NK * S], KV[:, 4 * sg + b, 4 * half + j, :],
                                      AH[:, n % 2, j, :, b * S:(b + 1) * S], start=True, stop=True,
                                      tile_position=(0, 32 * j))
                last.then_inc(sem["skv_ps"], 1)

            for c in range(12):
                gaps(c)
            eng.wait_ge(sem["kv_ready"], count(st, "kv_ready", i, 1))
            sampled(0)
            for c in range(12, AHEAD):
                gaps(c)
            for u in range(NU3):
                eng.wait_ge(sem["prod_ready"], count(st, "prod_ready", i, u + 1))
                if u >= 2:
                    eng.wait_ge(sem["sm_in"], count(st, "sm_in", i, u - 1))
                eng.matmul(ps[:, 5 + u % 2, 0:NK * S], const("spread"), PRD[:, u % 2, :, :].rearrange("p k q -> p (k q)"),
                           start=True, stop=True).then_inc(sem["score_ps"], 1)
                for c in with_unit(u):
                    gaps(c)
                if u + 1 < NU3:
                    sampled(u + 1)
            eng.wait_ge(sem["o_ready"], count(st, "o_ready", i, NU3))
            for j in range(GT):
                for h in range(2):
                    last = eng.matmul(ps[:, 7, j * P:(j + 1) * P], OX[:, h, j * P:(j + 1) * P], wox3[:, h, :],
                                      start=(h == 0), stop=(h == 1))
            last.then_inc(sem["out_ps"], 1)

        def chunk_width(c):
            return SG * len(CHUNKS[c % 12][1])

        def a3_act(eng, i):
            st = "a3"
            warm(eng, ACT.Exp)
            turn_act(eng, st, i, 1, XT)
            eng.wait_ge(sem["q_ps"], count(st, "q_ps", i, 1))
            eng.activation(QT3, ps[:, 1, :], ACT.Identity, bias=bq3).then_inc(sem["q_ready"], 1)

            def gap(c):
                eng.wait_ge(sem["gap_ps"], count(st, "gap_ps", i, c + 1))
                if c >= 3:
                    made = "hat_ready" if c % 2 else "odd_hat_ready"
                    eng.wait_ge(sem[made], count(st, made, i, (c - 3) // 2 + 1))
                w = chunk_width(c)
                eng.activation(AB[:, c % 3, 0:w], ps[:, c % 3, 0:w], ACT.Abs, bias=const("negm"))\
                   .then_inc(sem["gap_ready"], 1)

            def hats(chunks):
                for c in chunks:
                    gap(c)
                for c in chunks:
                    if c % 2 == 0:
                        j, ks = CHUNKS[c % 12]
                        eng.wait_ge(sem["gap_ready"], count(st, "gap_ready", i, c + 1))
                        eng.activation(AH[:, (c // 12) % 2, j, ks[0]:ks[-1] + 1, :],
                                       AB[:, c % 3, 0:chunk_width(c)].rearrange("p (k c) -> p k c", k=len(ks)),
                                       ACT.Relu, bias=const("ones")[:, 0:1], scale=-1.0)\
                           .then_inc(sem["hat_ready"], 1)

            for c in range(0, AHEAD, 2):
                hats(range(c, min(c + 2, AHEAD)))
            for u in range(NU3):
                hats(with_unit(u)[:2])
                eng.wait_ge(sem["sm_in"], count(st, "sm_in", i, u + 1))
                eng.activation(EX[:, u % 2, :, :].rearrange("p k q -> p (k q)"),
                               TT[:, u % 2, :, :].rearrange("p k q -> p (k q)"),
                               ACT.Exp).then_inc(sem["ex_ready"], 1)
                hats(with_unit(u)[2:])

        def a3_pool(eng, i):
            st = "a3"
            stage_ct(eng, st, i)
            norm_pool(eng, st, i, 1)
            def add_places(steps, r, of, to, signal):
                eng.tensor_tensor(PAIRS[:, r, :, :], of[:, r, 0:2, :], of[:, r, 2:4, :], ALU.add)\
                   .then_inc(sem["sum_step"], 1)
                eng.wait_ge(sem["sum_step"], count(st, "sum_step", i, steps + 1))
                eng.tensor_tensor(to[:, r, :], PAIRS[:, r, 0, :], PAIRS[:, r, 1, :], ALU.add).then_inc(sem["sum_step"], 1)
                eng.wait_ge(sem["sum_step"], count(st, "sum_step", i, steps + 2))
                eng.tensor_tensor(to[:, r, :], to[:, r, :], of[:, r, 4, :], ALU.add).then_inc(sem[signal], 1)

            for u in range(NU3):
                eng.wait_ge(sem["ex_ready"], count(st, "ex_ready", i, u + 1))
                add_places(4 * u, u % 2, EX, SMQ, "sum_ready")
                eng.wait_ge(sem["skv_read"], count(st, "skv_read", i, u + 1))
                add_places(4 * u + 2, u % 2, WW, UQ, "values_ready")

        def a3_dve(eng, link, i):
            st = "a3"
            link.start(st, i)
            norm_dve(eng, link, st, i, 1, group(xs, i), XH, "rows_ready")
            eng.wait_ge(sem["k_ps"], count(st, "k_ps", i, 1))

            def keep(n, bias):
                link(eng.tensor_tensor(KVT, ps[:, 5:7, :].rearrange("p a (b c) -> p (a b) c", b=4), b3(bias, GB, 1),
                                       ALU.add))
                for b in range(GB):
                    last = eng.tensor_tensor(KV[:, b, :, 16 * n:16 * n + 16],
                                             KVT[:, b, :].rearrange("p (h c) -> p h c", h=8),
                                             const("headhalf").rearrange("p (h c) -> p h c", h=8), ALU.mult)
                return last

            keep(0, bk3).then_inc(sem["k_read"], 1)
            eng.wait_ge(sem["off_ps"], count(st, "off_ps", i, 1))

            def by_batch(ap):
                return ap.rearrange("p (b s) -> p b s", b=GB)

            def of_batch(ap):
                return b3(ap[:, bass.ds(i * GB, GB)], S, 2)

            v, q = by_batch(LT1), by_batch(LT2)
            link(eng.tensor_scalar(LT1, ps[0:KH, 4, :], boff3[0:KH, :], const("ref", KH), ALU.add, ALU.add))
            link(eng.tensor_tensor(LT1, LT1, const("loc", KH), ALU.add))
            link(eng.tensor_tensor(v, v, of_batch(SGN), ALU.mult))
            link(eng.tensor_tensor(q, v, of_batch(INV), ALU.mult))
            link(eng.tensor_scalar(LT2, LT2, 12582912.0, None, ALU.add))
            link(eng.tensor_scalar(LT2, LT2, 12582912.0, None, ALU.subtract))
            link(eng.tensor_tensor(q, q, of_batch(LEN), ALU.mult))
            link(eng.tensor_tensor(LT1, LT1, LT2, ALU.subtract))
            link(eng.tensor_scalar(LT2, LT1, 0.0, None, ALU.is_lt))
            link(eng.tensor_tensor(q, q, of_batch(LEN), ALU.mult))
            link(eng.tensor_tensor(LT1, LT1, LT2, ALU.add))
            link(eng.tensor_tensor(v, v, of_batch(SGN), ALU.mult))
            link(eng.tensor_scalar(LT1, LT1, 2.0 / (S - 1), 1.0, ALU.mult, ALU.subtract))
            link(eng.tensor_scalar(LT1, LT1, 1.0, float(S // 2), ALU.add, ALU.mult))
            link(eng.tensor_scalar(IXT, LT1, 0.5, None, ALU.subtract))
            link(eng.tensor_copy(PARTS[:, 0, :], IXT))
            link(eng.tensor_tensor(LT1, IXT, PARTS[:, 0, :], ALU.subtract))
            link(eng.tensor_copy(PARTS[:, 1, :], LT1))
            link(eng.tensor_tensor(PARTS[:, 2, :], LT1, PARTS[:, 1, :], ALU.subtract))
            for n in range(3):
                for part in range(3):
                    last = eng.tensor_copy(IXB[32 * part:32 * part + 32, n, :], PARTS[32 * n:32 * n + 32, part, :])
            last.then_inc(sem["ix_ready"], 1)

            eng.wait_ge(sem["qx_ps"], count(st, "qx_ps", i, 1))
            for h in range(2):
                last = eng.tensor_scalar(QX[:, h, :], ps[:, 2 + h, :], bqx3[:, h:h + 1], HD ** -0.5, ALU.add, ALU.mult)
            last.then_inc(sem["qx_read"], 1)
            eng.wait_ge(sem["k_read"], count(st, "k_read", i, 1))
            eng.wait_ge(sem["v_ps"], count(st, "v_ps", i, 1))

            def odd_hat(c):
                j, ks = CHUNKS[c % 12]
                eng.wait_ge(sem["gap_ready"], count(st, "gap_ready", i, c + 1))
                eng.tensor_scalar(AH[:, (c // 12) % 2, j, ks[0]:ks[-1] + 1, :],
                                  AB[:, c % 3, 0:chunk_width(c)].rearrange("p (k c) -> p k c", k=len(ks)), 1.0, 0.0,
                                  ALU.subtract, ALU.min).then_inc(sem["odd_hat_ready"], 1)

            def by_place(ap):
                return ap.rearrange("p k q -> p q k")

            def skv(u):
                return ps[:, SKV_BANK[u % 3], 0:NK * S].rearrange("p (k q) -> p k q", k=NK)

            def weigh(u):
                r = u % 2
                eng.wait_ge(sem["ex_ready"], count(st, "ex_ready", i, u + 1))
                eng.tensor_tensor(WW[:, r, :, :], EX[:, r, :, :], skv(u), ALU.mult).then_inc(sem["skv_read"], 1)

            def finish(u):
                _, sg, half, b = unit(u)
                r = u % 2
                at = sg * SG + b * S
                eng.wait_ge(sem["sum_ready"], count(st, "sum_ready", i, u + 1))
                link(eng.reciprocal(RQ[:, r, :], SMQ[:, r, :]))
                eng.wait_ge(sem["values_ready"], count(st, "values_ready", i, u + 1))
                eng.tensor_tensor(OX[:, half, at:at + S], UQ[:, r, :], RQ[:, r, :], ALU.mult).then_inc(sem["o_ready"], 1)

            for c in range(1, AHEAD, 2):
                odd_hat(c)
                if c == 3:
                    keep(1, bv3).then_inc(sem["kv_ready"], 1)
            for u in range(NU3):
                n, sg, half, b = unit(u)
                r = u % 2
                eng.wait_ge(sem["skv_ps"], count(st, "skv_ps", i, u + 1))
                at = sg * SG + b * S
                eng.tensor_tensor(PRD[:, r, :, :], skv(u), b3(QX[:, half, at:at + S], NK, 1), ALU.mult)\
                   .then_inc(sem["prod_ready"], 1)
                odd = [c for c in with_unit(u - 1) if c % 2]
                for c in odd[:1]:
                    odd_hat(c)
                if u >= 1:
                    weigh(u - 1)
                for c in odd[1:]:
                    odd_hat(c)
                if u >= 2:
                    finish(u - 2)
                eng.wait_ge(sem["score_ps"], count(st, "score_ps", i, u + 1))
                score = ps[:, 5 + r, 0:NK * S].rearrange("p (k q) -> p k q", k=NK)
                link(eng.tensor_reduce(MQ[:, r, :], by_place(score), X_AX, ALU.max))
                eng.tensor_tensor(TT[:, r, :, :], score, b3(MQ[:, r, :], NK, 1), ALU.subtract).then_inc(sem["sm_in"], 1)
            weigh(NU3 - 1)
            finish(NU3 - 2)
            finish(NU3 - 1)
            eng.wait_ge(sem["out_ps"], count(st, "out_ps", i, 1))
            link(eng.tensor_tensor(XH, quad(ps[:, 7, :]), b3(bo3, GT, 1), ALU.add))
            g = group(xs, i)
            eng.tensor_tensor(g, g, XH, ALU.add).then_inc(sem["x_ready"], 1)
            link.end()

        def row(a, n=P):
            return a.rearrange("(o n) -> o n", o=1).to_broadcast([n, a.shape[0]])

        def column(a):
            return a.rearrange("(p o) -> p o", o=1)

        def tok(a):
            return a.rearrange("b s d -> (b s) d").rearrange("(t p) d -> p t d", p=P)

        def hidden(a):
            return a.rearrange("(f p) d -> p f d", p=P)

        load_list = {
            "pre": [(con[:, 0:NFIRST], t["constants"][:, 0:NFIRST]), (xs[:, :, :], tok(t["x"])), (cs[:, :, :], tok(t["ctx_1024"])),
                    (m0i[:, :], t["mask_BxS2_ik0"])],
            "r0": [(con[:, NFIRST:NCONST], t["constants"][:, NFIRST:NCONST])],
            "a0": [(wq0, t["L0_xattn_WQ"]), (wk0, t["L0_xattn_WK"]), (wv0, t["L0_xattn_WV"]), (wo0, t["L0_xattn_WO"]),
                   (g_ln, row(t["L0_ffn_ln_g"])), (b_ln, row(t["L0_ffn_ln_b"])), (wr0[:, 0:7], t["L0_ffn_Wr"])],
            "f0": [(W1[:, 0:7, :], t["L0_ffn_W1"].rearrange("e p f -> p e f")), (W1[:, 7, :], t["L0_ffn_W1s"]),
                   (W3[:, 0:7, :], t["L0_ffn_W3"].rearrange("e p f -> p e f")), (W3[:, 7, :], t["L0_ffn_W3s"])]
            + [(W2[:, e, :, :], hidden(t["L0_ffn_W2"][e, :, :])) for e in range(7)]
            + [(W2[:, 7, :, :], hidden(t["L0_ffn_W2s"]))],
            "a1": [(m2i[:, :, :], tok(t["mask_BxSxS2_ik1"])), (w1a, t["L1_xattn_w1"]), (w2a, hidden(t["L1_xattn_w2"])),
                   (b1a, t["L1_xattn_b1"]), (b2a, row(t["L1_xattn_b2"]))]
            + [(ga[n], row(t[f"L1_xattn_g{n + 1}"])) for n in range(3)]
            + [(ba[n], row(t[f"L1_xattn_beta{n + 1}"])) for n in range(3)]
            + [(wr1, t["L1_ffn_Wr"]), (br1, row(t["L1_ffn_br"]))],
            "a2": [(g2, row(t["L2_xattn_gamma"])), (be2, row(t["L2_xattn_beta"])), (wg2, t["L2_ffn_gate_wT"]),
                   (gb2, row(t["L2_ffn_gate_b"])), (b2f2[0:16, :], t["L2_ffn_be2"]),
                   (b2f2[16:17, :], row(t["L2_ffn_bs2"], 1))],
            "a3": [(wq3, t["L3_xattn_WqT"]), (wk3, t["L3_xattn_WkT"]), (wv3, t["L3_xattn_WvT"]),
                   (bk3, row(t["L3_xattn_bk"])), (bv3, row(t["L3_xattn_bv"])), (bo3, row(t["L3_xattn_bo"])),
                   (woff3[:, 0:H * NK], t["L3_xattn_WoffT"]), (boff3[0:H * NK, :], column(t["L3_xattn_boff"])),
                   (bq3, column(t["L3_xattn_bq"])), (wg3, t["L3_ffn_Wg"]), (bg3, row(t["L3_ffn_bg"]))]
            + [(wqx3[:, h, 32 * j:32 * j + 16], t["L3_xattn_WqT"][:, 16 * (4 * h + j):16 * (4 * h + j) + 16])
               for h in range(2) for j in range(4)]
            + [(bqx3[32 * j:32 * j + 16, h:h + 1], column(t["L3_xattn_bq"][16 * (4 * h + j):16 * (4 * h + j) + 16]))
               for h in range(2) for j in range(4)]
            + [(wox3[32 * j + 16:32 * j + 32, h, :], t["L3_xattn_WoT"][16 * (4 * h + j):16 * (4 * h + j) + 16, :])
               for h in range(2) for j in range(4)],
            "f2": [(U1[:, 0:1024].rearrange("p (e f) -> p e f", e=EG), t["L2_ffn_We1"].rearrange("e p f -> p e f")),
                   (U1[:, 1024:NU], t["L2_ffn_ws1"]),
                   (U3[:, 0:1024].rearrange("p (e f) -> p e f", e=EG), t["L2_ffn_We3"].rearrange("e p f -> p e f")),
                   (U3[:, 1024:NU], t["L2_ffn_ws3"]),
                   (U2[:, 0:8, :], hidden(t["L2_ffn_We2"].rearrange("e f d -> (e f) d"))),
                   (U2[:, 8, :], t["L2_ffn_ws2"]),
                   (UB1[:, 0:1024], row(t["L2_ffn_be1"].rearrange("e f -> (e f)"))), (UB1[:, 1024:NU], row(t["L2_ffn_bs1"])),
                   (UB3[:, 0:1024], row(t["L2_ffn_be3"].rearrange("e f -> (e f)"))), (UB3[:, 1024:NU], row(t["L2_ffn_bs3"])),
                   (M3, t["mask_BxS2_if0"].rearrange("(o b) s -> o b s", o=1).to_broadcast([KH, B, S])),
                   (windows, t["windows"])],
        }
        for n, layer in (("f1", "L1"), ("f3", "L3")):
            load_list[n] = [(V1, t[layer + "_ffn_W1"].rearrange("e p f -> p e f"))]\
                + [(V2[:, e, :, :], hidden(t[layer + "_ffn_W2"][e, :, :])) for e in range(E)]\
                + [(VB1[:, e, :], row(t[layer + "_ffn_b1"][e, :])) for e in range(E)]\
                + [(b2r[:, e, :], row(t[layer + "_ffn_b2"][e, :])) for e in range(E)]

        block = ctx.enter_context(nc.Block())

        @block.sync
        def _(eng):
            def load(name):
                for dst, src in load_list[name]:
                    eng.dma_start(dst, src).then_inc(loads[name], 16)

            load("pre")
            load("a0")
            load("r0")
            eng.wait_ge(s_zeros, 1)
            for rows in (xe, ye):
                eng.dma_start(rows.rearrange("(n p) d -> p n d", p=P),
                              wb[:, 0:ROWS].rearrange("p (n d) -> p n d", d=D)).then_inc(s_zero, 16)
            load("f0")
            load("a1")
            eng.wait_ge(s_zero, 16 * 2)
            load("f1")
            eng.wait_ge(sem["ht_ready"], total("r0", "ht_ready"))
            eng.wait_ge(sem["slot_ready"], total("g0", "slot_ready"))
            s0[4](eng)
            eng.wait_ge(s_sent, 16 * 2 * NT)
            f0[4](eng)
            eng.wait_ge(sem["y_read"], total("f0_last", "y_read"))
            load("f2")
            eng.wait_ge(s_sent, 16 * 2 * NT * 2)
            f1[4](eng)
            eng.wait_ge(s_init, 1)
            load("a2")
            load("a3")
            eng.wait_ge(sem["y_read"], total("f1_last", "y_read"))
            load("f3")
            eng.wait_ge(s_sent, 16 * 2 * NT * 3)
            f3[4](eng)
            for g in range(NG):
                eng.wait_ge(sem["x_ready"], count("c3", "x_ready", 0, g + 1))
                eng.dma_start(tok(out)[:, g * GT:(g + 1) * GT, :], xs[:, g * GT:(g + 1) * GT, :]).then_inc(s_out, 16)
            for name in loads:
                eng.wait_ge(loads[name], 16 * len(load_list[name]))
            eng.wait_ge(s_out, 16 * NG)

        needs = {"pre": ["pre"], "a0": ["a0"], "r0": ["r0"], "s0": ["f0"], "a1": ["a1"], "f1": ["f1"], "a2": ["a2"], "f2": ["f2"],
                 "a3": ["a3"], "f3": ["f3"], "m3": ["f2"]}

        @block.tensor
        def _(eng):
            for n, value in EARLY.items():
                eng.sem_inc(sem[n], value)
            turns = {"a0": a0_pe, "a1": a1_pe, "a2": a2_pe, "a3": a3_pe, "f2": f2[0],
                     "r0": lambda eng, i: logits_pe(eng, "r0", i, wr0[:, 0:7], 7),
                     "r1": lambda eng, i: logits_pe(eng, "r1", i, wr1, 8),
                     "r2": lambda eng, i: logits_pe(eng, "r2", i, wg2, EG),
                     "r3": lambda eng, i: logits_pe(eng, "r3", i, wg3, E), "b1": b1_pe}
            for st in ORDER:
                wait_loads(eng, *needs.get(st, []))
                if st in ("s0", "f0", "f1", "f3"):
                    eng.wait_ge(sem["slot_ready"], total("g" + st[1], "slot_ready"))
                if st == "pre":
                    for g in range(NG):
                        if g >= 1:
                            eng.wait_ge(sem["cols_ready"], count(st, "cols_ready", g, 0))
                        for j in range(GT):
                            last = eng.transpose(ps[:, 0, j * P:(j + 1) * P], cs[:, g * GT + j, :], ident)
                        last.then_inc(sem["turned"], 1)
                elif st in experts_loops:
                    experts_loops[st][0](eng)
                elif st in turns:
                    with eng.Fori(0, LOOPS[st]) as i:
                        turns[st](eng, i)
                elif st in ("g0", "g3"):
                    cum_pe(eng, st, 1, A3)
                elif st == "g1":
                    cum_pe(eng, st, 1, T2[:, 0:256])
                    cum_pe(eng, st, 2, T3[:, 256:384])

        @block.scalar
        def _(eng):
            turns = {"a0": a0_act, "a1": a1_act, "a2": a2_act, "a3": a3_act, "f2": f2[1],
                     "r0": lambda eng, i: logits_act(eng, "r0", i, False, 7),
                     "r1": lambda eng, i: logits_act(eng, "r1", i, True, 8),
                     "r2": lambda eng, i: logits_act(eng, "r2", i, True, EG),
                     "r3": lambda eng, i: logits_act(eng, "r3", i, False, E)}
            for st in ORDER:
                wait_loads(eng, *needs.get(st, []))
                if st == "pre":
                    for g in range(NG):
                        turn_act(eng, st, g, 1, cT[:, g * GW:(g + 1) * GW])
                elif st in experts_loops:
                    experts_loops[st][1](eng)
                elif st in turns:
                    with eng.Fori(0, LOOPS[st]) as i:
                        turns[st](eng, i)
                elif st in ("g0", "g3"):
                    exp_gate(eng, st)

        @block.gpsimd
        def _(eng):
            def a(st, norms, ct=False):
                def f(eng, i):
                    if ct:
                        stage_ct(eng, st, i)
                    for k in range(norms):
                        norm_pool(eng, st, i, k + 1)
                return f

            def sides(st, norms, then=None):
                def f(eng, i):
                    for k in range(norms):
                        for q in SIDES:
                            norm_side_pool(eng, st, i, k + 1, q)
                    if then:
                        then(eng, st, i)
                return f

            turns = {"a0": a("a0", 1, True), "a3": a3_pool,
                     "f2": f2[3],
                     "r0": sides("r0", 2, rows_pool), "r1": sides("r1", 1, rows_pool),
                     "r2": sides("r2", 1, logits_pool), "r3": sides("r3", 1, rows_pool)}
            for st in ORDER:
                wait_loads(eng, *needs.get(st, []))
                if st == "a0":
                    eng.wait_ge(sem["cols_ready"], total("pre", "cols_ready"))
                if st == "a3":
                    eng.wait_ge(sem["x_ready"], count("a3", "x_ready"))
                if st == "f2":
                    eng.wait_ge(sem["ht_ready"], total("r2", "ht_ready"))
                    eng.wait_ge(sem["c_ready"], total("g2", "c_ready"))
                if st in ("f0", "f1", "f3"):
                    dispatch_pool(eng, st[1])
                if st in ("a1", "a2"):
                    gather_turns_pool(eng, st, int(st[1]) - 1, {"a1": 4, "a2": 2}[st])
                if st in experts_loops and st != "s0":
                    experts_loops[st][3](eng)
                elif st in turns:
                    with eng.Fori(0, LOOPS[st]) as i:
                        turns[st](eng, i)
                if st == "f3":
                    gather_pool(eng)

        @block.vector
        def _(eng):
            link = Chain(eng)
            eng.memset(wb[:, 0:ROWS], 0.0).then_inc(s_zeros, 1)

            def router(st, norms, n, **kw):
                def f(eng, link, i):
                    link.start(st, i)
                    eng.wait_ge(sem["ht_ready"], count(st, "ht_ready", i))
                    for q in SIDES:
                        norm_in(eng, link, q, of_side(xs, i, q))
                    if norms == 1:
                        for q in SIDES:
                            norm_out(eng, st, i, 1, q, of_side(xs, i, q), XH_[q]).then_inc(sem["rows_ready"], 1)
                    else:
                        for q in SIDES:
                            link(norm_out(eng, st, i, 1, q, of_side(xs, i, q), XH_[q]))
                            norm_in(eng, link, q, XH_[q])
                        for q in SIDES:
                            link(norm_out(eng, st, i, 2, q, XH_[q], XH_[q]))
                            link(eng.tensor_tensor(XH_[q], XH_[q], b3(g_ln, GT, 1), ALU.mult))
                            eng.tensor_tensor(XH_[q], XH_[q], b3(b_ln, GT, 1), ALU.add).then_inc(sem["rows_ready"], 1)
                    logits_dve(eng, link, st, i, n, **kw)
                    link.end()
                return f

            turns = {"a0": a0_dve, "a1": a1_dve, "a2": a2_dve, "a3": a3_dve, "f2": f2[2],
                     "b1": b1_dve, "r0": router("r0", 2, 7), "r1": router("r1", 1, E, bias=br1, softmax=True),
                     "r2": router("r2", 1, EG, softmax=True),
                     "r3": router("r3", 1, E, bias=bg3, scale=1.0 / (1.0 + 1e-6))}
            once = {"g0": g0_dve, "t1": t1_dve, "g1": g1_dve, "g2": g2_dve, "g3": g3_dve, "m3": m3_dve}
            for st in ORDER:
                if st == "f1":
                    eng.wait_ge(sem["lg_ps"], total("r1", "lg_ps"))
                    eng.memset(wsm[:, :], 0.0).then_inc(s_init, 1)
                wait_loads(eng, *needs.get(st, []))
                if st[0] in "ar" and st != "a0":
                    eng.wait_ge(sem["x_ready"], count(st, "x_ready"))
                if st == "a0":
                    link.start("a0", 0)
                    eng.tensor_scalar(qkeep[:, :], m0i[:, :], 0.0, None, ALU.is_equal).then_inc(s_keep, 1)
                    eng.wait_ge(s_keep, 1)
                if st == "r0":
                    eng.memset(lg[:, :, 7:8], NEG)
                if st in ("s0", "f0", "f1", "f3"):
                    eng.wait_ge(sem["slot_ready"], total("g" + st[1], "slot_ready"))
                if st == "c3":
                    combine_dve(eng, link)
                if st == "f2":
                    eng.wait_ge(sem["c_ready"], total("g2", "c_ready"))
                if st in experts_loops:
                    experts_loops[st][2](eng)
                elif st in turns:
                    with eng.Fori(0, LOOPS[st]) as i:
                        turns[st](eng, link, i)
                elif st in once:
                    once[st](eng, link)


TURNED = {"L2_ffn_gate_w": "L2_ffn_gate_wT", "L3_xattn_Wq": "L3_xattn_WqT", "L3_xattn_Wk": "L3_xattn_WkT",
          "L3_xattn_Wv": "L3_xattn_WvT", "L3_xattn_Wo": "L3_xattn_WoT", "L3_xattn_Woff": "L3_xattn_WoffT"}


def kernel(**inputs):
    import concourse.bacc as bacc
    from concourse.bass_utils import run_bass_kernel_spmd

    nc = bacc.Bacc("TRN2", target_bir_lowering=False, num_devices=1)
    laid = {}
    for name, a in inputs.items():
        a = np.asarray(a)
        if name in ("mask_BxS2_ik0", "L1_xattn_b1"):
            a = a.reshape(-1, P).T
        if name in ("L3_xattn_Woff", "L3_xattn_boff"):
            a = a.reshape(H, NK, -1).transpose(1, 0, 2).reshape(a.shape)
        laid[TURNED.get(name, name)] = np.ascontiguousarray(a.T if name in TURNED else a)
    laid["constants"] = constants()
    laid["windows"] = (np.arange(2048)[None, :] // S == np.arange(96)[:, None] % 32).astype(np.float32)
    arrays, t = {}, {}
    for name, a in laid.items():
        arrays[f"in_{name}"] = a
        t[name] = nc.dram_tensor(f"in_{name}", a.shape, mybir.dt.from_np(a.dtype), kind="ExternalInput").ap()
    out = nc.dram_tensor("out_x", (B, S, D), F32, kind="ExternalOutput").ap()
    build(nc, t, out)
    r = run_bass_kernel_spmd(nc, [arrays], core_ids=[0])
    return r.results[0]["out_x"]
```
